# Optimizing a Trainium2 kernel written in Bass

```python
import numpy as np
import jax
import jax.numpy as jnp

def _softmax(x, axis=-1):
    return jax.nn.softmax(x, axis=axis)

def _gelu(x):
    return jax.nn.gelu(x, approximate=True)

def _silu(x):
    return jax.nn.silu(x)

def _sigmoid(x):
    return jax.nn.sigmoid(x)

def _layernorm(x, axis=-1, eps=1e-05):
    m = jnp.mean(x, axis=axis, keepdims=True)
    v = jnp.var(x, axis=axis, keepdims=True)
    return (x - m) / jnp.sqrt(v + eps)

def _scatter_add(tgt, idx, src, axis=0):
    return tgt.at[idx].add(src)

def _segment_sum(src, seg, n):
    return jax.ops.segment_sum(src, seg, n)
kernel_name = 'mk_hybrid_d1_jaxref_r8_c5497d'

def setup_inputs(seed: int=0):
    np.random.seed(seed)
    _w = jnp.asarray

    def _L0_attn_a_setup():
        import jax, jax.numpy as jnp
        import numpy as np

        def apply_rope(x):
            b, h, n, d = x.shape
            half = d // 2
            freqs = jnp.arange(0, half, dtype=x.dtype) / half
            theta = 1.0 / 1250 ** freqs
            positions = jnp.arange(n, dtype=x.dtype)
            angles = positions[:, None] * theta[None, :]
            cos = jnp.cos(angles)[None, None, :, :]
            sin = jnp.sin(angles)[None, None, :, :]
            x1 = x[..., ::2]
            x2 = x[..., 1::2]
            r1 = x1 * cos - x2 * sin
            r2 = x1 * sin + x2 * cos
            return jnp.stack([r1, r2], axis=-1).reshape(b, h, n, d)
        key = jax.random.key(seed)
        ks = jax.random.split(key, 4)
        B, N, D = (2, 256, 128)
        x = jax.random.normal(ks[0], (B, N, D), dtype=jnp.float32)
        w_qkv = jax.random.normal(ks[1], (D, 3 * D), dtype=jnp.float32) * (1.0 / np.sqrt(D))
        b_qkv = jnp.zeros((3 * D,), dtype=jnp.float32)
        w_out = jax.random.normal(ks[2], (D, D), dtype=jnp.float32) * (1.0 / np.sqrt(D))
        b_out = jnp.zeros((D,), dtype=jnp.float32)
        return {'x': x, 'w_qkv': w_qkv, 'b_qkv': b_qkv, 'w_out': w_out, 'b_out': b_out}
    _L0_attn_a_in = _L0_attn_a_setup()

    def _L0_attn_b_setup():
        import jax, jax.numpy as jnp
        import numpy as np
        from jax import lax
        D_MODEL, D_STATE, D_CONV, EXPAND = (128, 16, 4, 2)
        D_INNER = D_MODEL * EXPAND
        LN_EPS = 1e-05

        def _silu(v):
            return v * jax.nn.sigmoid(v)

        def _forward(x, W_in, conv_w, conv_b, W_x, W_dt, b_dt, A_log, D_param, W_out, ln_g, ln_b):
            B, T, _ = x.shape
            xz = jnp.einsum('btd,ed->bte', x, W_in)
            xp, z = (xz[..., :D_INNER], xz[..., D_INNER:])
            xc = lax.conv_general_dilated(jnp.transpose(xp, (0, 2, 1)), conv_w, window_strides=(1,), padding=[(D_CONV - 1, 0)], feature_group_count=D_INNER, dimension_numbers=('NCH', 'OIH', 'NCH')) + conv_b[None, :, None]
            xc = _silu(jnp.transpose(xc, (0, 2, 1)))
            ssm = jnp.einsum('bti,si->bts', xc, W_x)
            Bp, Cp = (ssm[..., :D_STATE], ssm[..., D_STATE:])
            dt = jax.nn.softplus(jnp.einsum('bti,oi->bto', xc, W_dt) + b_dt)
            A = -jnp.exp(A_log)

            def step(h, inp):
                x_t, b_t, c_t, dt_t = inp
                dA = jnp.exp(dt_t[..., None] * A)
                h = dA * h + dt_t[..., None] * b_t[:, None, :] * x_t[..., None]
                y_t = jnp.einsum('bds,bs->bd', h, c_t)
                return (h, y_t)
            h0 = jnp.zeros((B, D_INNER, D_STATE), dtype=x.dtype)
            tm = lambda a: jnp.moveaxis(a, 1, 0)
            _, ys = lax.scan(step, h0, (tm(xc), tm(Bp), tm(Cp), tm(dt)))
            y = jnp.moveaxis(ys, 0, 1)
            mu = jnp.mean(y, axis=-1, keepdims=True)
            var = jnp.mean((y - mu) ** 2, axis=-1, keepdims=True)
            y = (y - mu) * lax.rsqrt(var + LN_EPS) * ln_g + ln_b
            y = y + xc * D_param
            y = y * _silu(z)
            return jnp.einsum('bti,di->btd', y, W_out)
        key = jax.random.key(seed)
        ks = jax.random.split(key, 12)
        B, T = (4, 256)
        x = jax.random.normal(ks[0], (B, T, D_MODEL), dtype=jnp.float32)
        W_in = jax.random.normal(ks[1], (2 * D_INNER, D_MODEL), dtype=jnp.float32) * D_MODEL ** (-0.5)
        conv_w = jax.random.normal(ks[2], (D_INNER, 1, D_CONV), dtype=jnp.float32) * D_CONV ** (-0.5)
        conv_b = jax.random.normal(ks[3], (D_INNER,), dtype=jnp.float32) * 0.01
        W_x = jax.random.normal(ks[4], (2 * D_STATE, D_INNER), dtype=jnp.float32) * D_INNER ** (-0.5)
        dt_init_std = D_INNER ** (-0.5)
        W_dt = jax.random.uniform(ks[5], (D_INNER, D_INNER), minval=-dt_init_std, maxval=dt_init_std, dtype=jnp.float32)
        dt = jnp.exp(jax.random.uniform(ks[6], (D_INNER,)) * (np.log(0.1) - np.log(0.001)) + np.log(0.001))
        b_dt = dt + jnp.log(-jnp.expm1(-dt))
        A_log = jnp.log(jnp.arange(1, D_STATE + 1, dtype=jnp.float32) * 0.5)
        D_param = jnp.ones((D_INNER,), dtype=jnp.float32)
        W_out = jax.random.normal(ks[7], (D_MODEL, D_INNER), dtype=jnp.float32) * D_MODEL ** (-0.5)
        ln_g = jnp.ones((D_INNER,), dtype=jnp.float32)
        ln_b = jnp.zeros((D_INNER,), dtype=jnp.float32)
        return {'x': x, 'W_in': W_in, 'conv_w': conv_w, 'conv_b': conv_b, 'W_x': W_x, 'W_dt': W_dt, 'b_dt': b_dt, 'A_log': A_log, 'D_param': D_param, 'W_out': W_out, 'ln_g': ln_g, 'ln_b': ln_b}
    _L0_attn_b_in = _L0_attn_b_setup()

    def _L0_ffn_setup():
        import jax, jax.numpy as jnp
        import numpy as np
        TOP_K = 2
        key = jax.random.key(seed)
        ks = jax.random.split(key, 6)
        B, S, H, F, E = (4, 256, 128, 512, 8)
        x = jax.random.normal(ks[0], (B, S, H), dtype=jnp.float32)
        gate_w = jax.random.normal(ks[1], (E, H), dtype=jnp.float32) * 0.02
        W1 = jax.random.normal(ks[2], (E, H, F), dtype=jnp.float32) * (1.0 / np.sqrt(H))
        b1 = jnp.zeros((E, F), dtype=jnp.float32)
        W2 = jax.random.normal(ks[3], (E, F, H), dtype=jnp.float32) * (1.0 / np.sqrt(F))
        b2 = jnp.zeros((E, H), dtype=jnp.float32)
        sW1 = jax.random.normal(ks[4], (H, F), dtype=jnp.float32) * (1.0 / np.sqrt(H))
        sb1 = jnp.zeros((F,), dtype=jnp.float32)
        sW2 = jax.random.normal(ks[5], (F, H), dtype=jnp.float32) * (1.0 / np.sqrt(F))
        sb2 = jnp.zeros((H,), dtype=jnp.float32)
        return {'x': x, 'gate_w': gate_w, 'W1': W1, 'b1': b1, 'W2': W2, 'b2': b2, 'sW1': sW1, 'sb1': sb1, 'sW2': sW2, 'sb2': sb2}
    _L0_ffn_in = _L0_ffn_setup()
    _d = {'L0_attn_a_x': _L0_attn_a_in['x'], 'L0_attn_a_w_qkv': _L0_attn_a_in['w_qkv'], 'L0_attn_a_b_qkv': _L0_attn_a_in['b_qkv'], 'L0_attn_a_w_out': _L0_attn_a_in['w_out'], 'L0_attn_a_b_out': _L0_attn_a_in['b_out'], 'L0_attn_b_W_in': _L0_attn_b_in['W_in'], 'L0_attn_b_conv_w': _L0_attn_b_in['conv_w'], 'L0_attn_b_conv_b': _L0_attn_b_in['conv_b'], 'L0_attn_b_W_x': _L0_attn_b_in['W_x'], 'L0_attn_b_W_dt': _L0_attn_b_in['W_dt'], 'L0_attn_b_b_dt': _L0_attn_b_in['b_dt'], 'L0_attn_b_A_log': _L0_attn_b_in['A_log'], 'L0_attn_b_D_param': _L0_attn_b_in['D_param'], 'L0_attn_b_W_out': _L0_attn_b_in['W_out'], 'L0_attn_b_ln_g': _L0_attn_b_in['ln_g'], 'L0_attn_b_ln_b': _L0_attn_b_in['ln_b'], 'L0_ffn_gate_w': _L0_ffn_in['gate_w'], 'L0_ffn_W1': _L0_ffn_in['W1'], 'L0_ffn_b1': _L0_ffn_in['b1'], 'L0_ffn_W2': _L0_ffn_in['W2'], 'L0_ffn_b2': _L0_ffn_in['b2'], 'L0_ffn_sW1': _L0_ffn_in['sW1'], 'L0_ffn_sb1': _L0_ffn_in['sb1'], 'L0_ffn_sW2': _L0_ffn_in['sW2'], 'L0_ffn_sb2': _L0_ffn_in['sb2']}
    _x0 = _d['L0_attn_a_x']
    _d['L0_attn_a_x'] = jax.random.normal(jax.random.fold_in(jax.random.key(seed), 1), (16, 512, 128), dtype=_x0.dtype)
    del _x0
    return _d

def reference(L0_attn_a_x, L0_attn_a_w_qkv, L0_attn_a_b_qkv, L0_attn_a_w_out, L0_attn_a_b_out, L0_attn_b_W_in, L0_attn_b_conv_w, L0_attn_b_conv_b, L0_attn_b_W_x, L0_attn_b_W_dt, L0_attn_b_b_dt, L0_attn_b_A_log, L0_attn_b_D_param, L0_attn_b_W_out, L0_attn_b_ln_g, L0_attn_b_ln_b, L0_ffn_gate_w, L0_ffn_W1, L0_ffn_b1, L0_ffn_W2, L0_ffn_b2, L0_ffn_sW1, L0_ffn_sb1, L0_ffn_sW2, L0_ffn_sb2):

    def _L0_attn_a_ref(x, w_qkv, b_qkv, w_out, b_out):
        import jax, jax.numpy as jnp
        import numpy as np

        def apply_rope(x):
            b, h, n, d = x.shape
            half = d // 2
            freqs = jnp.arange(0, half, dtype=x.dtype) / half
            theta = 1.0 / 1250 ** freqs
            positions = jnp.arange(n, dtype=x.dtype)
            angles = positions[:, None] * theta[None, :]
            cos = jnp.cos(angles)[None, None, :, :]
            sin = jnp.sin(angles)[None, None, :, :]
            x1 = x[..., ::2]
            x2 = x[..., 1::2]
            r1 = x1 * cos - x2 * sin
            r2 = x1 * sin + x2 * cos
            return jnp.stack([r1, r2], axis=-1).reshape(b, h, n, d)
        B, N, D = x.shape
        H = 16
        hd = D // H
        qkv = x @ w_qkv + b_qkv
        q, k, v = jnp.split(qkv, 3, axis=-1)
        to_heads = lambda t: t.reshape(B, N, H, hd).transpose(0, 2, 1, 3)
        q, k, v = (to_heads(q), to_heads(k), to_heads(v))
        q = jax.nn.elu(q) + 1
        k = jax.nn.elu(k) + 1
        rot_q = apply_rope(q)
        rot_k = apply_rope(k)
        attn_num = jnp.einsum('bhid,bhjd->bhij', rot_q, rot_k)
        attn_denom = jnp.einsum('bhid,bhjd->bhij', q, k)
        attn_weights = attn_num / attn_denom
        out = jnp.einsum('bhij,bhjd->bhid', attn_weights, v)
        out = out.transpose(0, 2, 1, 3).reshape(B, N, D)
        return out @ w_out + b_out

    def _L0_attn_b_ref(x, W_in, conv_w, conv_b, W_x, W_dt, b_dt, A_log, D_param, W_out, ln_g, ln_b):
        import jax, jax.numpy as jnp
        import numpy as np
        from jax import lax
        D_MODEL, D_STATE, D_CONV, EXPAND = (128, 16, 4, 2)
        D_INNER = D_MODEL * EXPAND
        LN_EPS = 1e-05

        def _silu(v):
            return v * jax.nn.sigmoid(v)

        def _forward(x, W_in, conv_w, conv_b, W_x, W_dt, b_dt, A_log, D_param, W_out, ln_g, ln_b):
            B, T, _ = x.shape
            xz = jnp.einsum('btd,ed->bte', x, W_in)
            xp, z = (xz[..., :D_INNER], xz[..., D_INNER:])
            xc = lax.conv_general_dilated(jnp.transpose(xp, (0, 2, 1)), conv_w, window_strides=(1,), padding=[(D_CONV - 1, 0)], feature_group_count=D_INNER, dimension_numbers=('NCH', 'OIH', 'NCH')) + conv_b[None, :, None]
            xc = _silu(jnp.transpose(xc, (0, 2, 1)))
            ssm = jnp.einsum('bti,si->bts', xc, W_x)
            Bp, Cp = (ssm[..., :D_STATE], ssm[..., D_STATE:])
            dt = jax.nn.softplus(jnp.einsum('bti,oi->bto', xc, W_dt) + b_dt)
            A = -jnp.exp(A_log)

            def step(h, inp):
                x_t, b_t, c_t, dt_t = inp
                dA = jnp.exp(dt_t[..., None] * A)
                h = dA * h + dt_t[..., None] * b_t[:, None, :] * x_t[..., None]
                y_t = jnp.einsum('bds,bs->bd', h, c_t)
                return (h, y_t)
            h0 = jnp.zeros((B, D_INNER, D_STATE), dtype=x.dtype)
            tm = lambda a: jnp.moveaxis(a, 1, 0)
            _, ys = lax.scan(step, h0, (tm(xc), tm(Bp), tm(Cp), tm(dt)))
            y = jnp.moveaxis(ys, 0, 1)
            mu = jnp.mean(y, axis=-1, keepdims=True)
            var = jnp.mean((y - mu) ** 2, axis=-1, keepdims=True)
            y = (y - mu) * lax.rsqrt(var + LN_EPS) * ln_g + ln_b
            y = y + xc * D_param
            y = y * _silu(z)
            return jnp.einsum('bti,di->btd', y, W_out)
        return _forward(x, W_in, conv_w, conv_b, W_x, W_dt, b_dt, A_log, D_param, W_out, ln_g, ln_b)

    def _L0_ffn_ref(x, gate_w, W1, b1, W2, b2, sW1, sb1, sW2, sb2):
        import jax, jax.numpy as jnp
        import numpy as np
        TOP_K = 2
        B, S, H = x.shape
        E = gate_w.shape[0]
        x_flat = x.reshape(-1, H)
        logits = x_flat @ gate_w.T
        probs = jax.nn.softmax(logits.astype(jnp.float32), axis=-1)
        top_w, sel = jax.lax.top_k(probs, TOP_K)
        top_w = top_w / jnp.sum(top_w, axis=-1, keepdims=True)
        combine = jnp.sum(jax.nn.one_hot(sel, E, dtype=top_w.dtype) * top_w[..., None], axis=1)
        combine = combine.astype(x.dtype)
        h = jax.nn.gelu(jnp.einsum('th,ehf->tef', x_flat, W1) + b1[None], approximate=False)
        y = jnp.einsum('tef,efh->teh', h, W2) + b2[None]
        out = jnp.einsum('teh,te->th', y, combine)
        sh = jax.nn.gelu(x_flat @ sW1 + sb1, approximate=False)
        out = out + sh @ sW2 + sb2
        return out.reshape(B, S, H)
    x = L0_attn_a_x
    x = x + _L0_attn_a_ref(_layernorm(x, axis=-1), L0_attn_a_w_qkv, L0_attn_a_b_qkv, L0_attn_a_w_out, L0_attn_a_b_out)
    x = x + _L0_ffn_ref(_layernorm(x, axis=-1), L0_ffn_gate_w, L0_ffn_W1, L0_ffn_b1, L0_ffn_W2, L0_ffn_b2, L0_ffn_sW1, L0_ffn_sb1, L0_ffn_sW2, L0_ffn_sb2)
    x = x + _L0_attn_b_ref(_layernorm(x, axis=-1), L0_attn_b_W_in, L0_attn_b_conv_w, L0_attn_b_conv_b, L0_attn_b_W_x, L0_attn_b_W_dt, L0_attn_b_b_dt, L0_attn_b_A_log, L0_attn_b_D_param, L0_attn_b_W_out, L0_attn_b_ln_g, L0_attn_b_ln_b)
    x = x + _L0_ffn_ref(_layernorm(x, axis=-1), L0_ffn_gate_w, L0_ffn_W1, L0_ffn_b1, L0_ffn_W2, L0_ffn_b2, L0_ffn_sW1, L0_ffn_sb1, L0_ffn_sW2, L0_ffn_sb2)
    return x

_drawn_inputs = setup_inputs


def setup_inputs(seed=0):
    import zlib

    import numpy as np

    out = dict(_drawn_inputs(seed))
    spreads = {'L0_attn_a_b_qkv': (0.0, 0.1),
     'L0_attn_a_b_out': (0.0, 0.8),
     'L0_attn_b_D_param': (1.0, 0.6),
     'L0_attn_b_ln_g': (1.0, 0.6),
     'L0_attn_b_ln_b': (0.0, 0.8),
     'L0_ffn_b1': (0.0, 0.8),
     'L0_ffn_b2': (0.0, 0.8),
     'L0_ffn_sb1': (0.0, 0.8),
     'L0_ffn_sb2': (0.0, 0.537)}
    factors = {'L0_attn_b_conv_b': 32.75, 'L0_attn_b_W_dt': 5.164}
    for name, (base, spread) in spreads.items():
        noise = np.random.default_rng([zlib.crc32(name.encode()), seed]).standard_normal(out[name].shape)
        drawn = base * np.exp(spread * noise) if base else spread * noise
        out[name] = jnp.asarray(drawn.astype(out[name].dtype))
    for name, factor in factors.items():
        out[name] = (out[name] * factor).astype(out[name].dtype)
    return out
```

```python
from contextlib import ExitStack

import numpy as np

import concourse.bass as bass
from concourse import mybir

F32 = mybir.dt.float32
BF16 = mybir.dt.bfloat16
U32 = mybir.dt.uint32
ALU = mybir.AluOpType
ACT = mybir.ActivationFunctionType
LOG_EXP = "natural_log_exp_and_others"
GELU_SET = "gelu_and_others"
SILU_SET = "silu_and_others"

P = 128
D = 128
NH, HD = 16, 8
NE, FF = 8, 512
FC = FF // P
NCH = (NE + 1) * FC
DI = 256
NS = 16
NCONV = 4
EPS = 1e-5
JB = 4
NC = 4
NK = 4
STEPS = NK * JB
UNITS = STEPS * NC
PARTS = 3
QROWS = (0, 0, 1, 1, 0, 2)
KROWS = (0, 1, 0, 1, 2, 0)
PK_DMAS = 2 * len(QROWS)
RESET = 1e30

FFN_AT_X = {0: [("mean", 0)], 1: [("var", 0)], 2: [("router", 0), ("ups", 0)], 3: [("turn", 0), ("burst", 0), ("downs", 0), ("ups", 1)]}
for _q in range(1, NE + 1):
    FFN_AT_X.setdefault(3 + (3 * _q + 1) // 2 if 3 + (3 * _q + 1) // 2 < STEPS else STEPS - 1, []).extend(
        [("spread", _q), ("burst", _q), ("downs", _q)] + ([("ups", _q + 1)] if _q < NE else []))
PERIODS = [[("spread", _q), ("burst", _q), ("downs", _q)] + ([("ups", _q + 1)] if _q < NE else []) for _q in range(1, NE + 1)]

X_ORDER = [("A", "scores", 0)]
for _s in range(STEPS):
    X_ORDER += [("A", "den_num", _s)]
    X_ORDER += [("F", n, q) for n, q in FFN_AT_X.get(_s, [])]
    X_ORDER += [("A", "av", _s)]
X_ORDER += [("A", "close", 0), ("F", "close", 0)]

Y_ORDER = [
    ("M", "mean", 0), ("F", "mean", 0), ("M", "var", 0), ("F", "var", 0), ("M", "inproj", 0), ("F", "router", 0),
    ("F", "ups", 0), ("M", "conv", 0), ("F", "turn", 0), ("F", "burst", 0), ("F", "downs", 0), ("F", "ups", 1),
    ("M", "silu", 0), ("M", "dt", 0)]
Y_ORDER += [("F", n, q) for n, q in PERIODS[0]]
Y_ORDER += [("M", "state", 0)]
_PRE = [("load", 0), ("mean", 0), ("var", 0), ("qk", 0), ("qk", 1), ("rope", 0), ("qk", 2), ("qk", 3), ("rope", 1), ("v", 0)]
for _s in range(NS):
    Y_ORDER += [("M", "unit", _s)]
    if _s < len(_PRE):
        Y_ORDER += [("P", *_PRE[_s])]
    if _s % 2 == 1 and _s // 2 + 1 < NE:
        Y_ORDER += [("F", n, q) for n, q in PERIODS[_s // 2 + 1]]
Y_ORDER += [("M", "close", 0), ("F", "close", 0)]


def hybrid_layer_kernel(nc: bass.Bass, x, w_qkv, b_qkv, w_out, b_out, W_in, conv_w, conv_b, W_x, W_dt, b_dt, A_log,
                        D_param, W_out, ln_g, ln_b, gate_w, W1, b1, W2, b2, sW1, sb1, sW2, sb2,
                        rope_cos, rope_sin, out):
    NB, T, _ = x.shape
    assert T == JB * P and T == 512

    ctx = ExitStack()
    with ctx:
        def sb(name, shape, dt=F32):
            return ctx.enter_context(nc.sbuf_tensor(name, shape, dt))

        def sem(name):
            return ctx.enter_context(nc.semaphore(name))

        ps = [ctx.enter_context(nc.psum_tensor(f"bank{i}", [P, 512], F32)) for i in range(8)]

        qscr = nc.dram_tensor("qscr", (2, 2, P, NC * 512), BF16, kind="Internal").ap()
        kscr = nc.dram_tensor("kscr", (2, 2, 2, P, NC * 512), BF16, kind="Internal").ap()

        W1s = sb("W1s", [P, NE + 1, FF])
        W2s = sb("W2s", [P, NE + 1, FC, D])
        wqk = sb("wqk", [P, 4, P])
        wv = sb("wv", [P, D])
        wos = sb("wos", [P, D])
        WinT = sb("WinT", [P, 4, P])
        WdtT = sb("WdtT", [P, 2, DI])
        WoT = sb("WoT", [P, 2, D])
        wxT = sb("wxT", [P, 2, PARTS * 2 * NS])
        gateT = sb("gateT", [P, NE])
        ropeC = sb("ropeC", [P, 512])
        ropeS = sb("ropeS", [P, 512])
        ident = sb("ident", [P, P])
        onesD = sb("onesD", [P, P])
        onesI = sb("onesI", [P, P])
        pick = sb("pick", [96, 32], BF16)
        bvrow = sb("bvrow", [P, JB, D])
        iota8 = sb("iota8", [P, NE])
        eps = sb("eps", [P, 1])
        one = sb("one", [P, 1])
        R0, R1, R2, R3, R4, R5, R6, R7, R8, R9 = 0, 32, 36, 44, 45, 46, 48, 50, 52, 54
        NROW = 56
        rows = sb("rows", [NROW, P])
        cols = sb("cols", [P, NROW])
        convw = sb("convw", [P, 2, NCONV])
        alog = sb("alog", [P, NS])
        Acol = sb("Acol", [P, NS])
        brow = sb("brow", [1, 3 * D])
        bperm = sb("bperm", [1, 4, P])
        bqk = sb("bqk", [P, 4])
        b1c = cols[:, R0:R2]
        b2c = cols[:, R2:R4]
        boc = cols[:, R4:R5]
        cbc = cols[:, R5:R6]
        bdc = cols[:, R6:R7]
        dpc = cols[:, R7:R8]
        lgc = cols[:, R8:R9]
        lbc = cols[:, R9:NROW]

        xin = sb("xin", [P, JB, D])
        xA = sb("xA", [P, 512])
        xFin = sb("xFin", [P, 512])
        xM = sb("xM", [P, 512])
        acc = sb("acc", [P, 512])
        outS = sb("outS", [P, JB, D])

        xnA = sb("xnA", [P, 512])
        eA = sb("eA", [P, 2, 512])
        sqA = eA[:, 0, :]
        rsA = eA[:, 1, :]
        til = sb("til", [P, 2, 512])
        rot = sb("rot", [P, 512])
        parts = sb("parts", [P, 2, PARTS, 512], BF16)
        qpk = sb("qpk", [P, 2, 2, NC * 512], BF16)
        kpk = sb("kpk", [P, 2, 2, NC * 512], BF16)
        vpad = sb("vpad", [P, JB * NC, 160])

        region = sb("region", [P, 10, 512])
        rP = region[:, 0:8, :].rearrange("p (s c) t -> p s c t", s=2)
        oT = region[:, 8, :]
        ws = region[:, 0:6, :].rearrange("p (s h) t -> p s h t", s=3)
        dAs = region[:, 6:10, :].rearrange("p (s h) t -> p s h t", s=2)

        xnF = sb("xnF", [P, 512])
        sqF = sb("sqF", [P, 512])
        rsF = sb("rsF", [P, 512])
        hF = sb("hF", [P, 4, 512])
        cpk = sb("cpk", [96, 512], BF16)
        mid = sb("mid", [96, 512], BF16)
        cBs = sb("cBs", [P, 512])
        tmp = sb("tmp", [P, 2, 512])
        lg = sb("lg", [P, JB, NE])
        mx8 = sb("mx8", [P, JB, NE])
        ix8 = sb("ix8", [P, JB, NE], U32)
        ixf = sb("ixf", [P, JB, 2])
        gp = sb("gp", [P, 4, JB])
        oh = sb("oh", [P, 2, JB, NE])
        c96 = sb("c96", [P, JB, PARTS, 32])

        xnM = sb("xnM", [P, 512])
        sqM = sb("sqM", [P, 512])
        rsM = sb("rsM", [P, 512])
        xpad = sb("xpad", [P, 2, 3 + 512])
        xcs = sb("xcs", [P, 2, 512])
        zs = sb("zs", [P, 2, 512])
        dte = sb("dte", [P, 2, 512])
        dtx = sb("dtx", [P, 2, 512])
        yM = sb("yM", [P, 2, 512])
        spk = sb("spk", [96, 512], BF16)

        rawin = region[:, 0, :].rearrange("p (e d) -> p e d", e=4)
        rawdt = region[:, 1, :].rearrange("p (o i) -> p o i", o=2)
        rawout = region[:, 2, 0:DI]
        rawx = region[0:2 * NS, 3, 0:DI]
        rawg = region[0:NE, 4, 0:P]
        rawqkv = region[:, 5, 0:3 * D]
        zero16 = region[:, 6:8, :].rearrange("p a t -> p (a t)").bitcast(BF16)

        s_gate = sem("gate")
        s_wload = sem("wload")
        s_wbig = sem("wbig")
        s_consts = sem("consts")
        s_pconst = sem("pconst")
        s_setup_turned = sem("setup_turned")
        s_setup = sem("setup")
        s_zeroed = sem("zeroed")
        s_acol = sem("acol")
        s_x_in = sem("x_in")
        s_x_turned = sem("x_turned")
        s_xA_done = sem("xA_done")
        s_A_mean = sem("A_mean")
        s_A_xc = sem("A_xc")
        s_A_sq = sem("A_sq")
        s_A_var = sem("A_var")
        s_A_rs = sem("A_rs")
        s_A_xn = sem("A_xn")
        s_A_qk = sem("A_qk")
        s_A_exp = sem("A_exp")
        s_A_relu = sem("A_relu")
        s_A_til = sem("A_til")
        s_A_rope = sem("A_rope")
        s_A_split = sem("A_split")
        s_pk = [sem("pk0"), sem("pk1")]
        s_A_v = sem("A_v")
        s_A_vp = sem("A_vp")
        s_q_ld = sem("q_ld")
        s_k_ld = [sem("k_ld0"), sem("k_ld1")]
        s_den = sem("den")
        s_ln = sem("ln")
        s_ex = sem("ex")
        s_num = sem("num")
        s_mul = sem("mul")
        s_av = sem("av")
        s_o_copied = sem("o_copied")
        s_oproj = sem("oproj")
        s_x1_done = sem("x1_done")
        s_F_mean = sem("F_mean")
        s_F_xc = sem("F_xc")
        s_F_sq = sem("F_sq")
        s_F_var = sem("F_var")
        s_F_rs = sem("F_rs")
        s_F_xn = sem("F_xn")
        s_F_log = sem("F_log")
        s_F_route = sem("F_route")
        s_F_ed = sem("F_ed")
        s_F_turn = sem("F_turn")
        s_F_cpk = sem("F_cpk")
        s_up = sem("up")
        s_ge = sem("ge")
        s_dn = sem("dn")
        s_cb = sem("cb")
        s_cbs = sem("cbs")
        s_yv = sem("yv")
        s_fadd = sem("fadd")
        s_out_t = sem("out_t")
        s_out_c = sem("out_c")
        s_out_d = sem("out_d")
        s_M_mean = sem("M_mean")
        s_M_xc = sem("M_xc")
        s_M_sq = sem("M_sq")
        s_M_var = sem("M_var")
        s_M_rs = sem("M_rs")
        s_M_xn = sem("M_xn")
        s_M_ip = sem("M_ip")
        s_M_xp = sem("M_xp")
        s_M_cv = sem("M_cv")
        s_M_si = sem("M_si")
        s_M_dt = sem("M_dt")
        s_M_sp = sem("M_sp")
        s_M_dtr = sem("M_dtr")
        s_M_dtx = sem("M_dtx")
        s_M_ss = sem("M_ss")
        s_M_spk = sem("M_spk")
        s_Bm = sem("Bm")
        s_Cm = sem("Cm")
        s_da = sem("da")
        s_dbx = sem("dbx")
        s_sc = sem("sc")
        s_hc = sem("hc")
        s_ya = sem("ya")
        s_E_mean = sem("E_mean")
        s_E_yc = sem("E_yc")
        s_E_sq = sem("E_sq")
        s_E_var = sem("E_var")
        s_E_rs = sem("E_rs")
        s_E_op = sem("E_op")
        s_E_proj = sem("E_proj")
        s_x3_done = sem("x3_done")

        def floor(v):
            return max(v, 0) if isinstance(v, int) else v

        def settled(eng):
            eng.sem_inc(s_gate, 1)

        N_WLOAD = 26
        N_WBIG = 2 * (NE + 1)
        N_CONST, N_PCONST = 9, 3 + PARTS
        N_ROUTE, N_EOP = 21, 6

        def outs_done(i):
            return max(i - 1, 0) if isinstance(i, int) else i - 1

        def f1(i):
            return i if isinstance(i, int) and i < 2 else 2 * i - 1

        def f2(i):
            return 2 * NB - 1 if isinstance(i, int) and i == NB + 1 else 2 * i - 2

        def phases(run_x, run_y, e):
            for i in (0, 1, 2):
                run_x(i, True, i == 2, i)
                run_y(i, True, i >= 1, True, i + 1)
            with e.Fori(3, NB - 1) as i:
                run_x(i, True, True, i)
                run_y(i, True, True, True, i + 1)
            run_x(NB - 1, True, True, NB - 1)
            run_y(NB - 1, True, True, False, NB)
            run_x(NB, False, True, NB)
            run_y(NB, False, True, False, NB)
            run_x(NB + 1, False, True, NB)

        block = ctx.enter_context(nc.Block())

        @block.sync
        def _(sp):
            def wl(dst, src):
                sp.dma_start(dst, src).then_inc(s_wload, 16)

            wl(rawqkv, w_qkv)
            wl(brow[:, :], b_qkv.rearrange("(a n) -> a n", a=1))
            wl(rawin, W_in.rearrange("(e p) d -> p e d", p=P))
            wl(rawdt, W_dt.rearrange("(o p) i -> p o i", p=P))
            wl(rawout, W_out)
            wl(rawx, W_x)
            wl(rawg, gate_w)
            wl(wos[:, :], w_out)
            wl(ropeC[:, :], rope_cos)
            wl(ropeS[:, :], rope_sin)
            wl(rows[R0:R1, :], b1.rearrange("e (c f) -> (e c) f", f=P))
            wl(rows[R1:R2, :], sb1.rearrange("(c f) -> c f", f=P))
            wl(rows[R2:R3, :], b2)
            wl(rows[R3:R4, :], sb2.rearrange("(a n) -> a n", a=1))
            wl(rows[R4:R5, :], b_out.rearrange("(a n) -> a n", a=1))
            wl(rows[R5:R6, :], conv_b.rearrange("(h n) -> h n", n=P))
            wl(rows[R6:R7, :], b_dt.rearrange("(h n) -> h n", n=P))
            wl(rows[R7:R8, :], D_param.rearrange("(h n) -> h n", n=P))
            wl(rows[R8:R9, :], ln_g.rearrange("(h n) -> h n", n=P))
            wl(rows[R9:NROW, :], ln_b.rearrange("(h n) -> h n", n=P))
            wl(convw[:, :, :], conv_w.rearrange("(h p) a k -> p h (a k)", p=P))
            wl(alog[:, :], A_log.rearrange("(a n) -> a n", a=1).broadcast_to([P, NS]))
            bv = b_qkv[2 * D:3 * D].rearrange("(a n) -> a n", a=1).broadcast_to([P, D])
            for j in range(JB):
                wl(bvrow[:, j, :], bv)
            for e in (NE, *range(NE)):
                w1, w2 = (sW1, sW2) if e == NE else (W1[e], W2[e])
                sp.dma_start(W1s[:, e, :], w1).then_inc(s_wbig, 16)
                sp.dma_start(W2s[:, e, :, :], w2.rearrange("(c f) h -> f c h", f=P)).then_inc(s_wbig, 16)
            sp.wait_ge(s_consts, 1)
            for k2 in range(2):
                for u in range(2):
                    sp.dma_start(qscr[k2, u], zero16).then_inc(s_zeroed, 16)
                    for par in range(2):
                        sp.dma_start(kscr[k2, par, u], zero16).then_inc(s_zeroed, 16)
            sp.wait_ge(s_zeroed, 16 * 12)

            def pre(b, name, n):
                if name == "load":
                    sp.wait_ge(s_x_turned, floor(b))
                    sp.dma_start(xin[:, :, :], x[b].rearrange("(j p) d -> p j d", p=P)).then_inc(s_x_in, 16)
                if name == "rope":
                    for u in range(2):
                        t = 2 * n + u
                        sp.wait_ge(s_A_split, floor(16 * b + 4 * (t + 1)))
                        settled(sp)
                        if t == 0:
                            sp.wait_ge(s_q_ld, floor(32 * b))
                        if t == 2:
                            sp.wait_ge(s_k_ld[0], floor(32 * b))
                            sp.wait_ge(s_k_ld[1], floor(32 * b))
                        rowmap = QROWS if n == 0 else KROWS
                        for par in range(2):
                            for r, part in enumerate(rowmap):
                                row = 64 * par + 8 * r
                                src = parts[64 * par:64 * par + 64, u, part, :]
                                if n == 0:
                                    dst = qscr[:, u, row:row + 8, :]
                                else:
                                    dst = kscr[:, par, u, row:row + 8, :]
                                dst = dst.rearrange("k d (c t) -> k (d c) t", c=NC)
                                sp.dma_start(dst, src).then_inc(s_pk[u], 16)

            def load_k(b, k):
                sp.wait_ge(s_num, floor(UNITS * b + JB * NC * (k - 1)))
                sp.dma_start(kpk[:, k % 2, :, :], kscr[k // 2, k % 2].rearrange("u p n -> p u n")).then_inc(
                    s_k_ld[k % 2], 16)

            def run_x(i, has_a, has_f, b):
                if has_a:
                    sp.wait_ge(s_pk[0], floor(32 * PK_DMAS * (b + 1)))
                    sp.wait_ge(s_pk[1], floor(32 * PK_DMAS * (b + 1)))
                    load_k(b, 0)
                    sp.wait_ge(s_num, floor(UNITS * b))
                    for k2 in range(2):
                        sp.dma_start(qpk[:, k2, :, :], qscr[k2].rearrange("u p n -> p u n")).then_inc(s_q_ld, 16)
                    for k in range(1, NK):
                        load_k(b, k)
                if has_f:
                    sp.wait_ge(s_out_c, floor((i - 2) + 1))
                    settled(sp)
                    sp.dma_start(out[i - 2].rearrange("(j p) d -> p j d", p=P), outS[:, :, :]).then_inc(s_out_d, 16)

            def run_y(i, has_f, has_m, has_p, a_done):
                if has_p:
                    for kind, name, n in Y_ORDER:
                        if kind == "P":
                            pre(i + 1, name, n)

            for name, n in _PRE:
                pre(0, name, n)
            phases(run_x, run_y, sp)
            sp.wait_ge(s_out_d, 16 * NB)

        @block.tensor
        def _(pe):
            def turn_in():
                pe.wait_ge(s_wload, 16 * N_WLOAD)
                pe.wait_ge(s_consts, N_CONST)
                pe.wait_ge(s_pconst, N_PCONST)
                for e in range(4):
                    pe.transpose(ps[0][:, e * P:e * P + P], rawin[:, e, :], ident[:, :])
                for o in range(2):
                    for c in range(2):
                        pe.transpose(ps[1][:, (c * 2 + o) * P:(c * 2 + o) * P + P], rawdt[:, o, c * P:c * P + P], ident[:, :])
                for c in range(2):
                    pe.transpose(ps[2][:, c * P:c * P + P], rawout[:, c * P:c * P + P], ident[:, :])
                    pe.transpose(ps[3][:, c * 2 * NS:(c + 1) * 2 * NS], rawx[:, c * P:c * P + P], ident[0:2 * NS, 0:2 * NS])
                pe.transpose(ps[4][:, 0:NE], rawg, ident[0:NE, 0:NE])
                pe.transpose(ps[5][:, 0:NROW], rows[:, :], ident[0:NROW, 0:NROW])
                pe.wait_ge(s_acol, 2)
                for t in range(4):
                    mm = pe.matmul(ps[6][:, t:t + 1], bperm[:, t, :], one[0:1, :], start=True, stop=True)
                mm.then_inc(s_setup_turned, 1)

            def ones_mm(bank, ones, src, n=1):
                for h in range(n):
                    mm = pe.matmul(ps[bank][:, :], ones[:, :], src[h], start=(h == 0), stop=(h == n - 1))
                return mm

            def pre(b, name, n):
                if name == "load":
                    pe.wait_ge(s_x_in, floor(16 * (b + 1)))
                    pe.wait_ge(s_o_copied, floor(b))
                    for j in range(JB):
                        mm = pe.transpose(ps[3][:, j * P:j * P + P], xin[:, j, :], ident[:, :])
                    mm.then_inc(s_x_turned, 1)
                elif name == "mean":
                    pe.wait_ge(s_xA_done, floor(b + 1))
                    ones_mm(3, onesD, [xA[:, :]]).then_inc(s_A_mean, 1)
                elif name == "var":
                    pe.wait_ge(s_A_sq, floor(b + 1))
                    ones_mm(3, onesD, [sqA]).then_inc(s_A_var, 1)
                elif name == "qk":
                    pe.wait_ge(s_A_xn, floor(b + 1))
                    pe.wait_ge(s_A_exp, floor(4 * b + n))
                    pe.wait_ge(s_A_relu, floor(4 * b + n))
                    pe.matmul(ps[3][:, :], wqk[:, n, :], xnA[:, :], start=True, stop=True).then_inc(s_A_qk, 1)
                elif name == "v":
                    pe.wait_ge(s_A_exp, floor(4 * b + 4))
                    pe.wait_ge(s_A_relu, floor(4 * b + 4))
                    for j in range(JB):
                        mm = pe.matmul(ps[3][:, j * D:j * D + D], xnA[:, j * P:j * P + P], wv[:, :], start=True, stop=True)
                    mm.then_inc(s_A_v, 1)

            def score(b, s, c, u):
                k, jb = divmod(s, JB)
                n = NC * s + c
                if jb == 0 and c == 0:
                    pe.wait_ge(s_k_ld[k % 2], floor(32 * b + 16 * (k // 2) + 16))
                if n == 0:
                    pe.wait_ge(s_q_ld, floor(32 * b + 32))
                lhs = kpk[:, k % 2, u, c * 512 + jb * P:c * 512 + jb * P + P]
                rhs = qpk[:, k // 2, u, c * 512:(c + 1) * 512]
                if u == 0:
                    pe.wait_ge(s_ln, floor(UNITS * b + n - 1))
                    pe.matmul(ps[n % 2][:, :], lhs, rhs, start=True, stop=True).then_inc(s_den, 1)
                else:
                    pe.wait_ge(s_mul, floor(UNITS * b + n))
                    pe.matmul(ps[2][:, :], lhs, rhs, start=True, stop=True).then_inc(s_num, 1)

            def att(b, m_done, name, s):
                if name == "scores":
                    pe.wait_ge(s_x3_done, floor(m_done))
                    pe.wait_ge(s_x1_done, floor(b))
                    for c in range(NC):
                        score(b, 0, c, 0)
                elif name == "den_num":
                    for c in range(NC):
                        if s + 1 < STEPS:
                            score(b, s + 1, c, 0)
                        score(b, s, c, 1)
                elif name == "av":
                    k, jb = divmod(s, JB)
                    if s == 0:
                        pe.wait_ge(s_A_vp, floor(b + 1))
                    for c in range(NC):
                        pe.wait_ge(s_mul, floor(UNITS * b + NC * s + c + 1))
                        mm = pe.matmul(ps[3][32 * c:32 * c + 32, :], vpad[:, jb * NC + c, 32 * k:32 * k + 32],
                                       rP[:, s % 2, c, :], start=(s == 0), stop=(s == STEPS - 1))
                    mm.then_inc(s_av, 1)
                elif name == "close":
                    pe.wait_ge(s_o_copied, floor(b + 1))
                    pe.wait_ge(s_mul, floor(UNITS * (b + 1)))
                    pe.matmul(ps[2][:, :], wos[:, :], oT, start=True, stop=True).then_inc(s_oproj, 1)

            def ffn(f, ready, last_ready, fin, name, q):
                if name == "mean":
                    pe.wait_ge(ready, floor(last_ready))
                    pe.wait_ge(s_yv, floor((NE + 1) * f))
                    pe.wait_ge(s_out_c, floor(fin))
                    ones_mm(7, onesD, [xFin[:, :]]).then_inc(s_F_mean, 1)
                elif name == "var":
                    pe.wait_ge(s_F_sq, floor(f + 1))
                    ones_mm(7, onesD, [sqF[:, :]]).then_inc(s_F_var, 1)
                elif name == "router":
                    pe.wait_ge(s_F_xn, floor(f + 1))
                    for j in range(JB):
                        mm = pe.matmul(ps[7][:, j * NE:j * NE + NE], xnF[:, j * P:j * P + P], gateT[:, :], start=True, stop=True)
                    mm.then_inc(s_F_log, 1)
                elif name == "turn":
                    pe.wait_ge(s_F_route, floor(N_ROUTE * (f + 1)))
                    for j in range(JB):
                        mm = pe.transpose(ps[7][0:96, j * P:j * P + P], c96[:, j, :, :].rearrange("p a b -> p (a b)"), ident[:, :])
                    mm.then_inc(s_F_turn, 1)
                elif name == "ups":
                    for c in range(FC - 1):
                        up(f, FC * q + c)
                elif name == "burst":
                    up(f, FC * q + FC - 1)
                elif name == "spread":
                    pe.wait_ge(s_yv, floor((NE + 1) * f + q))
                    pe.wait_ge(s_F_cpk, floor(5 * (f + 1)))
                    pe.matmul(ps[7][:, :], pick[:, q - 1:q].broadcast_to([96, P]), cpk[:, :], start=True, stop=True).then_inc(s_cb, 1)
                elif name == "downs":
                    if q == 0:
                        pe.wait_ge(s_F_cpk, floor(5 * f + 2))
                    else:
                        pe.wait_ge(s_cbs, floor(NE * f + q))
                    w = NE if q == 0 else q - 1
                    for c in range(FC):
                        n = FC * q + c
                        pe.wait_ge(s_ge, floor(NCH * f + n + 1))
                        pe.matmul(ps[7][:, :], W2s[:, w, c, :], hF[:, n % 4, :], start=(c == 0), stop=(c == FC - 1)).then_inc(s_dn, 1)

            def up(f, n):
                pe.wait_ge(s_ge, floor(NCH * f + n - 2))
                w = NE if n < FC else n // FC - 1
                pe.matmul(ps[4 + n % 3][:, :], W1s[:, w, n % FC * P:n % FC * P + P], xnF[:, :], start=True, stop=True).then_inc(s_up, 1)

            def spread_b(m, s):
                pe.wait_ge(s_dbx, floor(NS * m + s))
                pe.matmul(ps[0][:, :], pick[:, s:s + 1].broadcast_to([96, P]), spk[:, :], start=True, stop=True).then_inc(s_Bm, 1)

            def scan(m, a_done, name, s):
                if name == "mean":
                    pe.wait_ge(s_fadd, floor(NE * (f1(m) + 1)))
                    pe.wait_ge(s_x1_done, floor(a_done))
                    ones_mm(0, onesD, [xM[:, :]]).then_inc(s_M_mean, 1)
                elif name == "var":
                    pe.wait_ge(s_M_sq, floor(m + 1))
                    ones_mm(1, onesD, [sqM[:, :]]).then_inc(s_M_var, 1)
                elif name == "inproj":
                    pe.wait_ge(s_M_xn, floor(m + 1))
                    for e, bank in enumerate((0, 1, 2)):
                        pe.matmul(ps[bank][:, :], WinT[:, e, :], xnM[:, :], start=True, stop=True).then_inc(s_M_ip, 1)
                    pe.wait_ge(s_M_xp, floor(2 * m + 1))
                    pe.matmul(ps[0][:, :], WinT[:, 3, :], xnM[:, :], start=True, stop=True).then_inc(s_M_ip, 1)
                elif name == "dt":
                    pe.wait_ge(s_M_si, floor(4 * m + 4))
                    pe.wait_ge(s_M_xp, floor(2 * m + 2))
                    for o in range(2):
                        for c in range(2):
                            mm = pe.matmul(ps[1 + o][:, :], WdtT[:, c, o * P:o * P + P], xcs[:, c, :], start=(c == 0), stop=(c == 1))
                        mm.then_inc(s_M_dt, 1)
                    for c in range(2):
                        mm = pe.matmul(ps[0][0:96, :], wxT[:, c, :], xcs[:, c, :], start=(c == 0), stop=(c == 1))
                    mm.then_inc(s_M_ss, 1)
                elif name == "unit":
                    if s == 0:
                        pe.wait_ge(s_M_spk, floor(5 * (m + 1)))
                        pe.wait_ge(s_M_dtr, floor(2 * m + 2))
                        pe.wait_ge(s_M_sp, floor(4 * m + 2))
                        spread_b(m, 0)
                    pe.wait_ge(s_hc, floor(NS * m + s))
                    pe.matmul(ps[1][:, :], pick[:, NS + s:NS + s + 1].broadcast_to([96, P]), spk[:, :], start=True, stop=True).then_inc(s_Cm, 1)
                    if s + 1 < NS:
                        spread_b(m, s + 1)
                elif name == "close":
                    pe.wait_ge(s_ya, floor((NS - 1) * (m + 1)))
                    ones_mm(2, onesI, [yM[:, 0, :], yM[:, 1, :]], 2).then_inc(s_E_mean, 1)
                    pe.wait_ge(s_E_sq, floor(m + 1))
                    pe.wait_ge(s_dbx, floor(NS * (m + 1)))
                    ones_mm(0, onesI, [dAs[:, 0, 0, :], dAs[:, 0, 1, :]], 2).then_inc(s_E_var, 1)
                    pe.wait_ge(s_E_op, floor(N_EOP * (m + 1)))
                    for h in range(2):
                        mm = pe.matmul(ps[1][:, :], WoT[:, h, :], yM[:, h, :], start=(h == 0), stop=(h == 1))
                    mm.then_inc(s_E_proj, 1)

            def run_x(i, has_a, has_f, b):
                m_done = i - 1 if not isinstance(i, int) else max(i - 1, 0)
                for kind, name, n in X_ORDER:
                    if kind == "A" and has_a:
                        att(b, m_done, name, n)
                    if kind == "F" and has_f:
                        if name == "close":
                            pe.wait_ge(s_fadd, floor(NE * (f2(i) + 1)))
                            pe.wait_ge(s_yv, floor((NE + 1) * (f2(i) + 1)))
                            for j in range(JB):
                                mm = pe.transpose(ps[7][:, j * P:j * P + P], acc[:, j * P:j * P + P], ident[:, :])
                            mm.then_inc(s_out_t, 1)
                        else:
                            ffn(f2(i), s_x3_done, i - 1, i - 2, name, n)

            def run_y(i, has_f, has_m, has_p, a_done):
                for kind, name, n in Y_ORDER:
                    if kind == "F" and has_f:
                        ffn(f1(i), s_x1_done, i + 1, outs_done(i), name, n)
                    if kind == "M" and has_m:
                        scan(i - 1, a_done, name, n)
                    if kind == "P" and has_p:
                        pre(i + 1, name, n)

            turn_in()
            pe.wait_ge(s_setup, 1)
            for name, n in _PRE:
                pre(0, name, n)
            pe.wait_ge(s_wbig, 16 * N_WBIG)
            phases(run_x, run_y, pe)

        @block.scalar
        def _(act):
            def a(out_, in_, fn, **kw):
                return nc.scalar.activation(out_, in_, fn, **kw)

            act.preload_act_table_set(LOG_EXP)
            act.wait_ge(s_wload, 16 * N_WLOAD)
            a(Acol[:, :], alog[:, :], ACT.Exp).then_inc(s_acol, 1)

            def rstd(s_var, s_rs, b, dst, bank):
                act.wait_ge(s_var, floor(b + 1))
                a(dst, ps[bank][:, :], ACT.Ln, bias=eps[:, :]).then_inc(s_rs, 1)
                act.wait_ge(s_rs, floor(2 * b + 1))
                a(dst, dst, ACT.Exp, scale=-0.5).then_inc(s_rs, 1)

            def pre(b, name, n):
                if name == "load":
                    act.wait_ge(s_x_turned, floor(b + 1))
                    act.wait_ge(s_x1_done, floor(b))
                    a(xA[:, :], ps[3][:, :], ACT.Copy).then_inc(s_xA_done, 1)
                elif name == "mean":
                    act.wait_ge(s_A_xc, floor(b + 1))
                    a(sqA, xnA[:, :], ACT.Square).then_inc(s_A_sq, 1)
                elif name == "var":
                    rstd(s_A_var, s_A_rs, b, rsA, 3)
                elif name == "qk":
                    act.wait_ge(s_A_relu, floor(4 * b + n + 1))
                    act.wait_ge(s_A_til, floor(4 * b + n - 1))
                    a(eA[:, n % 2, :], ps[3][:, :], ACT.Exp, bias=bqk[:, n:n + 1]).then_inc(s_A_exp, 1)

            def logs(b, s):
                act.wait_ge(s_av, floor(STEPS * b + s - 1))
                for c in range(NC):
                    n = NC * s + c
                    act.wait_ge(s_den, floor(UNITS * b + n + 1))
                    a(rP[:, s % 2, c, :], ps[n % 2][:, :], ACT.Ln).then_inc(s_ln, 1)
                act.wait_ge(s_ln, floor(UNITS * b + NC * (s + 1)))
                a(rP[:, s % 2, :, :], rP[:, s % 2, :, :], ACT.Exp, scale=-1.0).then_inc(s_ex, 1)

            def att(b, m_done, name, s):
                if name == "scores":
                    act.wait_ge(s_x3_done, floor(m_done))
                    act.wait_ge(s_oproj, floor(b))
                    logs(b, 0)
                elif name == "den_num" and s + 1 < STEPS:
                    logs(b, s + 1)
                elif name == "close":
                    act.wait_ge(s_av, floor(STEPS * (b + 1)))
                    a(oT, ps[3][:, :], ACT.Copy).then_inc(s_o_copied, 1)

            def ffn(f, name, q):
                if name == "mean":
                    act.wait_ge(s_F_xc, floor(f + 1))
                    a(sqF[:, :], xnF[:, :], ACT.Square).then_inc(s_F_sq, 1)
                elif name == "var":
                    rstd(s_F_var, s_F_rs, f, rsF[:, :], 7)
                elif name == "router":
                    act.wait_ge(s_F_route, floor(N_ROUTE * f + 10))
                    a(gp[:, 1, :], gp[:, 0, :], ACT.Exp).then_inc(s_F_ed, 1)
                elif name == "burst":
                    act.preload_act_table_set(GELU_SET)
                    w = NE if q == 0 else q - 1
                    for c in range(FC):
                        n = FC * q + c
                        act.wait_ge(s_up, floor(NCH * f + n + 1))
                        act.wait_ge(s_dn, floor(NCH * f + n - 3))
                        a(hF[:, n % 4, :], ps[4 + n % 3][:, :], ACT.Gelu, bias=b1c[:, w * FC + c:w * FC + c + 1]).then_inc(s_ge, 1)
                    act.preload_act_table_set(LOG_EXP)

            def scan(m, a_done, name, s):
                if name == "mean":
                    act.wait_ge(s_M_xc, floor(m + 1))
                    a(sqM[:, :], xnM[:, :], ACT.Square).then_inc(s_M_sq, 1)
                elif name == "var":
                    rstd(s_M_var, s_M_rs, m, rsM[:, :], 1)
                elif name == "silu":
                    act.preload_act_table_set(SILU_SET)
                    act.wait_ge(s_x3_done, floor(m))
                    act.wait_ge(s_M_cv, floor(8 * m + 8))
                    for h in range(2):
                        a(xcs[:, h, :], xcs[:, h, :], ACT.Silu).then_inc(s_M_si, 1)
                    act.wait_ge(s_M_ip, floor(4 * m + 4))
                    a(zs[:, 0, :], ps[2][:, :], ACT.Silu).then_inc(s_M_si, 1)
                    a(zs[:, 1, :], ps[0][:, :], ACT.Silu).then_inc(s_M_si, 1)
                    act.preload_act_table_set(LOG_EXP)
                elif name == "dt":
                    act.wait_ge(s_x1_done, floor(a_done))
                    for o in range(2):
                        act.wait_ge(s_M_dtr, floor(2 * m + o + 1))
                        a(ws[:, 0, o, :], ps[1 + o][:, :], ACT.Abs, bias=bdc[:, o:o + 1]).then_inc(s_M_sp, 1)
                    act.wait_ge(s_M_sp, floor(4 * m + 2))
                    a(ws[:, 0, :, :], ws[:, 0, :, :], ACT.Exp, scale=-1.0).then_inc(s_M_sp, 1)
                    act.wait_ge(s_M_sp, floor(4 * m + 3))
                    a(ws[:, 0, :, :], ws[:, 0, :, :], ACT.Ln, bias=1.0).then_inc(s_M_sp, 1)
                elif name == "unit":
                    if s == 0:
                        act.wait_ge(s_M_dtx, floor(3 * (m + 1)))
                    act.wait_ge(s_sc, floor(NS * m + s - 1))
                    a(dAs[:, s % 2, :, :], dte[:, :, :], ACT.Exp, scale=Acol[:, s:s + 1]).then_inc(s_da, 1)
                elif name == "close":
                    act.wait_ge(s_E_yc, floor(m + 1))
                    act.wait_ge(s_sc, floor(NS * (m + 1)))
                    a(dAs[:, 0, :, :], yM[:, :, :], ACT.Square).then_inc(s_E_sq, 1)
                    rstd(s_E_var, s_E_rs, m, rsM[:, :], 0)

            def run_x(i, has_a, has_f, b):
                m_done = i - 1 if not isinstance(i, int) else max(i - 1, 0)
                for kind, name, n in X_ORDER:
                    if kind == "A" and has_a:
                        att(b, m_done, name, n)
                    if kind == "F" and has_f:
                        if name == "close":
                            act.wait_ge(s_out_t, floor((i - 2) + 1))
                            act.wait_ge(s_out_d, floor(16 * (i - 2)))
                            a(outS[:, :, :], ps[7][:, :].rearrange("p (j d) -> p j d", j=JB), ACT.Copy).then_inc(s_out_c, 1)
                        else:
                            ffn(f2(i), name, n)

            def run_y(i, has_f, has_m, has_p, a_done):
                for kind, name, n in Y_ORDER:
                    if kind == "F" and has_f:
                        ffn(f1(i), name, n)
                    if kind == "M" and has_m:
                        scan(i - 1, a_done, name, n)
                    if kind == "P" and has_p:
                        pre(i + 1, name, n)

            act.wait_ge(s_setup, 1)
            for name, n in _PRE:
                pre(0, name, n)
            phases(run_x, run_y, act)

        @block.vector
        def _(v):
            v.memset(zero16, 0.0).then_inc(s_consts, 1)
            v.memset(onesD[:, :], 1.0 / D).then_inc(s_consts, 1)
            v.memset(onesI[:, :], 1.0 / DI).then_inc(s_consts, 1)
            v.memset(eps[:, :], EPS).then_inc(s_consts, 1)
            v.memset(one[:, :], 1.0).then_inc(s_consts, 1)
            for e in range(NE):
                ins = v.memset(iota8[:, e:e + 1], float(e))
            ins.then_inc(s_consts, 1)
            v.memset(vpad[:, :, :], 0.0).then_inc(s_consts, 1)
            v.memset(c96[:, :, :, :], 0.0).then_inc(s_consts, 1)
            v.memset(xpad[:, :, 0:3], 0.0).then_inc(s_consts, 1)
            v.wait_ge(s_wload, 16 * N_WLOAD)
            src = rawqkv.rearrange("p (s c k r m e) -> p s r e k m c", s=3, c=NC, k=2, r=2, m=HD // 2)
            dst = wqk[:, :, :].rearrange("p u (r k m e c) -> p u r e k m c", r=2, k=2, m=HD // 2, e=2)
            bsrc = brow[:, :].rearrange("p (s c k r m e) -> p s r e k m c", s=3, c=NC, k=2, r=2, m=HD // 2)
            bdst = bperm[:, :, :].rearrange("p u (r k m e c) -> p u r e k m c", r=2, k=2, m=HD // 2, e=2)
            for u in range(4):
                for r in range(2):
                    for e in range(2):
                        f = e if u % 2 == 0 else 1 - e
                        v.tensor_copy(bdst[:, u, r, e], bsrc[:, u // 2, r, f])
                        ins = v.tensor_copy(dst[:, u, r, e], src[:, u // 2, r, f])
            v.tensor_copy(wv[:, :], rawqkv[:, 2 * D:3 * D])
            v.wait_ge(s_acol, 1)
            v.tensor_scalar(Acol[:, :], Acol[:, :], -1.0, None, ALU.mult).then_inc(s_acol, 1)
            v.wait_ge(s_setup_turned, 1)
            v.tensor_copy(WinT[:, :, :], ps[0][:, :].rearrange("p (e m) -> p e m", e=4))
            v.tensor_copy(WdtT[:, :, :], ps[1][:, :].rearrange("p (c o) -> p c o", c=2))
            v.tensor_copy(WoT[:, :, :], ps[2][:, 0:DI].rearrange("p (c d) -> p c d", c=2))
            for r in range(PARTS):
                v.tensor_copy(wxT[:, :, r * 2 * NS:(r + 1) * 2 * NS], ps[3][:, 0:4 * NS].rearrange("p (c s) -> p c s", c=2))
            v.tensor_copy(gateT[:, :], ps[4][:, 0:NE])
            v.tensor_copy(cols[:, :], ps[5][:, 0:NROW])
            v.tensor_copy(bqk[:, :], ps[6][:, 0:4]).then_inc(s_setup, 1)

            def pre(b, name, n):
                if name == "mean":
                    v.wait_ge(s_A_mean, floor(b + 1))
                    v.wait_ge(s_A_v, floor(b))
                    v.wait_ge(s_xA_done, floor(b + 1))
                    v.tensor_tensor(xnA[:, :], xA[:, :], ps[3][:, :], ALU.subtract).then_inc(s_A_xc, 1)
                elif name == "var":
                    v.wait_ge(s_A_rs, floor(2 * b + 2))
                    v.wait_ge(s_A_sq, floor(b + 1))
                    v.tensor_tensor(xnA[:, :], xnA[:, :], rsA, ALU.mult).then_inc(s_A_xn, 1)
                elif name == "qk":
                    v.wait_ge(s_A_qk, floor(4 * b + n + 1))
                    if n % 2 == 0:
                        v.wait_ge(s_A_split, floor(16 * b + 4 * n - 4))
                    else:
                        v.wait_ge(s_A_rope, floor(6 * b + 3 * (n // 2)))
                    v.tensor_scalar(til[:, n % 2, :], ps[3][:, :], bqk[:, n:n + 1], 0.0, ALU.add, ALU.max).then_inc(s_A_relu, 1)
                    v.wait_ge(s_A_relu, floor(4 * b + n + 1))
                    v.wait_ge(s_A_exp, floor(4 * b + n + 1))
                    v.scalar_tensor_tensor(til[:, n % 2, :], eA[:, n % 2, :], 1.0, til[:, n % 2, :], ALU.min, ALU.add).then_inc(s_A_til, 1)
                elif name == "v":
                    v.wait_ge(s_A_v, floor(b + 1))
                    v.wait_ge(s_av, floor(STEPS * b))
                    v.tensor_tensor(vpad[:, :, :].rearrange("p g (k w) -> p g k w", w=40)[:, :, :, 0:HD],
                                    ps[3][:, :].rearrange("p (g k d) -> p g k d", g=JB * NC, k=NK),
                                    bvrow[:, :, :].rearrange("p j (c k d) -> p (j c) k d", c=NC, k=NK), ALU.add).then_inc(s_A_vp, 1)

            def att(b, name, s):
                if name == "den_num":
                    v.wait_ge(s_ex, floor(STEPS * b + s + 1))
                    for c in range(NC):
                        v.wait_ge(s_num, floor(UNITS * b + NC * s + c + 1))
                        v.tensor_tensor(rP[:, s % 2, c, :], ps[2][:, :], rP[:, s % 2, c, :], ALU.mult).then_inc(s_mul, 1)

            def att_close(b, f_before):
                v.wait_ge(s_oproj, floor(b + 1))
                v.wait_ge(s_yv, floor(f_before))
                v.scalar_tensor_tensor(xFin[:, :], ps[2][:, :], boc, xA[:, :], ALU.add, ALU.add).then_inc(s_x1_done, 1)

            def split_rows(src, pk, rest, base, chain):
                v.tensor_copy(pk[:, :], src).then_inc(chain, 1)
                v.wait_ge(chain, floor(base + 1))
                v.tensor_tensor(rest, src, pk[:, :], ALU.subtract).then_inc(chain, 1)
                v.wait_ge(chain, floor(base + 2))
                v.tensor_copy(mid[64:96, :], rest[64:96]).then_inc(chain, 1)
                v.tensor_copy(pk[32:64, :], rest[32:64]).then_inc(chain, 1)
                v.wait_ge(chain, floor(base + 4))
                v.tensor_tensor(pk[64:96, :], rest[64:96], mid[64:96, :], ALU.subtract).then_inc(chain, 1)

            def ffn(f, in_place, acc_free, name, q):
                if name == "mean":
                    v.wait_ge(s_F_mean, floor(f + 1))
                    v.wait_ge(s_up, floor(NCH * f))
                    v.tensor_tensor(xnF[:, :], xFin[:, :], ps[7][:, :], ALU.subtract).then_inc(s_F_xc, 1)
                elif name == "var":
                    v.wait_ge(s_F_rs, floor(2 * f + 2))
                    v.tensor_tensor(xnF[:, :], xnF[:, :], rsF[:, :], ALU.mult).then_inc(s_F_xn, 1)
                elif name == "router":
                    base = N_ROUTE * f
                    count = [0]

                    def step(ins, wait=True):
                        ins.then_inc(s_F_route, 1)
                        count[0] += 1
                        if wait:
                            v.wait_ge(s_F_route, floor(base + count[0]))

                    v.wait_ge(s_F_log, floor(f + 1))
                    step(v.tensor_copy(lg[:, :, :], ps[7][:, 0:JB * NE].rearrange("p (j e) -> p j e", j=JB)))
                    settled(v)
                    for j in range(JB):
                        step(v.max(mx8[:, j, :], lg[:, j, :]), j == JB - 1)
                    settled(v)
                    for j in range(JB):
                        step(v.max_index(ix8[:, j, :], mx8[:, j, :], lg[:, j, :]), False)
                    step(v.tensor_tensor(gp[:, 0, :], mx8[:, :, 1], mx8[:, :, 0], ALU.subtract), False)
                    assert count[0] == 10
                    v.wait_ge(s_F_route, floor(base + 9))
                    step(v.tensor_copy(ixf[:, :, :], ix8[:, :, 0:2]), False)
                    v.wait_ge(s_F_ed, floor(f + 1))
                    step(v.tensor_scalar(gp[:, 2, :], gp[:, 1, :], 1.0, None, ALU.add))
                    step(v.reciprocal(gp[:, 2, :], gp[:, 2, :]))
                    step(v.tensor_tensor(gp[:, 3, :], gp[:, 1, :], gp[:, 2, :], ALU.mult))
                    wide = [P, JB, NE]
                    for t in range(2):
                        step(v.tensor_tensor(oh[:, t, :, :], iota8[:, :].unsqueeze(1).broadcast_to(wide),
                                             ixf[:, :, t:t + 1].broadcast_to(wide), ALU.is_equal), t == 1)
                    for t in range(2):
                        step(v.tensor_tensor(oh[:, t, :, :], oh[:, t, :, :],
                                             gp[:, 2 + t, :].unsqueeze(2).broadcast_to(wide), ALU.mult), t == 1)
                    v.wait_ge(s_F_turn, floor(f))
                    for r in range(PARTS):
                        step(v.tensor_tensor(c96[:, :, r, 0:NE], oh[:, 0, :, :], oh[:, 1, :, :], ALU.add), False)
                    assert count[0] == N_ROUTE
                elif name == "turn":
                    v.wait_ge(s_F_turn, floor(f + 1))
                    v.wait_ge(s_cb, floor(NE * f))
                    v.wait_ge(s_F_var, floor(f + 1))
                    split_rows(ps[7][0:96, :], cpk, sqF[0:96, :], 5 * f, s_F_cpk)
                elif name == "spread":
                    v.wait_ge(s_cb, floor(NE * f + q))
                    v.tensor_copy(cBs[:, :], ps[7][:, :]).then_inc(s_cbs, 1)
                elif name == "downs":
                    v.wait_ge(s_dn, floor(NCH * f + FC * (q + 1)))
                    if q == 0:
                        v.wait_ge(s_fadd, floor(NE * f))
                        v.wait_ge(s_out_t, floor(acc_free))
                        v.scalar_tensor_tensor(acc[:, :], ps[7][:, :], b2c[:, NE:NE + 1], xFin[:, :], ALU.add, ALU.add).then_inc(s_yv, 1)
                    else:
                        v.wait_ge(s_cbs, floor(NE * f + q))
                        v.wait_ge(s_fadd, floor(NE * f + q - 2))
                        v.scalar_tensor_tensor(tmp[:, q % 2, :], ps[7][:, :], b2c[:, q - 1:q], cBs[:, :], ALU.add, ALU.mult).then_inc(s_yv, 1)

            def scan(m, a_done, name, s):
                if name == "mean":
                    v.wait_ge(s_M_mean, floor(m + 1))
                    v.wait_ge(s_M_ip, floor(4 * m))
                    v.tensor_tensor(xnM[:, :], xM[:, :], ps[0][:, :], ALU.subtract).then_inc(s_M_xc, 1)
                elif name == "var":
                    v.wait_ge(s_M_rs, floor(2 * m + 2))
                    v.tensor_tensor(xnM[:, :], xnM[:, :], rsM[:, :], ALU.mult).then_inc(s_M_xn, 1)
                elif name == "inproj":
                    for h in range(2):
                        v.wait_ge(s_M_ip, floor(4 * m + 1 + h))
                        v.wait_ge(s_M_cv, floor(8 * m))
                        v.tensor_copy(xpad[:, h, 3:515], ps[h][:, :]).then_inc(s_M_xp, 1)
                elif name == "conv":
                    v.wait_ge(s_M_xp, floor(2 * m + 2))
                    for k in range(NCONV):
                        for h in range(2):
                            src = xpad[:, h, k:k + 512]
                            if k == 0:
                                v.tensor_scalar(xcs[:, h, :], src, convw[:, h, 0:1], cbc[:, h:h + 1], ALU.mult, ALU.add).then_inc(s_M_cv, 1)
                            else:
                                v.wait_ge(s_M_cv, floor(8 * m + 2 * (k - 1) + h + 1))
                                v.scalar_tensor_tensor(xcs[:, h, :], src, convw[:, h, k:k + 1], xcs[:, h, :], ALU.mult, ALU.add).then_inc(s_M_cv, 1)
                elif name == "dt":
                    for o in range(2):
                        v.wait_ge(s_M_dt, floor(2 * m + o + 1))
                        v.tensor_scalar(dte[:, o, :], ps[1 + o][:, :], bdc[:, o:o + 1], 0.0, ALU.add, ALU.max).then_inc(s_M_dtr, 1)
                    v.wait_ge(s_M_sp, floor(4 * m + 4))
                    v.wait_ge(s_M_dtr, floor(2 * m + 2))
                    v.tensor_tensor(dte[:, :, :], dte[:, :, :], ws[:, 0, :, :], ALU.add).then_inc(s_M_dtx, 1)
                    v.wait_ge(s_M_dtx, floor(3 * m + 1))
                    v.tensor_tensor(dtx[:, :, :], dte[:, :, :], xcs[:, :, :], ALU.mult).then_inc(s_M_dtx, 1)
                    v.wait_ge(s_M_dtx, floor(3 * m + 2))
                    v.memset(dte[:, :, 0:1], RESET).then_inc(s_M_dtx, 1)
                elif name == "state":
                    v.wait_ge(s_M_ss, floor(m + 1))
                    v.wait_ge(s_Cm, floor(NS * m))
                    v.wait_ge(s_M_var, floor(m + 1))
                    split_rows(ps[0][0:96, :], spk, sqM[0:96, :], 5 * m, s_M_spk)
                elif name == "unit":
                    both = [P, 2, 512]
                    w = ws[:, s % 3, :, :]
                    if s == 0:
                        dbx(m, 0)
                    v.wait_ge(s_da, floor(NS * m + s + 1))
                    v.wait_ge(s_dbx, floor(NS * m + s + 1))
                    v.tensor_tensor_scan(w.rearrange("p h t -> p (h t)"), dAs[:, s % 2, :, :].rearrange("p h t -> p (h t)"),
                                         w.rearrange("p h t -> p (h t)"), 0.0, ALU.mult, ALU.add).then_inc(s_sc, 1)
                    if s + 1 < NS:
                        dbx(m, s + 1)
                    v.wait_ge(s_Cm, floor(NS * m + s + 1))
                    v.wait_ge(s_sc, floor(NS * m + s + 1))
                    dst = yM[:, :, :] if s == 0 else w
                    v.tensor_tensor(dst, ps[1][:, :].unsqueeze(1).broadcast_to(both), w, ALU.mult).then_inc(s_hc, 1)
                elif name == "close":
                    both = [P, 2, 512]
                    v.wait_ge(s_E_mean, floor(m + 1))
                    v.tensor_tensor(yM[:, :, :], yM[:, :, :], ps[2][:, :].unsqueeze(1).broadcast_to(both), ALU.subtract).then_inc(s_E_yc, 1)
                    v.wait_ge(s_E_rs, floor(2 * m + 2))
                    base = N_EOP * m
                    v.tensor_tensor(yM[:, :, :], yM[:, :, :], rsM[:, :].unsqueeze(1).broadcast_to(both), ALU.mult).then_inc(s_E_op, 1)
                    v.wait_ge(s_E_op, floor(base + 1))
                    for h in range(2):
                        v.tensor_scalar(yM[:, h, :], yM[:, h, :], lgc[:, h:h + 1], lbc[:, h:h + 1], ALU.mult, ALU.add).then_inc(s_E_op, 1)
                    for h in range(2):
                        v.wait_ge(s_E_op, floor(base + 2 + h))
                        v.scalar_tensor_tensor(yM[:, h, :], xcs[:, h, :], dpc[:, h:h + 1], yM[:, h, :], ALU.mult, ALU.add).then_inc(s_E_op, 1)
                    v.wait_ge(s_E_op, floor(base + 5))
                    v.tensor_tensor(yM[:, :, :], yM[:, :, :], zs[:, :, :], ALU.mult).then_inc(s_E_op, 1)

            def scan_close(m, f_before):
                v.wait_ge(s_E_proj, floor(m + 1))
                v.wait_ge(s_yv, floor(f_before))
                v.tensor_tensor(xFin[:, :], ps[1][:, :], xM[:, :], ALU.add).then_inc(s_x3_done, 1)

            def dbx(m, s):
                v.wait_ge(s_Bm, floor(NS * m + s + 1))
                if s >= 3:
                    v.wait_ge(s_ya, floor((NS - 1) * m + s - 3))
                v.tensor_tensor(ws[:, s % 3, :, :], ps[0][:, :].unsqueeze(1).broadcast_to([P, 2, 512]), dtx[:, :, :], ALU.mult).then_inc(s_dbx, 1)

            def run_x(i, has_a, has_f, b):
                for kind, name, n in X_ORDER:
                    if kind == "A" and has_a:
                        if name == "close":
                            att_close(b, (NE + 1) * f2(i) + 1 if has_f else 0)
                        else:
                            att(b, name, n)
                    if kind == "F" and has_f and name != "close":
                        ffn(f2(i), True, outs_done(i - 1), name, n)

            def run_y(i, has_f, has_m, has_p, a_done):
                for kind, name, n in Y_ORDER:
                    if kind == "F" and has_f:
                        ffn(f1(i), False, outs_done(i), name, n)
                    if kind == "M" and has_m:
                        scan(i - 1, a_done, name, n)
                        if name == "close":
                            scan_close(i - 1, (NE + 1) * f1(i) + 1 if has_f else 0)
                    if kind == "P" and has_p:
                        pre(i + 1, name, n)

            for name, n in _PRE:
                pre(0, name, n)
            phases(run_x, run_y, v)

        @block.gpsimd
        def _(pool):
            g = nc.gpsimd
            g.memset(ident[:, :], 0.0).then_inc(s_pconst, 1)
            g.memset(pick[:, :], 0.0).then_inc(s_pconst, 1)
            pool.wait_ge(s_pconst, 2)
            g.affine_select(out=ident[:, :], in_=ident[:, :], compare_op=ALU.not_equal, fill=1.0, base=0,
                            pattern=[[-1, P]], channel_multiplier=1).then_inc(s_pconst, 1)
            for r in range(PARTS):
                pool.wait_ge(s_pconst, floor(3 + r))
                g.affine_select(out=pick[:, :], in_=pick[:, :], compare_op=ALU.not_equal, fill=1.0, base=-32 * r,
                                pattern=[[-1, 32]], channel_multiplier=1).then_inc(s_pconst, 1)

            def cast(dst, src):
                return g.tensor_scalar(dst, src, 1.0, 1.0, ALU.mult, ALU.mult)

            def split(b, t, src):
                slot = t % 2
                base = 16 * b + 4 * t
                pool.wait_ge(s_pk[slot], floor(16 * PK_DMAS * (2 * b + t // 2)))
                settled(pool)
                cast(parts[:, slot, 0, :], src).then_inc(s_A_split, 1)
                pool.wait_ge(s_A_split, floor(base + 1))
                g.tensor_tensor(src, src, parts[:, slot, 0, :], ALU.subtract).then_inc(s_A_split, 1)
                pool.wait_ge(s_A_split, floor(base + 2))
                settled(pool)
                cast(parts[:, slot, 1, :], src).then_inc(s_A_split, 1)
                pool.wait_ge(s_A_split, floor(base + 3))
                g.tensor_tensor(parts[:, slot, 2, :], src, parts[:, slot, 1, :], ALU.subtract).then_inc(s_A_split, 1)

            def pre(b, name, n):
                if name == "rope":
                    pool.wait_ge(s_A_til, floor(4 * b + 2 * n + 2))
                    pool.wait_ge(s_A_split, floor(16 * b + 8 * n))
                    g.tensor_tensor(rot[:, :], til[:, 0, :], ropeC[:, :], ALU.mult).then_inc(s_A_rope, 1)
                    g.tensor_tensor(til[:, 1, :], til[:, 1, :], ropeS[:, :], ALU.mult).then_inc(s_A_rope, 1)
                    pool.wait_ge(s_A_rope, floor(6 * b + 3 * n + 2))
                    g.tensor_tensor(rot[:, :], rot[:, :], til[:, 1, :], ALU.add).then_inc(s_A_rope, 1)
                    split(b, 2 * n, til[:, 0, :])
                    pool.wait_ge(s_A_rope, floor(6 * b + 3 * n + 3))
                    split(b, 2 * n + 1, rot[:, :])

            def ffn(f, dst, name, q):
                if (name == "downs" and 1 <= q < NE) or name == "close":
                    pool.wait_ge(s_yv, floor((NE + 1) * f + q + 1))
                    pool.wait_ge(s_fadd, floor(NE * f + q - 1))
                    g.tensor_tensor(dst, acc[:, :], tmp[:, q % 2, :], ALU.add).then_inc(s_fadd, 1)

            def run_x(i, has_a, has_f, b):
                for kind, name, n in X_ORDER:
                    if kind == "F" and has_f:
                        ffn(f2(i), acc[:, :], name, NE if name == "close" else n)

            def run_y(i, has_f, has_m, has_p, a_done):
                for kind, name, n in Y_ORDER:
                    if kind == "F" and has_f:
                        if name == "close":
                            pool.wait_ge(s_x3_done, floor(i))
                            ffn(f1(i), xM[:, :], name, NE)
                        else:
                            ffn(f1(i), acc[:, :], name, n)
                    if kind == "M" and has_m and name == "unit" and n >= 1:
                        m = i - 1
                        pool.wait_ge(s_hc, floor(NS * m + n + 1))
                        pool.wait_ge(s_ya, floor((NS - 1) * m + n - 1))
                        g.tensor_tensor(yM[:, :, :], yM[:, :, :], ws[:, n % 3, :, :], ALU.add).then_inc(s_ya, 1)
                    if kind == "P" and has_p:
                        pre(i + 1, name, n)

            for name, n in _PRE:
                pre(0, name, n)
            phases(run_x, run_y, pool)


_INS = ['L0_attn_a_x', 'L0_attn_a_w_qkv', 'L0_attn_a_b_qkv', 'L0_attn_a_w_out', 'L0_attn_a_b_out',
        'L0_attn_b_W_in', 'L0_attn_b_conv_w', 'L0_attn_b_conv_b', 'L0_attn_b_W_x', 'L0_attn_b_W_dt', 'L0_attn_b_b_dt',
        'L0_attn_b_A_log', 'L0_attn_b_D_param', 'L0_attn_b_W_out', 'L0_attn_b_ln_g', 'L0_attn_b_ln_b',
        'L0_ffn_gate_w', 'L0_ffn_W1', 'L0_ffn_b1', 'L0_ffn_W2', 'L0_ffn_b2',
        'L0_ffn_sW1', 'L0_ffn_sb1', 'L0_ffn_sW2', 'L0_ffn_sb2']


def rope_tables(n_tokens):
    half = HD // 2
    theta = (1.0 / np.float32(1250) ** (np.arange(half, dtype=np.float32) / np.float32(half))).astype(np.float32)
    angles = np.arange(n_tokens, dtype=np.float32)[:, None] * theta[None, :]
    dim = (np.arange(P) // NC) % HD
    sign = np.where(dim % 2 == 0, np.float32(-1), np.float32(1))
    cos = np.cos(angles).astype(np.float32).T[dim // 2]
    sin = sign[:, None] * np.sin(angles).astype(np.float32).T[dim // 2]
    return np.ascontiguousarray(cos), np.ascontiguousarray(sin.astype(np.float32))


def kernel(**inputs):
    import concourse.bacc as _bacc
    from concourse.bass_utils import run_bass_kernel_spmd as _run

    nc = _bacc.Bacc("TRN2", target_bir_lowering=False, num_devices=1)
    arrays, args = {}, []
    cos, sin = rope_tables(inputs[_INS[0]].shape[1])
    for name, a in [(n, inputs[n]) for n in _INS] + [("rope_cos", cos), ("rope_sin", sin)]:
        a = np.ascontiguousarray(a)
        arrays[f"in_{name}"] = a
        args.append(nc.dram_tensor(f"in_{name}", a.shape, mybir.dt.from_np(a.dtype), kind="ExternalInput").ap())
    out = nc.dram_tensor("out_0", inputs[_INS[0]].shape, F32, kind="ExternalOutput").ap()
    hybrid_layer_kernel(nc, *args, out)
    r = _run(nc, [arrays], core_ids=[0])
    return r.results[0]["out_0"]
```

```python
from contextlib import ExitStack

import numpy as np

import concourse.bass as bass
from concourse import mybir

F32 = mybir.dt.float32
BF16 = mybir.dt.bfloat16
U32 = mybir.dt.uint32
ALU = mybir.AluOpType
ACT = mybir.ActivationFunctionType
LOG_EXP = "natural_log_exp_and_others"
GELU_SET = "gelu_and_others"
SILU_SET = "silu_and_others"

P = 128
D = 128
NH, HD = 16, 8
NE, FF = 8, 512
FC = FF // P
NCH = (NE + 1) * FC
DI = 256
NS = 16
NCONV = 4
EPS = 1e-5
JB = 4
NC = 4
NK = 4
STEPS = NK * JB
UNITS = STEPS * NC
PARTS = 3
QROWS = (0, 0, 1, 1, 0, 2)
KROWS = (0, 1, 0, 1, 2, 0)
PK_DMAS = 2 * len(QROWS)
RESET = 1e30

PASS = """
    E.norm_mean E.norm_var A.first A.unit E.gate A.unit*3 G.mean A.unit A.av A.unit*2 G.var A.unit A.av A.unit*2
    G.router G.up*2 A.unit*2 A.av A.unit G.burst G.up A.unit G.turn A.unit G.up*2 G.down*2 A.unit G.down*2 G.up
    M.take G.up A.av G.spread G.up G.burst A.unit G.up A.unit G.down A.unit G.up A.unit A.av A.unit G.down A.unit
    G.down A.unit*2 A.av A.unit G.burst G.down G.up G.spread A.unit G.up*2 A.unit G.down A.unit G.down*2 A.unit
    A.av A.unit G.down G.burst G.up*2 G.spread A.unit G.up*2 A.unit A.av G.up A.unit G.down A.unit G.down A.unit*2
    A.av G.down*2 G.burst G.up*2 A.unit G.spread G.up A.unit G.up A.unit*2 A.av A.unit G.down A.unit*2 G.down
    A.unit G.down A.av A.unit G.down G.burst A.unit G.up A.unit G.up*2 G.spread G.up*2 A.unit G.down*2 A.av
    G.down*2 G.burst G.up A.unit G.spread G.up A.unit G.down A.unit*2 A.av A.unit G.down A.unit G.down A.unit G.up
    A.unit G.burst G.down G.up A.unit A.av G.spread G.up G.down A.unit G.down*2 A.unit G.up A.unit G.burst G.down
    A.av A.unit G.up*2 A.unit G.spread M.mean A.unit G.up G.down A.unit G.down A.av G.down*2 A.close M.var G.close
    F.mean M.inproj M.conv F.var M.silu F.router F.up P.load M.dt F.up*2 F.turn F.up F.burst M.state F.up F.down
    P.mean F.down*2 M.unit F.burst F.up*2 F.down F.up M.unit F.up F.spread P.var F.up*2 M.unit F.down*2 F.burst
    F.down*2 P.qk F.up F.spread M.unit F.up*2 F.down*3 M.unit F.down F.up*2 F.burst M.unit P.qk P.rope F.spread
    F.up P.til F.up P.til M.unit F.up F.down*2 F.burst F.down P.qk P.split F.up M.unit F.down F.up P.til F.spread
    F.up M.unit F.down P.qk F.down F.up F.down P.split M.unit F.down P.v F.up F.burst F.spread M.unit F.down*2
    P.til P.rope F.down*2 F.up*2 M.unit F.spread F.up*3 F.burst F.up P.split M.unit F.up F.down F.burst F.down
    P.split F.down*2 F.up F.spread F.up M.unit F.up F.down M.unit F.up F.burst F.down*2 M.unit F.down F.up
    F.spread F.down*4
"""


def numbered(text):
    order, count = [], {}
    for word in text.split():
        part, _, times = word.partition("*")
        for _ in range(int(times or 1)):
            count[part] = count.get(part, -1) + 1
            stage, name = part.split(".")
            order.append((stage, name, count[part] + (name == "spread")))
    return order


ORDER = numbered(PASS)
assert sum(part[:2] == ("A", "unit") for part in ORDER) == UNITS
HEAD_ORDER = [("load", 0), ("mean", 0), ("var", 0), ("qk", 0), ("til", 0), ("qk", 1), ("til", 1), ("rope", 0), ("split", 0), ("qk", 2),
              ("til", 2), ("split", 1), ("qk", 3), ("til", 3), ("rope", 1), ("split", 2), ("v", 0), ("split", 3)]


def hybrid_layer_kernel(nc: bass.Bass, x, w_qkv, b_qkv, w_out, b_out, W_in, conv_w, conv_b, W_x, W_dt, b_dt, A_log,
                        D_param, W_out, ln_g, ln_b, gate_w, W1, b1, W2, b2, sW1, sb1, sW2, sb2,
                        rope_cos, rope_sin, out):
    NB, T, _ = x.shape
    assert T == JB * P and T == 512

    ctx = ExitStack()
    with ctx:
        def sb(name, shape, dt=F32):
            return ctx.enter_context(nc.sbuf_tensor(name, shape, dt))

        def sem(name):
            return ctx.enter_context(nc.semaphore(name))

        ps = [ctx.enter_context(nc.psum_tensor(f"bank{i}", [P, 512], F32)) for i in range(8)]

        qscr = nc.dram_tensor("qscr", (2, 2, P, NC * 512), BF16, kind="Internal").ap()
        kscr = nc.dram_tensor("kscr", (2, 2, 2, P, NC * 512), BF16, kind="Internal").ap()

        W1s = sb("W1s", [P, NE + 1, FF])
        W2s = sb("W2s", [P, NE + 1, FC, D])
        wqk = sb("wqk", [P, 4, P])
        wv = sb("wv", [P, D])
        wos = sb("wos", [P, D])
        WinT = sb("WinT", [P, 4, P])
        WdtT = sb("WdtT", [P, 2, DI])
        WoT = sb("WoT", [P, 2, D])
        wxT = sb("wxT", [P, 2, PARTS * 2 * NS])
        gateT = sb("gateT", [P, NE])
        ropeC = sb("ropeC", [P, 512])
        ropeS = sb("ropeS", [P, 512])
        ident = sb("ident", [P, P])
        onesD = sb("onesD", [P, P])
        onesI = sb("onesI", [P, P])
        pick = sb("pick", [96, 32], BF16)
        bvrow = sb("bvrow", [P, JB, D])
        iota8 = sb("iota8", [P, NE])
        eps = sb("eps", [P, 1])
        one = sb("one", [P, 1])
        R0, R1, R2, R3, R4, R5, R6, R7, R8, R9 = 0, 32, 36, 44, 45, 46, 48, 50, 52, 54
        NROW = 56
        rows = sb("rows", [NROW, P])
        cols = sb("cols", [P, NROW])
        convw = sb("convw", [P, 2, NCONV])
        alog = sb("alog", [P, NS])
        Acol = sb("Acol", [P, NS])
        brow = sb("brow", [1, 3 * D])
        bperm = sb("bperm", [1, 4, P])
        bqk = sb("bqk", [P, 4])
        b1c = cols[:, R0:R2]
        b2c = cols[:, R2:R4]
        boc = cols[:, R4:R5]
        cbc = cols[:, R5:R6]
        bdc = cols[:, R6:R7]
        dpc = cols[:, R7:R8]
        lgc = cols[:, R8:R9]
        lbc = cols[:, R9:NROW]

        xA = sb("xA", [P, 512])
        xFin = sb("xFin", [P, 512])
        xM = sb("xM", [P, 512])
        acc = sb("acc", [P, 512])

        xnA = sb("xnA", [P, 512])
        eA = sb("eA", [P, 2, 512])
        sqA = eA[:, 0, :]
        rsA = eA[:, 1, :]
        outS = eA[:, 0, :].rearrange("p (j d) -> p j d", j=JB)
        xin = eA[:, 1, :].rearrange("p (j d) -> p j d", j=JB)
        til = sb("til", [P, 4, 512])
        rot = sb("rot", [P, 512])
        parts = sb("parts", [P, 2, PARTS, 512], BF16)
        qpk = sb("qpk", [P, 2, 2, NC * 512], BF16)
        kpk = sb("kpk", [P, 2, 2, NC * 512], BF16)
        vpad = sb("vpad", [P, JB * NC, 160])

        region = sb("region", [P, 10, 512])
        rP = region[:, 0:8, :].rearrange("p (s c) t -> p s c t", s=2)
        oT = region[:, 8, :]
        ws = region[:, 0:6, :].rearrange("p (s h) t -> p s h t", s=3)
        dAs = region[:, 6:10, :].rearrange("p (s h) t -> p s h t", s=2)
        sqE = region[:, 8:10, :]

        xnF = sb("xnF", [P, 512])
        sqF = sb("sqF", [P, 512])
        rsF = sb("rsF", [P, 512])
        hF = sb("hF", [P, 4, 512])
        cpk = sb("cpk", [96, 512], BF16)
        mid = sb("mid", [96, 512], BF16)
        cBs = sb("cBs", [P, 512])
        tmp = sb("tmp", [P, 2, 512])
        lg = sb("lg", [P, JB, NE])
        mx8 = sb("mx8", [P, JB, NE])
        ix8 = sb("ix8", [P, JB, NE], U32)
        ixf = sb("ixf", [P, JB, 2])
        gp = sb("gp", [P, 4, JB])
        oh = sb("oh", [P, 2, JB, NE])
        c96 = sb("c96", [P, JB, PARTS, 32])

        xnM = sb("xnM", [P, 512])
        sqM = region[:, 9, :]
        rsM = sb("rsM", [P, 512])
        xpad = sb("xpad", [P, 2, 3 + 512])
        xcs = sb("xcs", [P, 2, 512])
        zs = sb("zs", [P, 2, 512])
        dte = sb("dte", [P, 2, 512])
        dtx = sb("dtx", [P, 2, 512])
        yM = sb("yM", [P, 2, 512])
        spk = sb("spk", [96, 512], BF16)

        rawin = region[:, 0, :].rearrange("p (e d) -> p e d", e=4)
        rawdt = region[:, 1, :].rearrange("p (o i) -> p o i", o=2)
        rawout = region[:, 2, 0:DI]
        rawx = region[0:2 * NS, 3, 0:DI]
        rawg = region[0:NE, 4, 0:P]
        rawqkv = region[:, 5, 0:3 * D]
        zero16 = region[:, 6:8, :].rearrange("p a t -> p (a t)").bitcast(BF16)

        s_gate = sem("gate")
        s_wload = sem("wload")
        s_wbig = sem("wbig")
        s_consts = sem("consts")
        s_pconst = sem("pconst")
        s_setup_turned = sem("setup_turned")
        s_setup = sem("setup")
        s_zeroed = sem("zeroed")
        s_acol = sem("acol")
        s_x_in = sem("x_in")
        s_x_turned = sem("x_turned")
        s_xA_done = sem("xA_done")
        s_A_mean = sem("A_mean")
        s_A_xc = sem("A_xc")
        s_A_sq = sem("A_sq")
        s_A_var = sem("A_var")
        s_A_rs = sem("A_rs")
        s_A_xn = sem("A_xn")
        s_A_qk = sem("A_qk")
        s_A_exp = sem("A_exp")
        s_A_relu = sem("A_relu")
        s_A_til = sem("A_til")
        s_A_rope = sem("A_rope")
        s_A_split = sem("A_split")
        s_pk = [sem("pk0"), sem("pk1")]
        s_A_v = sem("A_v")
        s_A_vp = sem("A_vp")
        s_q_ld = sem("q_ld")
        s_k_ld = [sem("k_ld0"), sem("k_ld1")]
        s_den = sem("den")
        s_ln = sem("ln")
        s_ex = sem("ex")
        s_num = sem("num")
        s_mul = sem("mul")
        s_av = sem("av")
        s_o_copied = sem("o_copied")
        s_oproj = sem("oproj")
        s_x1_done = sem("x1_done")
        s_F_mean = sem("F_mean")
        s_F_xc = sem("F_xc")
        s_F_sq = sem("F_sq")
        s_F_var = sem("F_var")
        s_F_rs = sem("F_rs")
        s_F_xn = sem("F_xn")
        s_F_log = sem("F_log")
        s_F_route = sem("F_route")
        s_F_ed = sem("F_ed")
        s_F_turn = sem("F_turn")
        s_F_cpk = sem("F_cpk")
        s_up = sem("up")
        s_ge = sem("ge")
        s_dn = sem("dn")
        s_cb = sem("cb")
        s_cbs = sem("cbs")
        s_yv = sem("yv")
        s_fadd = sem("fadd")
        s_out_t = sem("out_t")
        s_out_c = sem("out_c")
        s_out_d = sem("out_d")
        s_M_mean = sem("M_mean")
        s_M_xc = sem("M_xc")
        s_M_sq = sem("M_sq")
        s_M_var = sem("M_var")
        s_M_rs = sem("M_rs")
        s_M_xn = sem("M_xn")
        s_M_ip = sem("M_ip")
        s_M_xp = sem("M_xp")
        s_M_cv = sem("M_cv")
        s_M_si = sem("M_si")
        s_M_dt = sem("M_dt")
        s_M_sp = sem("M_sp")
        s_M_dtr = sem("M_dtr")
        s_M_dtx = sem("M_dtx")
        s_M_ss = sem("M_ss")
        s_M_spk = sem("M_spk")
        s_Bm = sem("Bm")
        s_Cm = sem("Cm")
        s_da = sem("da")
        s_dbx = sem("dbx")
        s_sc = sem("sc")
        s_hc = sem("hc")
        s_ya = sem("ya")
        s_E_mean = sem("E_mean")
        s_E_yc = sem("E_yc")
        s_E_sq = sem("E_sq")
        s_E_var = sem("E_var")
        s_E_rs = sem("E_rs")
        s_E_op = sem("E_op")
        s_E_proj = sem("E_proj")
        s_x3_done = sem("x3_done")

        def floor(v):
            return max(v, 0) if isinstance(v, int) else v

        def settled(eng):
            eng.sem_inc(s_gate, 1)

        N_WLOAD = 26
        N_WBIG = 2 * (NE + 1)
        N_CONST, N_PCONST = 9, 3 + PARTS
        N_ROUTE, N_EOP = 21, 6

        def outs_done(i):
            return max(i - 1, 0) if isinstance(i, int) else i - 1

        def f1(i):
            return i if isinstance(i, int) and i < 2 else 2 * i - 1

        def f2(i):
            return 2 * NB - 1 if isinstance(i, int) and i == NB + 1 else 2 * i - 2

        def heads(i):
            return min(i + 1, NB) if isinstance(i, int) else i + 1

        def passes(run, e):
            for i in (0, 1, 2):
                run(i, True, i >= 1, i == 2, True)
            with e.Fori(3, NB - 1) as i:
                run(i, True, True, True, True)
            run(NB - 1, True, True, True, False)
            run(NB, False, True, True, False)
            run(NB + 1, False, False, True, False)

        block = ctx.enter_context(nc.Block())

        @block.sync
        def _(sp):
            def wl(dst, src):
                sp.dma_start(dst, src).then_inc(s_wload, 16)

            wl(rawqkv, w_qkv)
            wl(brow[:, :], b_qkv.rearrange("(a n) -> a n", a=1))
            wl(rawin, W_in.rearrange("(e p) d -> p e d", p=P))
            wl(rawdt, W_dt.rearrange("(o p) i -> p o i", p=P))
            wl(rawout, W_out)
            wl(rawx, W_x)
            wl(rawg, gate_w)
            wl(wos[:, :], w_out)
            wl(ropeC[:, :], rope_cos)
            wl(ropeS[:, :], rope_sin)
            wl(rows[R0:R1, :], b1.rearrange("e (c f) -> (e c) f", f=P))
            wl(rows[R1:R2, :], sb1.rearrange("(c f) -> c f", f=P))
            wl(rows[R2:R3, :], b2)
            wl(rows[R3:R4, :], sb2.rearrange("(a n) -> a n", a=1))
            wl(rows[R4:R5, :], b_out.rearrange("(a n) -> a n", a=1))
            wl(rows[R5:R6, :], conv_b.rearrange("(h n) -> h n", n=P))
            wl(rows[R6:R7, :], b_dt.rearrange("(h n) -> h n", n=P))
            wl(rows[R7:R8, :], D_param.rearrange("(h n) -> h n", n=P))
            wl(rows[R8:R9, :], ln_g.rearrange("(h n) -> h n", n=P))
            wl(rows[R9:NROW, :], ln_b.rearrange("(h n) -> h n", n=P))
            wl(convw[:, :, :], conv_w.rearrange("(h p) a k -> p h (a k)", p=P))
            wl(alog[:, :], A_log.rearrange("(a n) -> a n", a=1).broadcast_to([P, NS]))
            bv = b_qkv[2 * D:3 * D].rearrange("(a n) -> a n", a=1).broadcast_to([P, D])
            for j in range(JB):
                wl(bvrow[:, j, :], bv)
            for e in (NE, *range(NE)):
                w1, w2 = (sW1, sW2) if e == NE else (W1[e], W2[e])
                sp.dma_start(W1s[:, e, :], w1).then_inc(s_wbig, 16)
                sp.dma_start(W2s[:, e, :, :], w2.rearrange("(c f) h -> f c h", f=P)).then_inc(s_wbig, 16)
            sp.wait_ge(s_consts, 1)
            for k2 in range(2):
                for u in range(2):
                    sp.dma_start(qscr[k2, u], zero16).then_inc(s_zeroed, 16)
                    for par in range(2):
                        sp.dma_start(kscr[k2, par, u], zero16).then_inc(s_zeroed, 16)
            sp.wait_ge(s_zeroed, 16 * 12)

            def load_x(b):
                sp.wait_ge(s_x_turned, floor(b))
                settled(sp)
                sp.wait_ge(s_A_til, floor(4 * b))
                settled(sp)
                sp.dma_start(xin, x[b].rearrange("(j p) d -> p j d", p=P)).then_inc(s_x_in, 16)

            def pre(b, name, t):
                if name == "split":
                    n, u = divmod(t, 2)
                    sp.wait_ge(s_A_split, floor(16 * b + 4 * (t + 1)))
                    settled(sp)
                    if t == 0:
                        sp.wait_ge(s_q_ld, floor(32 * b))
                    if t == 2:
                        sp.wait_ge(s_k_ld[0], floor(32 * b))
                        sp.wait_ge(s_k_ld[1], floor(32 * b))
                    rowmap = QROWS if n == 0 else KROWS
                    for par in range(2):
                        for r, part in enumerate(rowmap):
                            row = 64 * par + 8 * r
                            src = parts[64 * par:64 * par + 64, u, part, :]
                            if n == 0:
                                dst = qscr[:, u, row:row + 8, :]
                            else:
                                dst = kscr[:, par, u, row:row + 8, :]
                            dst = dst.rearrange("k d (c t) -> k (d c) t", c=NC)
                            sp.dma_start(dst, src).then_inc(s_pk[u], 16)

            def load_k(b, k):
                sp.wait_ge(s_num, floor(UNITS * b + JB * NC * (k - 1)))
                sp.dma_start(kpk[:, k % 2, :, :], kscr[k // 2, k % 2].rearrange("u p n -> p u n")).then_inc(
                    s_k_ld[k % 2], 16)

            def run(i, has_a, has_m, has_2, has_p):
                if has_a:
                    sp.wait_ge(s_pk[0], floor(32 * PK_DMAS * (i + 1)))
                    sp.wait_ge(s_pk[1], floor(32 * PK_DMAS * (i + 1)))
                    load_k(i, 0)
                    sp.wait_ge(s_num, floor(UNITS * i))
                    for k2 in range(2):
                        sp.dma_start(qpk[:, k2, :, :], qscr[k2].rearrange("u p n -> p u n")).then_inc(s_q_ld, 16)
                    load_k(i, 1)
                if has_p:
                    load_x(i + 1)
                if has_a:
                    for k in range(2, NK):
                        load_k(i, k)
                if has_2:
                    sp.wait_ge(s_out_c, floor((i - 2) + 1))
                    settled(sp)
                    sp.dma_start(out[i - 2].rearrange("(j p) d -> p j d", p=P), outS).then_inc(s_out_d, 16)
                if has_p:
                    for kind, name, n in ORDER:
                        if kind == "P":
                            pre(i + 1, name, n)

            load_x(0)
            for name, n in HEAD_ORDER:
                pre(0, name, n)
            passes(run, sp)
            sp.wait_ge(s_out_d, 16 * NB)

        @block.tensor
        def _(pe):
            def turn_in():
                pe.wait_ge(s_wload, 16 * N_WLOAD)
                pe.wait_ge(s_consts, N_CONST)
                pe.wait_ge(s_pconst, N_PCONST)
                for e in range(4):
                    pe.transpose(ps[0][:, e * P:e * P + P], rawin[:, e, :], ident[:, :])
                for o in range(2):
                    for c in range(2):
                        pe.transpose(ps[1][:, (c * 2 + o) * P:(c * 2 + o) * P + P], rawdt[:, o, c * P:c * P + P], ident[:, :])
                for c in range(2):
                    pe.transpose(ps[2][:, c * P:c * P + P], rawout[:, c * P:c * P + P], ident[:, :])
                    pe.transpose(ps[3][:, c * 2 * NS:(c + 1) * 2 * NS], rawx[:, c * P:c * P + P], ident[0:2 * NS, 0:2 * NS])
                pe.transpose(ps[4][:, 0:NE], rawg, ident[0:NE, 0:NE])
                pe.transpose(ps[5][:, 0:NROW], rows[:, :], ident[0:NROW, 0:NROW])
                pe.wait_ge(s_acol, 2)
                for t in range(4):
                    mm = pe.matmul(ps[6][:, t:t + 1], bperm[:, t, :], one[0:1, :], start=True, stop=True)
                mm.then_inc(s_setup_turned, 1)

            def ones_mm(bank, ones, src, n=1):
                for h in range(n):
                    mm = pe.matmul(ps[bank][:, :], ones[:, :], src[h], start=(h == 0), stop=(h == n - 1))
                return mm

            def pre(b, name, n):
                if name == "load":
                    pe.wait_ge(s_x_in, floor(16 * (b + 1)))
                    pe.wait_ge(s_o_copied, floor(b))
                    for j in range(JB):
                        mm = pe.transpose(ps[3][:, j * P:j * P + P], xin[:, j, :], ident[:, :])
                    mm.then_inc(s_x_turned, 1)
                elif name == "mean":
                    pe.wait_ge(s_xA_done, floor(b + 1))
                    ones_mm(3, onesD, [xA[:, :]]).then_inc(s_A_mean, 1)
                elif name == "var":
                    pe.wait_ge(s_A_sq, floor(b + 1))
                    ones_mm(3, onesD, [sqA]).then_inc(s_A_var, 1)
                elif name == "qk":
                    pe.wait_ge(s_A_xn, floor(b + 1))
                    pe.wait_ge(s_A_exp, floor(4 * b + n))
                    pe.wait_ge(s_A_relu, floor(4 * b + n))
                    pe.matmul(ps[3][:, :], wqk[:, n, :], xnA[:, :], start=True, stop=True).then_inc(s_A_qk, 1)
                elif name == "v":
                    pe.wait_ge(s_A_exp, floor(4 * b + 4))
                    pe.wait_ge(s_A_relu, floor(4 * b + 4))
                    for j in range(JB):
                        mm = pe.matmul(ps[3][:, j * D:j * D + D], xnA[:, j * P:j * P + P], wv[:, :], start=True, stop=True)
                    mm.then_inc(s_A_v, 1)

            def score(b, s, c, u):
                k, jb = divmod(s, JB)
                n = NC * s + c
                if jb == 0 and c == 0:
                    pe.wait_ge(s_k_ld[k % 2], floor(32 * b + 16 * (k // 2) + 16))
                if n == 0:
                    pe.wait_ge(s_q_ld, floor(32 * b + 32))
                lhs = kpk[:, k % 2, u, c * 512 + jb * P:c * 512 + jb * P + P]
                rhs = qpk[:, k // 2, u, c * 512:(c + 1) * 512]
                if u == 0:
                    pe.wait_ge(s_ln, floor(UNITS * b + n - 1))
                    pe.matmul(ps[n % 2][:, :], lhs, rhs, start=True, stop=True).then_inc(s_den, 1)
                else:
                    pe.wait_ge(s_mul, floor(UNITS * b + n))
                    pe.matmul(ps[2][:, :], lhs, rhs, start=True, stop=True).then_inc(s_num, 1)

            def att(b, m_done, name, s):
                if name == "first":
                    pe.wait_ge(s_dbx, floor(NS * m_done))
                    pe.wait_ge(s_hc, floor(NS * m_done))
                    for c in range(NC):
                        score(b, 0, c, 0)
                elif name == "unit":
                    step, c = divmod(s, NC)
                    if step + 1 < STEPS:
                        score(b, step + 1, c, 0)
                    score(b, step, c, 1)
                elif name == "av":
                    k, jb = divmod(s, JB)
                    if s == 0:
                        pe.wait_ge(s_A_vp, floor(b + 1))
                        pe.wait_ge(s_x3_done, floor(m_done))
                    for c in range(NC):
                        pe.wait_ge(s_mul, floor(UNITS * b + NC * s + c + 1))
                        mm = pe.matmul(ps[3][32 * c:32 * c + 32, :], vpad[:, jb * NC + c, 32 * k:32 * k + 32],
                                       rP[:, s % 2, c, :], start=(s == 0), stop=(s == STEPS - 1))
                    mm.then_inc(s_av, 1)
                elif name == "close":
                    pe.wait_ge(s_o_copied, floor(b + 1))
                    pe.wait_ge(s_mul, floor(UNITS * (b + 1)))
                    pe.matmul(ps[2][:, :], wos[:, :], oT, start=True, stop=True).then_inc(s_oproj, 1)

            def ffn(f, ready, last_ready, fin, name, q):
                if name == "mean":
                    pe.wait_ge(ready, floor(last_ready))
                    pe.wait_ge(s_yv, floor((NE + 1) * f))
                    pe.wait_ge(s_out_c, floor(fin))
                    ones_mm(7, onesD, [xFin[:, :]]).then_inc(s_F_mean, 1)
                elif name == "var":
                    pe.wait_ge(s_F_sq, floor(f + 1))
                    ones_mm(7, onesD, [sqF[:, :]]).then_inc(s_F_var, 1)
                elif name == "router":
                    pe.wait_ge(s_F_xn, floor(f + 1))
                    for j in range(JB):
                        mm = pe.matmul(ps[7][:, j * NE:j * NE + NE], xnF[:, j * P:j * P + P], gateT[:, :], start=True, stop=True)
                    mm.then_inc(s_F_log, 1)
                elif name == "turn":
                    pe.wait_ge(s_F_route, floor(N_ROUTE * (f + 1)))
                    for j in range(JB):
                        mm = pe.transpose(ps[7][0:96, j * P:j * P + P], c96[:, j, :, :].rearrange("p a b -> p (a b)"), ident[:, :])
                    mm.then_inc(s_F_turn, 1)
                elif name == "up":
                    pe.wait_ge(s_ge, floor(NCH * f + q - 2))
                    w = NE if q < FC else q // FC - 1
                    pe.matmul(ps[4 + q % 3][:, :], W1s[:, w, q % FC * P:q % FC * P + P], xnF[:, :], start=True, stop=True).then_inc(s_up, 1)
                elif name == "spread":
                    pe.wait_ge(s_yv, floor((NE + 1) * f + q))
                    pe.wait_ge(s_F_cpk, floor(5 * (f + 1)))
                    pe.matmul(ps[7][:, :], pick[:, q - 1:q].broadcast_to([96, P]), cpk[:, :], start=True, stop=True).then_inc(s_cb, 1)
                elif name == "down":
                    e, c = divmod(q, FC)
                    if c == 0 and e == 0:
                        pe.wait_ge(s_F_cpk, floor(5 * f + 2))
                    elif c == 0:
                        pe.wait_ge(s_cbs, floor(NE * f + e))
                    pe.wait_ge(s_ge, floor(NCH * f + q + 1))
                    pe.matmul(ps[7][:, :], W2s[:, NE if e == 0 else e - 1, c, :], hF[:, q % 4, :], start=(c == 0), stop=(c == FC - 1)).then_inc(s_dn, 1)

            def spread_b(m, s):
                pe.wait_ge(s_dbx, floor(NS * m + s))
                pe.matmul(ps[0][:, :], pick[:, s:s + 1].broadcast_to([96, P]), spk[:, :], start=True, stop=True).then_inc(s_Bm, 1)

            def scan(m, a_done, name, s):
                if name == "mean":
                    pe.wait_ge(s_fadd, floor(NE * (f1(m) + 1)))
                    pe.wait_ge(s_ln, floor(UNITS * a_done))
                    ones_mm(0, onesD, [xM[:, :]]).then_inc(s_M_mean, 1)
                elif name == "var":
                    pe.wait_ge(s_M_sq, floor(m + 1))
                    ones_mm(1, onesD, [sqM]).then_inc(s_M_var, 1)
                elif name == "inproj":
                    pe.wait_ge(s_M_xn, floor(m + 1))
                    pe.wait_ge(s_x1_done, floor(a_done))
                    for e, bank in enumerate((0, 1, 2)):
                        pe.matmul(ps[bank][:, :], WinT[:, e, :], xnM[:, :], start=True, stop=True).then_inc(s_M_ip, 1)
                    pe.wait_ge(s_M_xp, floor(2 * m + 1))
                    pe.matmul(ps[0][:, :], WinT[:, 3, :], xnM[:, :], start=True, stop=True).then_inc(s_M_ip, 1)
                elif name == "dt":
                    pe.wait_ge(s_M_si, floor(4 * m + 4))
                    pe.wait_ge(s_M_xp, floor(2 * m + 2))
                    for o in range(2):
                        for c in range(2):
                            mm = pe.matmul(ps[1 + o][:, :], WdtT[:, c, o * P:o * P + P], xcs[:, c, :], start=(c == 0), stop=(c == 1))
                        mm.then_inc(s_M_dt, 1)
                    for c in range(2):
                        mm = pe.matmul(ps[0][0:96, :], wxT[:, c, :], xcs[:, c, :], start=(c == 0), stop=(c == 1))
                    mm.then_inc(s_M_ss, 1)
                elif name == "unit":
                    if s == 0:
                        pe.wait_ge(s_M_spk, floor(5 * (m + 1)))
                        pe.wait_ge(s_M_dtr, floor(2 * m + 2))
                        pe.wait_ge(s_M_sp, floor(4 * m + 2))
                        spread_b(m, 0)
                    pe.wait_ge(s_hc, floor(NS * m + s))
                    pe.matmul(ps[1][:, :], pick[:, NS + s:NS + s + 1].broadcast_to([96, P]), spk[:, :], start=True, stop=True).then_inc(s_Cm, 1)
                    if s + 1 < NS:
                        spread_b(m, s + 1)

            def scan_norm(m, v_done, name):
                if name == "norm_mean":
                    pe.wait_ge(s_ya, floor((NS - 1) * (m + 1)))
                    pe.wait_ge(s_A_vp, floor(v_done))
                    ones_mm(3, onesI, [yM[:, 0, :], yM[:, 1, :]], 2).then_inc(s_E_mean, 1)
                elif name == "norm_var":
                    pe.wait_ge(s_E_sq, floor(m + 1))
                    ones_mm(3, onesI, [sqE[:, 0, :], sqE[:, 1, :]], 2).then_inc(s_E_var, 1)
                elif name == "gate":
                    pe.wait_ge(s_E_op, floor(N_EOP * (m + 1)))
                    for h in range(2):
                        mm = pe.matmul(ps[3][:, :], WoT[:, h, :], yM[:, h, :], start=(h == 0), stop=(h == 1))
                    mm.then_inc(s_E_proj, 1)

            def run(i, has_a, has_m, has_2, has_p):
                for kind, name, n in ORDER:
                    if kind == "A" and has_a:
                        att(i, i - 1, name, n)
                    if kind == "E" and has_2:
                        scan_norm(i - 2, heads(i), name)
                    if kind == "G" and has_2:
                        if name == "close":
                            pe.wait_ge(s_fadd, floor(NE * (f2(i) + 1)))
                            pe.wait_ge(s_yv, floor((NE + 1) * (f2(i) + 1)))
                            for j in range(JB):
                                mm = pe.transpose(ps[7][:, j * P:j * P + P], acc[:, j * P:j * P + P], ident[:, :])
                            mm.then_inc(s_out_t, 1)
                        else:
                            ffn(f2(i), s_x3_done, i - 1, i - 2, name, n)
                    if kind == "F" and has_a:
                        ffn(f1(i), s_x1_done, i + 1, outs_done(i), name, n)
                    if kind == "M" and has_m:
                        scan(i - 1, heads(i), name, n)
                    if kind == "P" and has_p:
                        pre(i + 1, name, n)

            turn_in()
            pe.wait_ge(s_setup, 1)
            for name, n in HEAD_ORDER:
                pre(0, name, n)
            pe.wait_ge(s_wbig, 16 * N_WBIG)
            passes(run, pe)

        @block.scalar
        def _(act):
            def a(out_, in_, fn, **kw):
                return nc.scalar.activation(out_, in_, fn, **kw)

            act.preload_act_table_set(LOG_EXP)
            act.wait_ge(s_wload, 16 * N_WLOAD)
            a(Acol[:, :], alog[:, :], ACT.Exp).then_inc(s_acol, 1)

            def rstd(s_var, s_rs, b, dst, bank):
                act.wait_ge(s_var, floor(b + 1))
                a(dst, ps[bank][:, :], ACT.Ln, bias=eps[:, :]).then_inc(s_rs, 1)
                act.wait_ge(s_rs, floor(2 * b + 1))
                a(dst, dst, ACT.Exp, scale=-0.5).then_inc(s_rs, 1)

            def pre(b, name, n):
                if name == "load":
                    act.wait_ge(s_x_turned, floor(b + 1))
                    act.wait_ge(s_x1_done, floor(b))
                    a(xA[:, :], ps[3][:, :], ACT.Copy).then_inc(s_xA_done, 1)
                elif name == "mean":
                    act.wait_ge(s_A_xc, floor(b + 1))
                    act.wait_ge(s_out_d, floor(16 * (b - 2)))
                    a(sqA, xnA[:, :], ACT.Square).then_inc(s_A_sq, 1)
                elif name == "var":
                    rstd(s_A_var, s_A_rs, b, rsA, 3)
                elif name == "qk":
                    act.wait_ge(s_A_relu, floor(4 * b + n + 1))
                    act.wait_ge(s_A_til, floor(4 * b + n - 1))
                    a(eA[:, n % 2, :], ps[3][:, :], ACT.Exp, bias=bqk[:, n:n + 1]).then_inc(s_A_exp, 1)

            def invert(b, s, c):
                n = NC * s + c
                if c == 0:
                    act.wait_ge(s_av, floor(STEPS * b + s - 1))
                act.wait_ge(s_den, floor(UNITS * b + n + 1))
                a(rP[:, s % 2, c, :], ps[n % 2][:, :], ACT.Ln).then_inc(s_ln, 1)
                if c == NC - 1:
                    act.wait_ge(s_ln, floor(UNITS * b + n + 1))
                    a(rP[:, s % 2, :, :], rP[:, s % 2, :, :], ACT.Exp, scale=-1.0).then_inc(s_ex, 1)

            def att(b, m_done, name, s):
                if name == "first":
                    act.wait_ge(s_ya, floor((NS - 1) * m_done))
                    act.wait_ge(s_sc, floor(NS * m_done))
                    for c in range(NC):
                        invert(b, 0, c)
                elif name == "unit" and s + NC < UNITS:
                    invert(b, s // NC + 1, s % NC)
                elif name == "close":
                    act.wait_ge(s_av, floor(STEPS * (b + 1)))
                    act.wait_ge(s_oproj, floor(b))
                    a(oT, ps[3][:, :], ACT.Copy).then_inc(s_o_copied, 1)

            def ffn(f, name, q):
                if name == "mean":
                    act.wait_ge(s_F_xc, floor(f + 1))
                    a(sqF[:, :], xnF[:, :], ACT.Square).then_inc(s_F_sq, 1)
                elif name == "var":
                    rstd(s_F_var, s_F_rs, f, rsF[:, :], 7)
                elif name == "router":
                    act.wait_ge(s_F_route, floor(N_ROUTE * f + 10))
                    a(gp[:, 1, :], gp[:, 0, :], ACT.Exp).then_inc(s_F_ed, 1)
                elif name == "burst":
                    act.preload_act_table_set(GELU_SET)
                    w = NE if q == 0 else q - 1
                    for c in range(FC):
                        n = FC * q + c
                        act.wait_ge(s_up, floor(NCH * f + n + 1))
                        act.wait_ge(s_dn, floor(NCH * f + n - 3))
                        a(hF[:, n % 4, :], ps[4 + n % 3][:, :], ACT.Gelu, bias=b1c[:, w * FC + c:w * FC + c + 1]).then_inc(s_ge, 1)
                    act.preload_act_table_set(LOG_EXP)

            def decay(m, s):
                act.wait_ge(s_sc, floor(NS * m + s - 1))
                if s == 1:
                    act.wait_ge(s_M_spk, floor(5 * (m + 1)))
                a(dAs[:, s % 2, :, :], dte[:, :, :], ACT.Exp, scale=Acol[:, s:s + 1]).then_inc(s_da, 1)

            def scan(m, a_done, name, s):
                if name == "mean":
                    act.wait_ge(s_M_xc, floor(m + 1))
                    a(sqM, xnM[:, :], ACT.Square).then_inc(s_M_sq, 1)
                elif name == "var":
                    rstd(s_M_var, s_M_rs, m, rsM[:, :], 1)
                elif name == "silu":
                    act.preload_act_table_set(SILU_SET)
                    act.wait_ge(s_x3_done, floor(m))
                    act.wait_ge(s_M_cv, floor(8 * m + 8))
                    for h in range(2):
                        a(xcs[:, h, :], xcs[:, h, :], ACT.Silu).then_inc(s_M_si, 1)
                    act.wait_ge(s_M_ip, floor(4 * m + 4))
                    a(zs[:, 0, :], ps[2][:, :], ACT.Silu).then_inc(s_M_si, 1)
                    a(zs[:, 1, :], ps[0][:, :], ACT.Silu).then_inc(s_M_si, 1)
                    act.preload_act_table_set(LOG_EXP)
                elif name == "dt":
                    act.wait_ge(s_x1_done, floor(a_done))
                    for o in range(2):
                        act.wait_ge(s_M_dtr, floor(2 * m + o + 1))
                        a(ws[:, 0, o, :], ps[1 + o][:, :], ACT.Abs, bias=bdc[:, o:o + 1]).then_inc(s_M_sp, 1)
                    act.wait_ge(s_M_sp, floor(4 * m + 2))
                    a(ws[:, 0, :, :], ws[:, 0, :, :], ACT.Exp, scale=-1.0).then_inc(s_M_sp, 1)
                    act.wait_ge(s_M_sp, floor(4 * m + 3))
                    a(ws[:, 0, :, :], ws[:, 0, :, :], ACT.Ln, bias=1.0).then_inc(s_M_sp, 1)
                elif name == "state":
                    act.wait_ge(s_M_dtx, floor(3 * (m + 1)))
                    decay(m, 0)
                elif name == "unit" and s + 1 < NS:
                    decay(m, s + 1)

            def scan_norm(m, name):
                if name == "norm_mean":
                    act.wait_ge(s_E_yc, floor(m + 1))
                    act.wait_ge(s_sc, floor(NS * (m + 1)))
                    a(sqE, yM[:, :, :], ACT.Square).then_inc(s_E_sq, 1)
                elif name == "norm_var":
                    rstd(s_E_var, s_E_rs, m, rsM[:, :], 3)

            def run(i, has_a, has_m, has_2, has_p):
                for kind, name, n in ORDER:
                    if kind == "A" and has_a:
                        att(i, i - 1, name, n)
                    if kind == "E" and has_2:
                        scan_norm(i - 2, name)
                    if kind == "G" and has_2:
                        if name == "close":
                            act.wait_ge(s_out_t, floor((i - 2) + 1))
                            act.wait_ge(s_out_d, floor(16 * (i - 2)))
                            act.wait_ge(s_A_til, floor(4 * heads(i)))
                            a(outS, ps[7][:, :].rearrange("p (j d) -> p j d", j=JB), ACT.Copy).then_inc(s_out_c, 1)
                        else:
                            ffn(f2(i), name, n)
                    if kind == "F" and has_a:
                        ffn(f1(i), name, n)
                    if kind == "M" and has_m:
                        scan(i - 1, heads(i), name, n)
                    if kind == "P" and has_p:
                        pre(i + 1, name, n)

            act.wait_ge(s_setup, 1)
            for name, n in HEAD_ORDER:
                pre(0, name, n)
            passes(run, act)

        @block.vector
        def _(v):
            v.memset(zero16, 0.0).then_inc(s_consts, 1)
            v.memset(onesD[:, :], 1.0 / D).then_inc(s_consts, 1)
            v.memset(onesI[:, :], 1.0 / DI).then_inc(s_consts, 1)
            v.memset(eps[:, :], EPS).then_inc(s_consts, 1)
            v.memset(one[:, :], 1.0).then_inc(s_consts, 1)
            for e in range(NE):
                ins = v.memset(iota8[:, e:e + 1], float(e))
            ins.then_inc(s_consts, 1)
            v.memset(vpad[:, :, :], 0.0).then_inc(s_consts, 1)
            v.memset(c96[:, :, :, :], 0.0).then_inc(s_consts, 1)
            v.memset(xpad[:, :, 0:3], 0.0).then_inc(s_consts, 1)
            v.wait_ge(s_wload, 16 * N_WLOAD)
            src = rawqkv.rearrange("p (s c k r m e) -> p s r e k m c", s=3, c=NC, k=2, r=2, m=HD // 2)
            dst = wqk[:, :, :].rearrange("p u (r k m e c) -> p u r e k m c", r=2, k=2, m=HD // 2, e=2)
            bsrc = brow[:, :].rearrange("p (s c k r m e) -> p s r e k m c", s=3, c=NC, k=2, r=2, m=HD // 2)
            bdst = bperm[:, :, :].rearrange("p u (r k m e c) -> p u r e k m c", r=2, k=2, m=HD // 2, e=2)
            for u in range(4):
                for r in range(2):
                    for e in range(2):
                        f = e if u % 2 == 0 else 1 - e
                        v.tensor_copy(bdst[:, u, r, e], bsrc[:, u // 2, r, f])
                        ins = v.tensor_copy(dst[:, u, r, e], src[:, u // 2, r, f])
            v.tensor_copy(wv[:, :], rawqkv[:, 2 * D:3 * D])
            v.wait_ge(s_acol, 1)
            v.tensor_scalar(Acol[:, :], Acol[:, :], -1.0, None, ALU.mult).then_inc(s_acol, 1)
            v.wait_ge(s_setup_turned, 1)
            v.tensor_copy(WinT[:, :, :], ps[0][:, :].rearrange("p (e m) -> p e m", e=4))
            v.tensor_copy(WdtT[:, :, :], ps[1][:, :].rearrange("p (c o) -> p c o", c=2))
            v.tensor_copy(WoT[:, :, :], ps[2][:, 0:DI].rearrange("p (c d) -> p c d", c=2))
            for r in range(PARTS):
                v.tensor_copy(wxT[:, :, r * 2 * NS:(r + 1) * 2 * NS], ps[3][:, 0:4 * NS].rearrange("p (c s) -> p c s", c=2))
            v.tensor_copy(gateT[:, :], ps[4][:, 0:NE])
            v.tensor_copy(cols[:, :], ps[5][:, 0:NROW])
            v.tensor_copy(bqk[:, :], ps[6][:, 0:4]).then_inc(s_setup, 1)

            def pre(b, name, n):
                if name == "mean":
                    v.wait_ge(s_A_mean, floor(b + 1))
                    v.wait_ge(s_A_v, floor(b))
                    v.wait_ge(s_xA_done, floor(b + 1))
                    v.tensor_tensor(xnA[:, :], xA[:, :], ps[3][:, :], ALU.subtract).then_inc(s_A_xc, 1)
                elif name == "var":
                    v.wait_ge(s_A_rs, floor(2 * b + 2))
                    v.wait_ge(s_A_sq, floor(b + 1))
                    v.tensor_tensor(xnA[:, :], xnA[:, :], rsA, ALU.mult).then_inc(s_A_xn, 1)
                elif name == "qk":
                    v.wait_ge(s_A_qk, floor(4 * b + n + 1))
                    v.wait_ge(s_A_split, floor(16 * b - 16 + 4 * n + 4))
                    v.tensor_scalar(til[:, n, :], ps[3][:, :], bqk[:, n:n + 1], 0.0, ALU.add, ALU.max).then_inc(s_A_relu, 1)
                elif name == "til":
                    v.wait_ge(s_A_relu, floor(4 * b + n + 1))
                    v.wait_ge(s_A_exp, floor(4 * b + n + 1))
                    v.scalar_tensor_tensor(til[:, n, :], eA[:, n % 2, :], 1.0, til[:, n, :], ALU.min, ALU.add).then_inc(s_A_til, 1)
                elif name == "v":
                    v.wait_ge(s_A_v, floor(b + 1))
                    v.wait_ge(s_av, floor(STEPS * b))
                    v.tensor_tensor(vpad[:, :, :].rearrange("p g (k w) -> p g k w", w=40)[:, :, :, 0:HD],
                                    ps[3][:, :].rearrange("p (g k d) -> p g k d", g=JB * NC, k=NK),
                                    bvrow[:, :, :].rearrange("p j (c k d) -> p (j c) k d", c=NC, k=NK), ALU.add).then_inc(s_A_vp, 1)

            def att(b, name, s):
                if name == "unit":
                    step, c = divmod(s, NC)
                    if c == 0:
                        v.wait_ge(s_ex, floor(STEPS * b + step + 1))
                    v.wait_ge(s_num, floor(UNITS * b + s + 1))
                    v.tensor_tensor(rP[:, step % 2, c, :], ps[2][:, :], rP[:, step % 2, c, :], ALU.mult).then_inc(s_mul, 1)

            def att_close(b, f_before):
                v.wait_ge(s_oproj, floor(b + 1))
                v.wait_ge(s_yv, floor(f_before))
                v.scalar_tensor_tensor(xFin[:, :], ps[2][:, :], boc, xA[:, :], ALU.add, ALU.add).then_inc(s_x1_done, 1)

            def split_rows(src, pk, rest, base, chain):
                v.tensor_copy(pk[:, :], src).then_inc(chain, 1)
                v.wait_ge(chain, floor(base + 1))
                v.tensor_tensor(rest, src, pk[:, :], ALU.subtract).then_inc(chain, 1)
                v.wait_ge(chain, floor(base + 2))
                v.tensor_copy(mid[64:96, :], rest[64:96]).then_inc(chain, 1)
                v.tensor_copy(pk[32:64, :], rest[32:64]).then_inc(chain, 1)
                v.wait_ge(chain, floor(base + 4))
                v.tensor_tensor(pk[64:96, :], rest[64:96], mid[64:96, :], ALU.subtract).then_inc(chain, 1)

            def ffn(f, acc_free, name, q):
                if name == "mean":
                    v.wait_ge(s_F_mean, floor(f + 1))
                    v.wait_ge(s_up, floor(NCH * f))
                    v.tensor_tensor(xnF[:, :], xFin[:, :], ps[7][:, :], ALU.subtract).then_inc(s_F_xc, 1)
                elif name == "var":
                    v.wait_ge(s_F_rs, floor(2 * f + 2))
                    v.tensor_tensor(xnF[:, :], xnF[:, :], rsF[:, :], ALU.mult).then_inc(s_F_xn, 1)
                elif name == "router":
                    base = N_ROUTE * f
                    count = [0]

                    def step(ins, wait=True):
                        ins.then_inc(s_F_route, 1)
                        count[0] += 1
                        if wait:
                            v.wait_ge(s_F_route, floor(base + count[0]))

                    v.wait_ge(s_F_log, floor(f + 1))
                    step(v.tensor_copy(lg[:, :, :], ps[7][:, 0:JB * NE].rearrange("p (j e) -> p j e", j=JB)))
                    settled(v)
                    for j in range(JB):
                        step(v.max(mx8[:, j, :], lg[:, j, :]), j == JB - 1)
                    settled(v)
                    for j in range(JB):
                        step(v.max_index(ix8[:, j, :], mx8[:, j, :], lg[:, j, :]), False)
                    step(v.tensor_tensor(gp[:, 0, :], mx8[:, :, 1], mx8[:, :, 0], ALU.subtract), False)
                    assert count[0] == 10
                    v.wait_ge(s_F_route, floor(base + 9))
                    step(v.tensor_copy(ixf[:, :, :], ix8[:, :, 0:2]), False)
                    v.wait_ge(s_F_ed, floor(f + 1))
                    step(v.tensor_scalar(gp[:, 2, :], gp[:, 1, :], 1.0, None, ALU.add))
                    step(v.reciprocal(gp[:, 2, :], gp[:, 2, :]))
                    step(v.tensor_tensor(gp[:, 3, :], gp[:, 1, :], gp[:, 2, :], ALU.mult))
                    wide = [P, JB, NE]
                    for t in range(2):
                        step(v.tensor_tensor(oh[:, t, :, :], iota8[:, :].unsqueeze(1).broadcast_to(wide),
                                             ixf[:, :, t:t + 1].broadcast_to(wide), ALU.is_equal), t == 1)
                    for t in range(2):
                        step(v.tensor_tensor(oh[:, t, :, :], oh[:, t, :, :],
                                             gp[:, 2 + t, :].unsqueeze(2).broadcast_to(wide), ALU.mult), t == 1)
                    v.wait_ge(s_F_turn, floor(f))
                    for r in range(PARTS):
                        step(v.tensor_tensor(c96[:, :, r, 0:NE], oh[:, 0, :, :], oh[:, 1, :, :], ALU.add), False)
                    assert count[0] == N_ROUTE
                elif name == "turn":
                    v.wait_ge(s_F_turn, floor(f + 1))
                    v.wait_ge(s_cb, floor(NE * f))
                    v.wait_ge(s_F_var, floor(f + 1))
                    split_rows(ps[7][0:96, :], cpk, sqF[0:96, :], 5 * f, s_F_cpk)
                elif name == "spread":
                    v.wait_ge(s_cb, floor(NE * f + q))
                    v.tensor_copy(cBs[:, :], ps[7][:, :]).then_inc(s_cbs, 1)
                elif name == "down" and q % FC == FC - 1:
                    q //= FC
                    v.wait_ge(s_dn, floor(NCH * f + FC * (q + 1)))
                    if q == 0:
                        v.wait_ge(s_fadd, floor(NE * f))
                        v.wait_ge(s_out_t, floor(acc_free))
                        v.scalar_tensor_tensor(acc[:, :], ps[7][:, :], b2c[:, NE:NE + 1], xFin[:, :], ALU.add, ALU.add).then_inc(s_yv, 1)
                    else:
                        v.wait_ge(s_cbs, floor(NE * f + q))
                        v.wait_ge(s_fadd, floor(NE * f + q - 2))
                        v.scalar_tensor_tensor(tmp[:, q % 2, :], ps[7][:, :], b2c[:, q - 1:q], cBs[:, :], ALU.add, ALU.mult).then_inc(s_yv, 1)

            def scan(m, name, s):
                if name == "mean":
                    v.wait_ge(s_M_mean, floor(m + 1))
                    v.wait_ge(s_M_ip, floor(4 * m))
                    v.tensor_tensor(xnM[:, :], xM[:, :], ps[0][:, :], ALU.subtract).then_inc(s_M_xc, 1)
                elif name == "var":
                    v.wait_ge(s_M_rs, floor(2 * m + 2))
                    v.tensor_tensor(xnM[:, :], xnM[:, :], rsM[:, :], ALU.mult).then_inc(s_M_xn, 1)
                elif name == "inproj":
                    for h in range(2):
                        v.wait_ge(s_M_ip, floor(4 * m + 1 + h))
                        v.wait_ge(s_M_cv, floor(8 * m))
                        v.tensor_copy(xpad[:, h, 3:515], ps[h][:, :]).then_inc(s_M_xp, 1)
                elif name == "conv":
                    v.wait_ge(s_M_xp, floor(2 * m + 2))
                    for k in range(NCONV):
                        for h in range(2):
                            src = xpad[:, h, k:k + 512]
                            if k == 0:
                                v.tensor_scalar(xcs[:, h, :], src, convw[:, h, 0:1], cbc[:, h:h + 1], ALU.mult, ALU.add).then_inc(s_M_cv, 1)
                            else:
                                v.wait_ge(s_M_cv, floor(8 * m + 2 * (k - 1) + h + 1))
                                v.scalar_tensor_tensor(xcs[:, h, :], src, convw[:, h, k:k + 1], xcs[:, h, :], ALU.mult, ALU.add).then_inc(s_M_cv, 1)
                elif name == "dt":
                    for o in range(2):
                        v.wait_ge(s_M_dt, floor(2 * m + o + 1))
                        v.tensor_scalar(dte[:, o, :], ps[1 + o][:, :], bdc[:, o:o + 1], 0.0, ALU.add, ALU.max).then_inc(s_M_dtr, 1)
                    v.wait_ge(s_M_sp, floor(4 * m + 4))
                    v.wait_ge(s_M_dtr, floor(2 * m + 2))
                    v.tensor_tensor(dte[:, :, :], dte[:, :, :], ws[:, 0, :, :], ALU.add).then_inc(s_M_dtx, 1)
                    v.wait_ge(s_M_dtx, floor(3 * m + 1))
                    v.tensor_tensor(dtx[:, :, :], dte[:, :, :], xcs[:, :, :], ALU.mult).then_inc(s_M_dtx, 1)
                    v.wait_ge(s_M_dtx, floor(3 * m + 2))
                    v.memset(dte[:, :, 0:1], RESET).then_inc(s_M_dtx, 1)
                elif name == "state":
                    v.wait_ge(s_M_ss, floor(m + 1))
                    v.wait_ge(s_Cm, floor(NS * m))
                    v.wait_ge(s_M_var, floor(m + 1))
                    split_rows(ps[0][0:96, :], spk, sqM[0:96], 5 * m, s_M_spk)
                elif name == "unit":
                    both = [P, 2, 512]
                    w = ws[:, s % 3, :, :]
                    if s == 0:
                        dbx(m, 0)
                    v.wait_ge(s_da, floor(NS * m + s + 1))
                    v.wait_ge(s_dbx, floor(NS * m + s + 1))
                    v.tensor_tensor_scan(w.rearrange("p h t -> p (h t)"), dAs[:, s % 2, :, :].rearrange("p h t -> p (h t)"),
                                         w.rearrange("p h t -> p (h t)"), 0.0, ALU.mult, ALU.add).then_inc(s_sc, 1)
                    if s + 1 < NS:
                        dbx(m, s + 1)
                    v.wait_ge(s_Cm, floor(NS * m + s + 1))
                    v.wait_ge(s_sc, floor(NS * m + s + 1))
                    dst = yM[:, :, :] if s == 0 else w
                    v.tensor_tensor(dst, ps[1][:, :].unsqueeze(1).broadcast_to(both), w, ALU.mult).then_inc(s_hc, 1)

            def scan_norm(m, f_before, name):
                if name == "norm_mean":
                    both = [P, 2, 512]
                    v.wait_ge(s_E_mean, floor(m + 1))
                    v.tensor_tensor(yM[:, :, :], yM[:, :, :], ps[3][:, :].unsqueeze(1).broadcast_to(both), ALU.subtract).then_inc(s_E_yc, 1)
                elif name == "norm_var":
                    both = [P, 2, 512]
                    v.wait_ge(s_E_rs, floor(2 * m + 2))
                    base = N_EOP * m
                    v.tensor_tensor(yM[:, :, :], yM[:, :, :], rsM[:, :].unsqueeze(1).broadcast_to(both), ALU.mult).then_inc(s_E_op, 1)
                    v.wait_ge(s_E_op, floor(base + 1))
                    for h in range(2):
                        v.tensor_scalar(yM[:, h, :], yM[:, h, :], lgc[:, h:h + 1], lbc[:, h:h + 1], ALU.mult, ALU.add).then_inc(s_E_op, 1)
                    for h in range(2):
                        v.wait_ge(s_E_op, floor(base + 2 + h))
                        v.scalar_tensor_tensor(yM[:, h, :], xcs[:, h, :], dpc[:, h:h + 1], yM[:, h, :], ALU.mult, ALU.add).then_inc(s_E_op, 1)
                    v.wait_ge(s_E_op, floor(base + 5))
                    v.tensor_tensor(yM[:, :, :], yM[:, :, :], zs[:, :, :], ALU.mult).then_inc(s_E_op, 1)
                elif name == "gate":
                    v.wait_ge(s_E_proj, floor(m + 1))
                    v.wait_ge(s_yv, floor(f_before))
                    v.tensor_tensor(xFin[:, :], ps[3][:, :], xM[:, :], ALU.add).then_inc(s_x3_done, 1)

            def dbx(m, s):
                v.wait_ge(s_Bm, floor(NS * m + s + 1))
                if s >= 3:
                    v.wait_ge(s_ya, floor((NS - 1) * m + s - 3))
                v.tensor_tensor(ws[:, s % 3, :, :], ps[0][:, :].unsqueeze(1).broadcast_to([P, 2, 512]), dtx[:, :, :], ALU.mult).then_inc(s_dbx, 1)

            def run(i, has_a, has_m, has_2, has_p):
                for kind, name, n in ORDER:
                    if kind == "A" and has_a:
                        if name == "close":
                            att_close(i, (NE + 1) * f2(i) + 1 if has_2 else 0)
                        else:
                            att(i, name, n)
                    if kind == "E" and has_2:
                        scan_norm(i - 2, (NE + 1) * f1(i - 1) + 1 if has_m else 0, name)
                    if kind == "G" and has_2 and name != "close":
                        ffn(f2(i), outs_done(i - 1), name, n)
                    if kind == "F" and has_a:
                        ffn(f1(i), outs_done(i), name, n)
                    if kind == "M" and has_m:
                        scan(i - 1, name, n)
                    if kind == "P" and has_p:
                        pre(i + 1, name, n)

            for name, n in HEAD_ORDER:
                pre(0, name, n)
            passes(run, v)

        @block.gpsimd
        def _(pool):
            g = nc.gpsimd
            g.memset(ident[:, :], 0.0).then_inc(s_pconst, 1)
            g.memset(pick[:, :], 0.0).then_inc(s_pconst, 1)
            pool.wait_ge(s_pconst, 2)
            g.affine_select(out=ident[:, :], in_=ident[:, :], compare_op=ALU.not_equal, fill=1.0, base=0,
                            pattern=[[-1, P]], channel_multiplier=1).then_inc(s_pconst, 1)
            for r in range(PARTS):
                pool.wait_ge(s_pconst, floor(3 + r))
                g.affine_select(out=pick[:, :], in_=pick[:, :], compare_op=ALU.not_equal, fill=1.0, base=-32 * r,
                                pattern=[[-1, 32]], channel_multiplier=1).then_inc(s_pconst, 1)

            def cast(dst, src):
                return g.tensor_scalar(dst, src, 1.0, 1.0, ALU.mult, ALU.mult)

            def split(b, t, src):
                slot = t % 2
                base = 16 * b + 4 * t
                pool.wait_ge(s_pk[slot], floor(16 * PK_DMAS * (2 * b + t // 2)))
                settled(pool)
                cast(parts[:, slot, 0, :], src).then_inc(s_A_split, 1)
                pool.wait_ge(s_A_split, floor(base + 1))
                g.tensor_tensor(src, src, parts[:, slot, 0, :], ALU.subtract).then_inc(s_A_split, 1)
                pool.wait_ge(s_A_split, floor(base + 2))
                settled(pool)
                cast(parts[:, slot, 1, :], src).then_inc(s_A_split, 1)
                pool.wait_ge(s_A_split, floor(base + 3))
                g.tensor_tensor(parts[:, slot, 2, :], src, parts[:, slot, 1, :], ALU.subtract).then_inc(s_A_split, 1)

            def pre(b, name, n):
                if name == "rope":
                    pool.wait_ge(s_A_til, floor(4 * b + 2 * n + 2))
                    g.tensor_tensor(rot[:, :], til[:, 2 * n, :], ropeC[:, :], ALU.mult).then_inc(s_A_rope, 1)
                    g.tensor_tensor(til[:, 2 * n + 1, :], til[:, 2 * n + 1, :], ropeS[:, :], ALU.mult).then_inc(s_A_rope, 1)
                    pool.wait_ge(s_A_rope, floor(6 * b + 3 * n + 2))
                    g.tensor_tensor(til[:, 2 * n + 1, :], rot[:, :], til[:, 2 * n + 1, :], ALU.add).then_inc(s_A_rope, 1)
                elif name == "split":
                    pool.wait_ge(s_A_rope, floor(6 * b + 3 * (n // 2) + 3))
                    split(b, n, til[:, n, :])

            def ffn(f, dst, name, q):
                if name == "down":
                    e, c = divmod(q, FC)
                    q = e if c == FC - 1 else 0
                if (name == "down" and 1 <= q < NE) or name == "close":
                    pool.wait_ge(s_yv, floor((NE + 1) * f + q + 1))
                    pool.wait_ge(s_fadd, floor(NE * f + q - 1))
                    g.tensor_tensor(dst, acc[:, :], tmp[:, q % 2, :], ALU.add).then_inc(s_fadd, 1)

            def run(i, has_a, has_m, has_2, has_p):
                for kind, name, n in ORDER:
                    if kind == "G" and has_2:
                        ffn(f2(i), acc[:, :], name, NE if name == "close" else n)
                    if kind == "F" and has_a:
                        ffn(f1(i), acc[:, :], name, n)
                    if kind == "M" and has_m and name == "take":
                        pool.wait_ge(s_x3_done, floor(i - 1))
                        ffn(f1(i - 1), xM[:, :], "close", NE)
                    if kind == "M" and has_m and name == "unit" and n >= 1:
                        m = i - 1
                        pool.wait_ge(s_hc, floor(NS * m + n + 1))
                        pool.wait_ge(s_ya, floor((NS - 1) * m + n - 1))
                        g.tensor_tensor(yM[:, :, :], yM[:, :, :], ws[:, n % 3, :, :], ALU.add).then_inc(s_ya, 1)
                    if kind == "P" and has_p:
                        pre(i + 1, name, n)

            for name, n in HEAD_ORDER:
                pre(0, name, n)
            passes(run, pool)


_INS = ['L0_attn_a_x', 'L0_attn_a_w_qkv', 'L0_attn_a_b_qkv', 'L0_attn_a_w_out', 'L0_attn_a_b_out',
        'L0_attn_b_W_in', 'L0_attn_b_conv_w', 'L0_attn_b_conv_b', 'L0_attn_b_W_x', 'L0_attn_b_W_dt', 'L0_attn_b_b_dt',
        'L0_attn_b_A_log', 'L0_attn_b_D_param', 'L0_attn_b_W_out', 'L0_attn_b_ln_g', 'L0_attn_b_ln_b',
        'L0_ffn_gate_w', 'L0_ffn_W1', 'L0_ffn_b1', 'L0_ffn_W2', 'L0_ffn_b2',
        'L0_ffn_sW1', 'L0_ffn_sb1', 'L0_ffn_sW2', 'L0_ffn_sb2']


def rope_tables(n_tokens):
    half = HD // 2
    theta = (1.0 / np.float32(1250) ** (np.arange(half, dtype=np.float32) / np.float32(half))).astype(np.float32)
    angles = np.arange(n_tokens, dtype=np.float32)[:, None] * theta[None, :]
    dim = (np.arange(P) // NC) % HD
    sign = np.where(dim % 2 == 0, np.float32(-1), np.float32(1))
    cos = np.cos(angles).astype(np.float32).T[dim // 2]
    sin = sign[:, None] * np.sin(angles).astype(np.float32).T[dim // 2]
    return np.ascontiguousarray(cos), np.ascontiguousarray(sin.astype(np.float32))


def kernel(**inputs):
    import concourse.bacc as _bacc
    from concourse.bass_utils import run_bass_kernel_spmd as _run

    nc = _bacc.Bacc("TRN2", target_bir_lowering=False, num_devices=1)
    arrays, args = {}, []
    cos, sin = rope_tables(inputs[_INS[0]].shape[1])
    for name, a in [(n, inputs[n]) for n in _INS] + [("rope_cos", cos), ("rope_sin", sin)]:
        a = np.ascontiguousarray(a)
        arrays[f"in_{name}"] = a
        args.append(nc.dram_tensor(f"in_{name}", a.shape, mybir.dt.from_np(a.dtype), kind="ExternalInput").ap())
    out = nc.dram_tensor("out_0", inputs[_INS[0]].shape, F32, kind="ExternalOutput").ap()
    hybrid_layer_kernel(nc, *args, out)
    r = _run(nc, [arrays], core_ids=[0])
    return r.results[0]["out_0"]
```

```python
from contextlib import ExitStack

import numpy as np

import concourse.bass as bass
from concourse import mybir

F32 = mybir.dt.float32
BF16 = mybir.dt.bfloat16
U32 = mybir.dt.uint32
F32R = mybir.dt.float32r
ALU = mybir.AluOpType
ACT = mybir.ActivationFunctionType
LOG_EXP = "natural_log_exp_and_others"
GELU_SET = "gelu_and_others"
SILU_SET = "silu_and_others"

P = 128
D = 128
NH, HD = 16, 8
NE, FF = 8, 512
FC = FF // P
NCH = (NE + 1) * FC
DI = 256
NS = 16
NCONV = 4
EPS = 1e-5
JB = 4
NC = 4
NK = 4
STEPS = NK * JB
UNITS = STEPS * NC
PARTS = 3
QROWS = (0, 0, 1, 1, 0, 2)
KROWS = (0, 1, 0, 1, 2, 0)
PK_DMAS = 2 * len(QROWS)
RESET = 1e30
BURST_START = {"F": tuple(range(0, NCH + 1, FC)), "G": (0, *range(FC, NCH + 1, 2 * FC))}
HSLOTS = 8

MAIN_PASS = """
    E.norm_mean E.norm_var A.first A.unit*2 E.gate A.unit*2 G.mean A.unit A.av A.unit*2 G.var A.unit A.av A.unit
    G.router G.up A.unit G.up*2 G.burst A.unit G.up A.unit G.turn A.av A.unit G.up G.down A.unit G.up A.unit*2
    G.down A.unit A.av A.unit G.up A.unit*2 G.down A.unit A.av A.unit*3 A.av A.unit M.take A.unit G.burst G.down
    A.unit G.up G.spread G.up*4 G.down*2 A.unit G.down*2 A.unit A.av G.up A.unit G.spread G.up A.unit G.down
    A.unit G.down A.unit G.burst A.av G.up G.down*2 A.unit G.up G.spread G.up*4 G.down G.up A.unit G.down A.unit
    G.down*2 A.unit A.av A.unit G.up A.unit*2 G.spread A.av A.unit G.up A.unit G.down A.unit*2 A.av A.unit G.burst
    G.down*3 A.unit G.up G.spread G.up*4 G.down G.up A.unit G.down A.unit G.down*2 A.unit A.av A.unit G.up
    A.unit*2 G.up G.spread A.unit A.av A.unit G.down A.unit*2 G.burst G.down*2 A.unit G.down A.av G.up*3 G.spread
    G.up*2 G.down*2 A.unit G.down A.unit G.down A.unit A.av G.spread A.unit M.mean G.down A.unit G.down A.unit
    G.down*2 A.unit M.var A.av A.close G.close F.mean M.inproj M.conv F.var P.load M.silu P.mean F.router M.dt
    P.rope P.var F.burst F.up P.rest F.up*2 F.turn F.up*3 P.qk M.state F.down P.qk F.up P.rest P.til F.down P.til
    M.unit F.burst P.cast F.up F.down*2 F.up M.unit F.spread F.up*2 F.down P.cast F.down M.unit P.rest F.burst
    F.down P.cast F.up F.down F.up*2 F.spread M.unit P.qk F.down P.til F.down*2 M.unit F.down F.burst F.up*3
    F.spread P.qk M.unit F.up F.down*2 F.up M.unit F.down*2 F.up F.burst F.up F.spread P.cast P.rest P.rope F.up
    P.til M.unit F.up F.down*3 M.unit F.down F.burst F.up*3 F.spread M.unit P.rest F.up P.cast F.down*2 M.unit
    F.down F.burst F.down F.up*2 P.rest F.up F.spread F.up M.unit P.cast F.burst F.down*3 M.unit P.rest F.up
    F.down F.up P.cast F.up P.rest F.up F.spread M.unit F.down*2 M.unit P.cast F.down*2 F.up F.burst M.unit P.v
    F.spread F.down*4
"""
FIRST_PASS = """
    A.first A.unit*5 A.av A.unit P.rope A.unit*3 A.av A.unit*4 A.av A.unit*4 A.av A.unit*3 A.av A.unit*5 A.av
    A.unit*4 A.av A.unit*4 A.av A.unit*4 A.av A.unit*5 A.av A.unit*3 A.av P.rest A.unit*3 A.av A.unit*2 P.rest
    A.unit*3 A.av A.unit*3 A.av A.unit*6 A.av A.unit*2 A.av A.close P.load F.mean P.mean F.var P.var F.router F.up
    P.qk F.burst F.up F.turn P.qk F.up*3 F.burst F.down P.cast P.til F.down*2 P.rest F.up*2 P.til F.up F.down F.up
    F.spread P.qk P.cast F.up F.down F.up F.down*3 F.burst F.up*2 F.spread F.up F.burst F.down P.qk P.til F.up
    F.down F.up F.down*2 F.spread P.rope F.up P.rest P.til P.cast F.up F.down F.burst F.down*2 P.cast F.up*3
    F.down F.spread F.up F.down F.up F.down F.burst F.up P.rest F.up F.down*2 F.spread P.rest F.up*2 F.down F.up
    F.down*2 F.up F.down F.burst P.cast F.spread P.cast F.up F.burst F.up F.down*4 P.cast F.up F.spread F.down*2
    P.rest F.up F.down P.rest F.down F.up P.cast F.spread F.down F.up*2 F.down*2 F.burst P.v F.down
"""
LAST_PASS = """
    E.norm_mean E.norm_var E.gate G.mean G.var G.router G.up*3 G.turn G.up*2 G.burst M.take G.up G.down*2 G.burst
    G.down*2 G.up*2 G.spread G.up*2 G.down G.up M.mean G.down G.up G.down*2 G.up G.spread M.var G.up G.down*2
    M.inproj G.down*2 G.up*2 G.burst G.spread G.up*2 G.down*2 G.up G.down*2 G.up*2 G.spread G.up*2 G.down*3 M.conv
    G.down G.up*2 G.spread G.up G.burst G.up*2 M.silu G.down*4 G.up*2 G.spread G.up G.down*4 G.up*2 G.spread
    G.burst G.up G.down*4 G.up G.spread G.up M.dt G.down*4 G.close M.state M.unit*16
"""


def numbered(text):
    order, count = [], {}
    for word in text.split():
        part, _, times = word.partition("*")
        for _ in range(int(times or 1)):
            count[part] = count.get(part, -1) + 1
            stage, name = part.split(".")
            order.append((stage, name, count[part] + (name == "spread")))
    return order


ORDER, FIRST, LAST = numbered(MAIN_PASS), numbered(FIRST_PASS), numbered(LAST_PASS)
assert sum(part[:2] == ("A", "unit") for part in ORDER) == UNITS
HEAD_ORDER = [("load", 0), ("mean", 0), ("var", 0), ("qk", 0), ("til", 0), ("qk", 1), ("til", 1), ("rope", 0), ("cast", 0),
              ("rest", 0), ("qk", 2), ("cast", 1), ("rest", 1), ("til", 2), ("cast", 2), ("rest", 2), ("qk", 3), ("cast", 3),
              ("rest", 3), ("til", 3), ("v", 0), ("rope", 1), ("cast", 4), ("rest", 4), ("cast", 5), ("rest", 5), ("cast", 6),
              ("rest", 6), ("cast", 7), ("rest", 7)]


def hybrid_layer_kernel(nc: bass.Bass, x, w_qkv, b_qkv, w_out, b_out, W_in, conv_w, conv_b, W_x, W_dt, b_dt, A_log,
                        D_param, W_out, ln_g, ln_b, gate_w, W1, b1, W2, b2, sW1, sb1, sW2, sb2,
                        rope_cos, rope_sin, out):
    NB, T, _ = x.shape
    assert T == JB * P and T == 512

    ctx = ExitStack()
    with ctx:
        def sb(name, shape, dt=F32):
            return ctx.enter_context(nc.sbuf_tensor(name, shape, dt))

        def sem(name):
            return ctx.enter_context(nc.semaphore(name))

        ps = [ctx.enter_context(nc.psum_tensor(f"bank{i}", [P, 512], F32)) for i in range(8)]

        qscr = nc.dram_tensor("qscr", (2, 2, P, NC * 512), BF16, kind="Internal").ap()
        kscr = nc.dram_tensor("kscr", (2, 2, 2, P, NC * 512), BF16, kind="Internal").ap()

        W1H = sb("W1H", [P, NE + 1, FF], F32R)
        W1L = sb("W1L", [P, NE + 1, FF], F32R)
        W2s = sb("W2s", [P, NE + 1, FC, D])
        wqk = sb("wqk", [P, 4, P])
        wv = sb("wv", [P, D])
        wos = sb("wos", [P, D])
        WinT = sb("WinT", [P, 4, P])
        WdtT = sb("WdtT", [P, 2, DI])
        WoT = sb("WoT", [P, 2, D])
        wxT = sb("wxT", [P, 2, PARTS * 2 * NS])
        gateT = sb("gateT", [P, NE])
        ropeC = sb("ropeC", [P, 512])
        ropeS = sb("ropeS", [P, 512])
        ident = sb("ident", [P, P])
        onesD = sb("onesD", [P, P])
        onesI = sb("onesI", [P, P])
        pick = sb("pick", [96, 32], BF16)
        bvrow = sb("bvrow", [P, JB, D])
        iota8 = sb("iota8", [P, NE])
        eps = sb("eps", [P, 1])
        one = sb("one", [P, 1])
        R0, R1, R2, R3, R4, R5, R6, R7, R8, R9 = 0, 32, 36, 44, 45, 46, 48, 50, 52, 54
        NROW = 56
        rows = sb("rows", [NROW, P])
        cols = sb("cols", [P, NROW])
        convw = sb("convw", [P, 2, NCONV])
        alog = sb("alog", [P, NS])
        Acol = sb("Acol", [P, NS])
        brow = sb("brow", [1, 3 * D])
        bperm = sb("bperm", [1, 4, P])
        bqk = sb("bqk", [P, 4])
        b1c = cols[:, R0:R2]
        b2c = cols[:, R2:R4]
        boc = cols[:, R4:R5]
        cbc = cols[:, R5:R6]
        bdc = cols[:, R6:R7]
        dpc = cols[:, R7:R8]
        lgc = cols[:, R8:R9]
        lbc = cols[:, R9:NROW]

        xA = sb("xA", [P, 512])
        xFin = sb("xFin", [P, 512])
        xM = sb("xM", [P, 512])
        acc = sb("acc", [P, 512])

        xnA = sb("xnA", [P, 512])
        eA = sb("eA", [P, 2, 512])
        sqA = eA[:, 0, :]
        rsA = eA[:, 1, :]
        outS = eA[:, 0, :].rearrange("p (j d) -> p j d", j=JB)
        xin = eA[:, 1, :].rearrange("p (j d) -> p j d", j=JB)
        qpk = sb("qpk", [P, 2, 2, NC * 512], BF16)
        shared = sb("shared", [P, 8, 512])
        kpk = shared[:, :, :].rearrange("p (s u a) t -> p s u (a t)", s=2, u=2).bitcast(BF16)
        til = shared[:, 0:4, :]
        rot = shared[:, 4, :]
        parts = shared[:, 5:8, :].rearrange("p a t -> p (a t)").bitcast(BF16).rearrange("p (u a t) -> p u a t", u=2, a=PARTS)
        vpad = sb("vpad", [P, JB * NC, 160])

        region = sb("region", [P, 10, 512])
        rP = region[:, 0:8, :].rearrange("p (s c) t -> p s c t", s=2)
        oT = region[:, 8, :]
        ws = region[:, 0:6, :].rearrange("p (s h) t -> p s h t", s=3)
        dAs = region[:, 6:10, :].rearrange("p (s h) t -> p s h t", s=2)
        sqE = region[:, 8:10, :]

        xnF = sb("xnF", [P, 512])
        xnH = sb("xnH", [P, 512], F32R)
        xnL = sb("xnL", [P, 512], F32R)
        sqF = sb("sqF", [P, 512])
        hF = sb("hF", [P, HSLOTS, 512])
        cpk = sb("cpk", [96, 512], BF16)
        mid = sb("mid", [96, 512], BF16)
        cBs = sb("cBs", [P, 512])
        tmp = sb("tmp", [P, 2, 512])
        rsF = tmp[:, 1, :]
        lg = sb("lg", [P, JB, NE])
        mx8 = sb("mx8", [P, JB, NE])
        ix8 = sb("ix8", [P, JB, NE], U32)
        ixf = sb("ixf", [P, JB, 2])
        gp = sb("gp", [P, 4, JB])
        oh = sb("oh", [P, 2, JB, NE])
        c96 = sb("c96", [P, JB, PARTS, 32])

        xnM = sb("xnM", [P, 512])
        sqM = region[:, 9, :]
        rsM = sb("rsM", [P, 512])
        xpad = sb("xpad", [P, 2, 3 + 512])
        xcs = sb("xcs", [P, 2, 512])
        zs = sb("zs", [P, 2, 512])
        steps = qpk[:, 1, :, :].rearrange("p u n -> p (u n)").bitcast(F32).rearrange("p (w h t) -> p w h t", w=2, h=2)
        dte = steps[:, 0]
        dtx = steps[:, 1]
        yM = sb("yM", [P, 2, 512])
        spk = sb("spk", [96, 512], BF16)

        rawin = region[:, 0, :].rearrange("p (e d) -> p e d", e=4)
        rawdt = region[:, 1, :].rearrange("p (o i) -> p o i", o=2)
        rawout = region[:, 2, 0:DI]
        rawx = region[0:2 * NS, 3, 0:DI]
        rawg = region[0:NE, 4, 0:P]
        rawqkv = region[:, 5, 0:3 * D]
        rawW1 = region[:, 0:NE + 1, :]
        zero16 = region[:, 6:8, :].rearrange("p a t -> p (a t)").bitcast(BF16)

        s_gate = sem("gate")
        s_wload = sem("wload")
        s_wbig = sem("wbig")
        s_consts = sem("consts")
        s_pconst = sem("pconst")
        s_setup_turned = sem("setup_turned")
        s_setup = sem("setup")
        s_zeroed = sem("zeroed")
        s_acol = sem("acol")
        s_x_in = sem("x_in")
        s_x_turned = sem("x_turned")
        s_xA_done = sem("xA_done")
        s_A_mean = sem("A_mean")
        s_A_xc = sem("A_xc")
        s_A_sq = sem("A_sq")
        s_A_var = sem("A_var")
        s_A_rs = sem("A_rs")
        s_A_xn = sem("A_xn")
        s_A_qk = sem("A_qk")
        s_A_exp = sem("A_exp")
        s_A_relu = sem("A_relu")
        s_A_til = sem("A_til")
        s_A_rope = sem("A_rope")
        s_A_split = sem("A_split")
        s_pk = [sem("pk0"), sem("pk1")]
        s_A_v = sem("A_v")
        s_A_vp = sem("A_vp")
        s_q_ld = [sem("q_ld0"), sem("q_ld1")]
        s_k_ld = [sem("k_ld0"), sem("k_ld1")]
        s_den = sem("den")
        s_ln = sem("ln")
        s_ex = sem("ex")
        s_num = sem("num")
        s_mul = sem("mul")
        s_av = sem("av")
        s_o_copied = sem("o_copied")
        s_oproj = sem("oproj")
        s_x1_done = sem("x1_done")
        s_F_mean = sem("F_mean")
        s_F_xc = sem("F_xc")
        s_F_sq = sem("F_sq")
        s_F_var = sem("F_var")
        s_F_rs = sem("F_rs")
        s_F_xn = sem("F_xn")
        s_F_low = sem("F_low")
        s_W1_low = sem("W1_low")
        s_F_log = sem("F_log")
        s_F_route = sem("F_route")
        s_F_ed = sem("F_ed")
        s_F_turn = sem("F_turn")
        s_F_cpk = sem("F_cpk")
        s_up = sem("up")
        s_ge = sem("ge")
        s_dn = sem("dn")
        s_cb = sem("cb")
        s_cbs = sem("cbs")
        s_yv = sem("yv")
        s_fadd = sem("fadd")
        s_out_t = sem("out_t")
        s_out_c = sem("out_c")
        s_out_d = sem("out_d")
        s_M_mean = sem("M_mean")
        s_M_xc = sem("M_xc")
        s_M_sq = sem("M_sq")
        s_M_var = sem("M_var")
        s_M_rs = sem("M_rs")
        s_M_xn = sem("M_xn")
        s_M_ip = sem("M_ip")
        s_M_xp = sem("M_xp")
        s_M_cv = sem("M_cv")
        s_M_si = sem("M_si")
        s_M_dt = sem("M_dt")
        s_M_sp = sem("M_sp")
        s_M_dtr = sem("M_dtr")
        s_M_dtx = sem("M_dtx")
        s_M_ss = sem("M_ss")
        s_M_spk = sem("M_spk")
        s_Bm = sem("Bm")
        s_Cm = sem("Cm")
        s_da = sem("da")
        s_dbx = sem("dbx")
        s_sc = sem("sc")
        s_hc = sem("hc")
        s_ya = sem("ya")
        s_E_mean = sem("E_mean")
        s_E_yc = sem("E_yc")
        s_E_sq = sem("E_sq")
        s_E_var = sem("E_var")
        s_E_rs = sem("E_rs")
        s_E_op = sem("E_op")
        s_E_proj = sem("E_proj")
        s_x3_done = sem("x3_done")

        def floor(v):
            return max(v, 0) if isinstance(v, int) else v

        def settled(eng):
            eng.sem_inc(s_gate, 1)

        N_WLOAD = 26
        N_WBIG = 2 * (NE + 1)
        N_CONST, N_PCONST = 9, 3 + PARTS
        N_ROUTE, N_EOP = 21, 6

        def outs_done(i):
            return max(i - 1, 0) if isinstance(i, int) else i - 1

        def f1(i):
            return i if isinstance(i, int) and i < 2 else 2 * i - 1

        def f2(i):
            return 2 * NB - 1 if isinstance(i, int) and i == NB + 1 else 2 * i - 2

        def heads(i):
            return min(i + 1, NB) if isinstance(i, int) else i + 1

        def passes(run, e):
            run(FIRST, 0, True, False, False, True)
            run(ORDER, 1, True, True, False, True)
            run(ORDER, 2, True, True, True, True)
            with e.Fori(3, NB - 1) as i:
                run(ORDER, i, True, True, True, True)
            run(ORDER, NB - 1, True, True, True, False)
            run(LAST, NB, False, True, True, False)
            run(LAST, NB + 1, False, False, True, False)

        block = ctx.enter_context(nc.Block())

        @block.sync
        def _(sp):
            def load_x(b):
                sp.wait_ge(s_x_turned, floor(b))
                settled(sp)
                sp.wait_ge(s_A_til, floor(4 * b))
                settled(sp)
                sp.dma_start(xin, x[b].rearrange("(j p) d -> p j d", p=P)).then_inc(s_x_in, 16)

            def wl(dst, src):
                sp.dma_start(dst, src).then_inc(s_wload, 16)

            load_x(0)
            wl(rawqkv, w_qkv)
            wl(brow[:, :], b_qkv.rearrange("(a n) -> a n", a=1))
            wl(rawin, W_in.rearrange("(e p) d -> p e d", p=P))
            wl(rawdt, W_dt.rearrange("(o p) i -> p o i", p=P))
            wl(rawout, W_out)
            wl(rawx, W_x)
            wl(rawg, gate_w)
            wl(wos[:, :], w_out)
            wl(ropeC[:, :], rope_cos)
            wl(ropeS[:, :], rope_sin)
            wl(rows[R0:R1, :], b1.rearrange("e (c f) -> (e c) f", f=P))
            wl(rows[R1:R2, :], sb1.rearrange("(c f) -> c f", f=P))
            wl(rows[R2:R3, :], b2)
            wl(rows[R3:R4, :], sb2.rearrange("(a n) -> a n", a=1))
            wl(rows[R4:R5, :], b_out.rearrange("(a n) -> a n", a=1))
            wl(rows[R5:R6, :], conv_b.rearrange("(h n) -> h n", n=P))
            wl(rows[R6:R7, :], b_dt.rearrange("(h n) -> h n", n=P))
            wl(rows[R7:R8, :], D_param.rearrange("(h n) -> h n", n=P))
            wl(rows[R8:R9, :], ln_g.rearrange("(h n) -> h n", n=P))
            wl(rows[R9:NROW, :], ln_b.rearrange("(h n) -> h n", n=P))
            wl(convw[:, :, :], conv_w.rearrange("(h p) a k -> p h (a k)", p=P))
            wl(alog[:, :], A_log.rearrange("(a n) -> a n", a=1).broadcast_to([P, NS]))
            bv = b_qkv[2 * D:3 * D].rearrange("(a n) -> a n", a=1).broadcast_to([P, D])
            for j in range(JB):
                wl(bvrow[:, j, :], bv)
            sp.wait_ge(s_consts, 1)
            for k2 in range(2):
                for u in range(2):
                    sp.dma_start(qscr[k2, u], zero16).then_inc(s_zeroed, 16)
                    for par in range(2):
                        sp.dma_start(kscr[k2, par, u], zero16).then_inc(s_zeroed, 16)
            sp.wait_ge(s_zeroed, 16 * 12)

            def pre(b, name, t):
                if name == "rest" and t % 2 == 1:
                    t //= 2
                    n, u = divmod(t, 2)
                    sp.wait_ge(s_A_split, floor(16 * b + 4 * (t + 1)))
                    settled(sp)
                    if t == 0:
                        sp.wait_ge(s_q_ld[0], floor(16 * b))
                        sp.wait_ge(s_q_ld[1], floor(16 * b))
                    if t == 2:
                        sp.wait_ge(s_k_ld[0], floor(32 * b))
                        sp.wait_ge(s_k_ld[1], floor(32 * b))
                    rowmap = QROWS if n == 0 else KROWS
                    for par in range(2):
                        for r, part in enumerate(rowmap):
                            row = 64 * par + 8 * r
                            src = parts[64 * par:64 * par + 64, u, part, :]
                            if n == 0:
                                dst = qscr[:, u, row:row + 8, :]
                            else:
                                dst = kscr[:, par, u, row:row + 8, :]
                            dst = dst.rearrange("k d (c t) -> k (d c) t", c=NC)
                            sp.dma_start(dst, src).then_inc(s_pk[u], 16)

            def load_k(b, k):
                sp.wait_ge(s_num, floor(UNITS * b + JB * NC * (k - 1)))
                sp.dma_start(kpk[:, k % 2, :, :], kscr[k // 2, k % 2].rearrange("u p n -> p u n")).then_inc(
                    s_k_ld[k % 2], 16)

            def run(order, i, has_a, has_m, has_2, has_p):
                if has_a:
                    sp.wait_ge(s_pk[0], floor(32 * PK_DMAS * (i + 1)))
                    sp.wait_ge(s_pk[1], floor(32 * PK_DMAS * (i + 1)))
                    load_k(i, 0)
                    sp.wait_ge(s_num, floor(UNITS * i))
                    sp.dma_start(qpk[:, 0, :, :], qscr[0].rearrange("u p n -> p u n")).then_inc(s_q_ld[0], 16)
                    load_k(i, 1)
                if has_p:
                    load_x(i + 1)
                if has_a:
                    sp.wait_ge(s_da, floor(NS * (i - 1)))
                    sp.wait_ge(s_dbx, floor(NS * (i - 1)))
                    sp.dma_start(qpk[:, 1, :, :], qscr[1].rearrange("u p n -> p u n")).then_inc(s_q_ld[1], 16)
                    for k in range(2, NK):
                        load_k(i, k)
                if has_2:
                    sp.wait_ge(s_out_c, floor((i - 2) + 1))
                    settled(sp)
                    sp.dma_start(out[i - 2].rearrange("(j p) d -> p j d", p=P), outS).then_inc(s_out_d, 16)
                if has_p:
                    for kind, name, n in order:
                        if kind == "P":
                            pre(i + 1, name, n)

            for name, n in HEAD_ORDER:
                pre(0, name, n)
            passes(run, sp)
            sp.wait_ge(s_out_d, 16 * NB)

        @block.tensor
        def _(pe):
            def turn_in():
                pe.wait_ge(s_wload, 16 * N_WLOAD)
                pe.wait_ge(s_consts, N_CONST)
                pe.wait_ge(s_pconst, N_PCONST)
                for e in range(4):
                    pe.transpose(ps[0][:, e * P:e * P + P], rawin[:, e, :], ident[:, :])
                for o in range(2):
                    for c in range(2):
                        pe.transpose(ps[1][:, (c * 2 + o) * P:(c * 2 + o) * P + P], rawdt[:, o, c * P:c * P + P], ident[:, :])
                for c in range(2):
                    pe.transpose(ps[2][:, c * P:c * P + P], rawout[:, c * P:c * P + P], ident[:, :])
                    pe.transpose(ps[3][:, c * 2 * NS:(c + 1) * 2 * NS], rawx[:, c * P:c * P + P], ident[0:2 * NS, 0:2 * NS])
                pe.transpose(ps[4][:, 0:NE], rawg, ident[0:NE, 0:NE])
                pe.transpose(ps[5][:, 0:NROW], rows[:, :], ident[0:NROW, 0:NROW])
                pe.wait_ge(s_acol, 2)
                for t in range(4):
                    mm = pe.matmul(ps[6][:, t:t + 1], bperm[:, t, :], one[0:1, :], start=True, stop=True)
                mm.then_inc(s_setup_turned, 1)

            def ones_mm(bank, ones, src, n=1):
                for h in range(n):
                    mm = pe.matmul(ps[bank][:, :], ones[:, :], src[h], start=(h == 0), stop=(h == n - 1))
                return mm

            def pre(b, name, n):
                if name == "load":
                    pe.wait_ge(s_x_in, floor(16 * (b + 1)))
                    pe.wait_ge(s_o_copied, floor(b))
                    for j in range(JB):
                        mm = pe.transpose(ps[3][:, j * P:j * P + P], xin[:, j, :], ident[:, :])
                    mm.then_inc(s_x_turned, 1)
                elif name == "mean":
                    pe.wait_ge(s_xA_done, floor(b + 1))
                    ones_mm(3, onesD, [xA[:, :]]).then_inc(s_A_mean, 1)
                elif name == "var":
                    pe.wait_ge(s_A_sq, floor(b + 1))
                    ones_mm(3, onesD, [sqA]).then_inc(s_A_var, 1)
                elif name == "qk":
                    pe.wait_ge(s_A_xn, floor(b + 1))
                    pe.wait_ge(s_A_exp, floor(4 * b + n))
                    pe.wait_ge(s_A_relu, floor(4 * b + n))
                    pe.matmul(ps[3][:, :], wqk[:, n, :], xnA[:, :], start=True, stop=True).then_inc(s_A_qk, 1)
                elif name == "v":
                    pe.wait_ge(s_A_exp, floor(4 * b + 4))
                    pe.wait_ge(s_A_relu, floor(4 * b + 4))
                    for j in range(JB):
                        mm = pe.matmul(ps[3][:, j * D:j * D + D], xnA[:, j * P:j * P + P], wv[:, :], start=True, stop=True)
                    mm.then_inc(s_A_v, 1)

            def score(b, s, c, u):
                k, jb = divmod(s, JB)
                n = NC * s + c
                if jb == 0 and c == 0:
                    pe.wait_ge(s_k_ld[k % 2], floor(32 * b + 16 * (k // 2) + 16))
                if n in (0, UNITS // 2):
                    pe.wait_ge(s_q_ld[n // (UNITS // 2)], floor(16 * b + 16))
                lhs = kpk[:, k % 2, u, c * 512 + jb * P:c * 512 + jb * P + P]
                rhs = qpk[:, k // 2, u, c * 512:(c + 1) * 512]
                if u == 0:
                    pe.wait_ge(s_ln, floor(UNITS * b + n - 1))
                    pe.matmul(ps[n % 2][:, :], lhs, rhs, start=True, stop=True).then_inc(s_den, 1)
                else:
                    pe.wait_ge(s_mul, floor(UNITS * b + n))
                    pe.matmul(ps[2][:, :], lhs, rhs, start=True, stop=True).then_inc(s_num, 1)

            def att(b, m_done, name, s):
                if name == "first":
                    pe.wait_ge(s_dbx, floor(NS * m_done))
                    pe.wait_ge(s_hc, floor(NS * m_done))
                    for c in range(NC):
                        score(b, 0, c, 0)
                elif name == "unit":
                    step, c = divmod(s, NC)
                    if step + 1 < STEPS:
                        score(b, step + 1, c, 0)
                    score(b, step, c, 1)
                elif name == "av":
                    k, jb = divmod(s, JB)
                    if s == 0:
                        pe.wait_ge(s_A_vp, floor(b + 1))
                        pe.wait_ge(s_x3_done, floor(m_done))
                    for c in range(NC):
                        pe.wait_ge(s_mul, floor(UNITS * b + NC * s + c + 1))
                        mm = pe.matmul(ps[3][32 * c:32 * c + 32, :], vpad[:, jb * NC + c, 32 * k:32 * k + 32],
                                       rP[:, s % 2, c, :], start=(s == 0), stop=(s == STEPS - 1))
                    mm.then_inc(s_av, 1)
                elif name == "close":
                    pe.wait_ge(s_o_copied, floor(b + 1))
                    pe.wait_ge(s_mul, floor(UNITS * (b + 1)))
                    pe.matmul(ps[2][:, :], wos[:, :], oT, start=True, stop=True).then_inc(s_oproj, 1)

            def ffn(f, ready, last_ready, fin, name, q):
                if name == "mean":
                    pe.wait_ge(ready, floor(last_ready))
                    pe.wait_ge(s_yv, floor((NE + 1) * f))
                    pe.wait_ge(s_out_c, floor(fin))
                    ones_mm(7, onesD, [xFin[:, :]]).then_inc(s_F_mean, 1)
                elif name == "var":
                    pe.wait_ge(s_F_sq, floor(f + 1))
                    ones_mm(7, onesD, [sqF[:, :]]).then_inc(s_F_var, 1)
                elif name == "router":
                    pe.wait_ge(s_F_xn, floor(f + 1))
                    for j in range(JB):
                        mm = pe.matmul(ps[7][:, j * NE:j * NE + NE], xnF[:, j * P:j * P + P], gateT[:, :], start=True, stop=True)
                    mm.then_inc(s_F_log, 1)
                elif name == "turn":
                    pe.wait_ge(s_F_route, floor(N_ROUTE * (f + 1)))
                    for j in range(JB):
                        mm = pe.transpose(ps[7][0:96, j * P:j * P + P], c96[:, j, :, :].rearrange("p a b -> p (a b)"), ident[:, :])
                    mm.then_inc(s_F_turn, 1)
                elif name == "up":
                    if q == 0:
                        pe.wait_ge(s_F_low, floor(2 * f + 2))
                    pe.wait_ge(s_ge, floor(NCH * f + q - 2))
                    w = NE if q < FC else q // FC - 1
                    part = slice(q % FC * P, q % FC * P + P)
                    high, low = W1H[:, w, part], W1L[:, w, part]
                    bank = ps[4 + q % 3][:, :]
                    pe.matmul(bank, low, xnH[:, :], start=True, stop=False)
                    pe.matmul(bank, high, xnL[:, :], start=False, stop=False)
                    pe.matmul(bank, high, xnH[:, :], start=False, stop=True).then_inc(s_up, 1)
                elif name == "spread":
                    pe.wait_ge(s_yv, floor((NE + 1) * f + q))
                    pe.wait_ge(s_F_cpk, floor(5 * (f + 1)))
                    pe.matmul(ps[7][:, :], pick[:, q - 1:q].broadcast_to([96, P]), cpk[:, :], start=True, stop=True).then_inc(s_cb, 1)
                elif name == "down":
                    e, c = divmod(q, FC)
                    if c == 0 and e == 0:
                        pe.wait_ge(s_F_cpk, floor(5 * f + 2))
                    elif c == 0:
                        pe.wait_ge(s_cbs, floor(NE * f + e))
                    pe.wait_ge(s_ge, floor(NCH * f + q + 1))
                    pe.matmul(ps[7][:, :], W2s[:, NE if e == 0 else e - 1, c, :], hF[:, q % HSLOTS, :], start=(c == 0), stop=(c == FC - 1)).then_inc(s_dn, 1)

            def spread_b(m, s):
                pe.wait_ge(s_dbx, floor(NS * m + s))
                pe.matmul(ps[0][:, :], pick[:, s:s + 1].broadcast_to([96, P]), spk[:, :], start=True, stop=True).then_inc(s_Bm, 1)

            def scan(m, a_done, name, s):
                if name == "mean":
                    pe.wait_ge(s_fadd, floor(NE * (f1(m) + 1)))
                    pe.wait_ge(s_ln, floor(UNITS * a_done))
                    ones_mm(0, onesD, [xM[:, :]]).then_inc(s_M_mean, 1)
                elif name == "var":
                    pe.wait_ge(s_M_sq, floor(m + 1))
                    ones_mm(1, onesD, [sqM]).then_inc(s_M_var, 1)
                elif name == "inproj":
                    pe.wait_ge(s_M_xn, floor(m + 1))
                    pe.wait_ge(s_x1_done, floor(a_done))
                    for e, bank in enumerate((0, 1, 2)):
                        pe.matmul(ps[bank][:, :], WinT[:, e, :], xnM[:, :], start=True, stop=True).then_inc(s_M_ip, 1)
                    pe.wait_ge(s_M_xp, floor(2 * m + 1))
                    pe.matmul(ps[0][:, :], WinT[:, 3, :], xnM[:, :], start=True, stop=True).then_inc(s_M_ip, 1)
                elif name == "dt":
                    pe.wait_ge(s_M_si, floor(4 * m + 4))
                    pe.wait_ge(s_M_xp, floor(2 * m + 2))
                    for o in range(2):
                        for c in range(2):
                            mm = pe.matmul(ps[1 + o][:, :], WdtT[:, c, o * P:o * P + P], xcs[:, c, :], start=(c == 0), stop=(c == 1))
                        mm.then_inc(s_M_dt, 1)
                    for c in range(2):
                        mm = pe.matmul(ps[0][0:96, :], wxT[:, c, :], xcs[:, c, :], start=(c == 0), stop=(c == 1))
                    mm.then_inc(s_M_ss, 1)
                elif name == "unit":
                    if s == 0:
                        pe.wait_ge(s_M_spk, floor(5 * (m + 1)))
                        pe.wait_ge(s_M_dtr, floor(2 * m + 2))
                        pe.wait_ge(s_M_sp, floor(4 * m + 2))
                        spread_b(m, 0)
                    pe.wait_ge(s_hc, floor(NS * m + s))
                    pe.matmul(ps[1][:, :], pick[:, NS + s:NS + s + 1].broadcast_to([96, P]), spk[:, :], start=True, stop=True).then_inc(s_Cm, 1)
                    if s + 1 < NS:
                        spread_b(m, s + 1)

            def scan_norm(m, v_done, name):
                if name == "norm_mean":
                    pe.wait_ge(s_ya, floor((NS - 1) * (m + 1)))
                    pe.wait_ge(s_A_vp, floor(v_done))
                    ones_mm(3, onesI, [yM[:, 0, :], yM[:, 1, :]], 2).then_inc(s_E_mean, 1)
                elif name == "norm_var":
                    pe.wait_ge(s_E_sq, floor(m + 1))
                    ones_mm(3, onesI, [sqE[:, 0, :], sqE[:, 1, :]], 2).then_inc(s_E_var, 1)
                elif name == "gate":
                    pe.wait_ge(s_E_op, floor(N_EOP * (m + 1)))
                    for h in range(2):
                        mm = pe.matmul(ps[3][:, :], WoT[:, h, :], yM[:, h, :], start=(h == 0), stop=(h == 1))
                    mm.then_inc(s_E_proj, 1)

            def run(order, i, has_a, has_m, has_2, has_p):
                for kind, name, n in order:
                    if kind == "A" and has_a:
                        att(i, i - 1, name, n)
                    if kind == "E" and has_2:
                        scan_norm(i - 2, heads(i), name)
                    if kind == "G" and has_2:
                        if name == "close":
                            pe.wait_ge(s_fadd, floor(NE * (f2(i) + 1)))
                            pe.wait_ge(s_yv, floor((NE + 1) * (f2(i) + 1)))
                            for j in range(JB):
                                mm = pe.transpose(ps[7][:, j * P:j * P + P], acc[:, j * P:j * P + P], ident[:, :])
                            mm.then_inc(s_out_t, 1)
                        else:
                            ffn(f2(i), s_x3_done, i - 1, i - 2, name, n)
                    if kind == "F" and has_a:
                        ffn(f1(i), s_x1_done, i + 1, outs_done(i), name, n)
                    if kind == "M" and has_m:
                        scan(i - 1, heads(i), name, n)
                    if kind == "P" and has_p:
                        pre(i + 1, name, n)

            turn_in()
            pe.wait_ge(s_setup, 1)
            for name, n in HEAD_ORDER:
                pre(0, name, n)
            pe.wait_ge(s_wbig, 16 * N_WBIG)
            pe.wait_ge(s_W1_low, 2)
            passes(run, pe)

        @block.scalar
        def _(act):
            def a(out_, in_, fn, **kw):
                return nc.scalar.activation(out_, in_, fn, **kw)

            act.preload_act_table_set(LOG_EXP)
            act.wait_ge(s_wload, 16 * N_WLOAD)
            a(Acol[:, :], alog[:, :], ACT.Exp).then_inc(s_acol, 1)
            def rstd(s_var, s_rs, b, dst, bank):
                act.wait_ge(s_var, floor(b + 1))
                a(dst, ps[bank][:, :], ACT.Ln, bias=eps[:, :]).then_inc(s_rs, 1)
                act.wait_ge(s_rs, floor(2 * b + 1))
                a(dst, dst, ACT.Exp, scale=-0.5).then_inc(s_rs, 1)

            def pre(b, name, n):
                if name == "load":
                    act.wait_ge(s_x_turned, floor(b + 1))
                    act.wait_ge(s_x1_done, floor(b))
                    a(xA[:, :], ps[3][:, :], ACT.Copy).then_inc(s_xA_done, 1)
                elif name == "mean":
                    act.wait_ge(s_A_xc, floor(b + 1))
                    act.wait_ge(s_out_d, floor(16 * (b - 2)))
                    a(sqA, xnA[:, :], ACT.Square).then_inc(s_A_sq, 1)
                elif name == "var":
                    rstd(s_A_var, s_A_rs, b, rsA, 3)
                elif name == "qk":
                    act.wait_ge(s_A_qk, floor(4 * b + n + 1))
                    act.wait_ge(s_A_split, floor(16 * b - 16 + 4 * n + 4))
                    a(til[:, n, :], ps[3][:, :], ACT.Relu, bias=bqk[:, n:n + 1]).then_inc(s_A_relu, 1)
                    act.wait_ge(s_A_til, floor(4 * b + n - 1))
                    a(eA[:, n % 2, :], ps[3][:, :], ACT.Exp, bias=bqk[:, n:n + 1]).then_inc(s_A_exp, 1)

                elif name == "cast":
                    t, part = divmod(n, 2)
                    slot = t % 2
                    act.wait_ge(s_A_rope, floor(6 * b + 3 * (t // 2) + 3))
                    act.wait_ge(s_A_split, floor(16 * b + 2 * n))
                    if part == 0:
                        act.wait_ge(s_pk[slot], floor(16 * PK_DMAS * (2 * b + t // 2)))
                    a(parts[:, slot, part, :], til[:, t, :], ACT.Copy).then_inc(s_A_split, 1)

            def invert(b, s, c):
                n = NC * s + c
                if c == 0:
                    act.wait_ge(s_av, floor(STEPS * b + s - 1))
                act.wait_ge(s_den, floor(UNITS * b + n + 1))
                a(rP[:, s % 2, c, :], ps[n % 2][:, :], ACT.Ln).then_inc(s_ln, 1)
                if c == NC - 1:
                    act.wait_ge(s_ln, floor(UNITS * b + n + 1))
                    a(rP[:, s % 2, :, :], rP[:, s % 2, :, :], ACT.Exp, scale=-1.0).then_inc(s_ex, 1)

            def att(b, m_done, name, s):
                if name == "first":
                    act.wait_ge(s_ya, floor((NS - 1) * m_done))
                    act.wait_ge(s_sc, floor(NS * m_done))
                    for c in range(NC):
                        invert(b, 0, c)
                elif name == "unit" and s + NC < UNITS:
                    invert(b, s // NC + 1, s % NC)
                elif name == "close":
                    act.wait_ge(s_av, floor(STEPS * (b + 1)))
                    act.wait_ge(s_oproj, floor(b))
                    a(oT, ps[3][:, :], ACT.Copy).then_inc(s_o_copied, 1)

            def ffn(f, beside_scan, start, name, q):
                if name == "mean":
                    act.wait_ge(s_F_xc, floor(f + 1))
                    a(sqF[:, :], xnF[:, :], ACT.Square).then_inc(s_F_sq, 1)
                elif name == "var":
                    act.wait_ge(s_fadd, floor(NE * f - 1))
                    rstd(s_F_var, s_F_rs, f, rsF, 7)
                elif name == "router":
                    act.wait_ge(s_F_route, floor(N_ROUTE * f + 10))
                    a(gp[:, 1, :], gp[:, 0, :], ACT.Exp).then_inc(s_F_ed, 1)
                elif name == "spread" and beside_scan:
                    act.wait_ge(s_cb, floor(NE * f + q))
                    a(cBs[:, :], ps[7][:, :], ACT.Copy).then_inc(s_cbs, 1)
                elif name == "burst":
                    act.preload_act_table_set(GELU_SET)
                    for n in range(start[q], start[q + 1]):
                        w = NE if n < FC else n // FC - 1
                        c = n % FC
                        act.wait_ge(s_up, floor(NCH * f + n + 1))
                        before = n - HSLOTS if n >= HSLOTS else n + (NCH - 1 - n) // HSLOTS * HSLOTS - NCH
                        act.wait_ge(s_dn, floor(NCH * f + before + 1))
                        a(hF[:, n % HSLOTS, :], ps[4 + n % 3][:, :], ACT.Gelu, bias=b1c[:, w * FC + c:w * FC + c + 1]).then_inc(s_ge, 1)
                    act.preload_act_table_set(LOG_EXP)

            def decay(m, s):
                act.wait_ge(s_sc, floor(NS * m + s - 1))
                if s == 1:
                    act.wait_ge(s_M_spk, floor(5 * (m + 1)))
                a(dAs[:, s % 2, :, :], dte[:, :, :], ACT.Exp, scale=Acol[:, s:s + 1]).then_inc(s_da, 1)

            def scan(m, a_done, name, s):
                if name == "mean":
                    act.wait_ge(s_M_xc, floor(m + 1))
                    a(sqM, xnM[:, :], ACT.Square).then_inc(s_M_sq, 1)
                elif name == "var":
                    rstd(s_M_var, s_M_rs, m, rsM[:, :], 1)
                elif name == "inproj":
                    for h in range(2):
                        act.wait_ge(s_M_ip, floor(4 * m + 1 + h))
                        act.wait_ge(s_M_cv, floor(8 * m))
                        a(xpad[:, h, 3:515], ps[h][:, :], ACT.Copy).then_inc(s_M_xp, 1)
                elif name == "silu":
                    act.preload_act_table_set(SILU_SET)
                    act.wait_ge(s_x3_done, floor(m))
                    act.wait_ge(s_M_cv, floor(8 * m + 8))
                    for h in range(2):
                        a(xcs[:, h, :], xcs[:, h, :], ACT.Silu).then_inc(s_M_si, 1)
                    act.wait_ge(s_M_ip, floor(4 * m + 4))
                    a(zs[:, 0, :], ps[2][:, :], ACT.Silu).then_inc(s_M_si, 1)
                    a(zs[:, 1, :], ps[0][:, :], ACT.Silu).then_inc(s_M_si, 1)
                    act.preload_act_table_set(LOG_EXP)
                elif name == "dt":
                    act.wait_ge(s_x1_done, floor(a_done))
                    for o in range(2):
                        act.wait_ge(s_M_dt, floor(2 * m + o + 1))
                        a(dte[:, o, :], ps[1 + o][:, :], ACT.Relu, bias=bdc[:, o:o + 1]).then_inc(s_M_dtr, 1)
                        a(ws[:, 0, o, :], ps[1 + o][:, :], ACT.Abs, bias=bdc[:, o:o + 1]).then_inc(s_M_sp, 1)
                    act.wait_ge(s_M_sp, floor(4 * m + 2))
                    a(ws[:, 0, :, :], ws[:, 0, :, :], ACT.Exp, scale=-1.0).then_inc(s_M_sp, 1)
                    act.wait_ge(s_M_sp, floor(4 * m + 3))
                    a(ws[:, 0, :, :], ws[:, 0, :, :], ACT.Ln, bias=1.0).then_inc(s_M_sp, 1)
                elif name == "state":
                    act.wait_ge(s_M_dtx, floor(3 * (m + 1)))
                    decay(m, 0)
                elif name == "unit" and s + 1 < NS:
                    decay(m, s + 1)

            def scan_norm(m, name):
                if name == "norm_mean":
                    act.wait_ge(s_E_yc, floor(m + 1))
                    act.wait_ge(s_sc, floor(NS * (m + 1)))
                    a(sqE, yM[:, :, :], ACT.Square).then_inc(s_E_sq, 1)
                elif name == "norm_var":
                    rstd(s_E_var, s_E_rs, m, rsM[:, :], 3)

            def run(order, i, has_a, has_m, has_2, has_p):
                for kind, name, n in order:
                    if kind == "A" and has_a:
                        att(i, i - 1, name, n)
                    if kind == "E" and has_2:
                        scan_norm(i - 2, name)
                    if kind == "G" and has_2:
                        if name == "close":
                            act.wait_ge(s_out_t, floor((i - 2) + 1))
                            act.wait_ge(s_out_d, floor(16 * (i - 2)))
                            act.wait_ge(s_A_til, floor(4 * heads(i)))
                            a(outS, ps[7][:, :].rearrange("p (j d) -> p j d", j=JB), ACT.Copy).then_inc(s_out_c, 1)
                        else:
                            ffn(f2(i), False, BURST_START[kind], name, n)
                    if kind == "F" and has_a:
                        ffn(f1(i), True, BURST_START[kind], name, n)
                    if kind == "M" and has_m:
                        scan(i - 1, heads(i), name, n)
                    if kind == "P" and has_p:
                        pre(i + 1, name, n)

            act.wait_ge(s_setup, 1)
            act.wait_ge(s_zeroed, 16 * 12)
            for e in (NE, *range(NE)):
                w1, w2 = (sW1, sW2) if e == NE else (W1[e], W2[e])
                act.dma_start(rawW1[:, e, :], w1).then_inc(s_wbig, 16)
                act.dma_start(W2s[:, e, :, :], w2.rearrange("(c f) h -> f c h", f=P)).then_inc(s_wbig, 16)
            for name, n in HEAD_ORDER:
                pre(0, name, n)
            act.wait_ge(s_W1_low, 2)
            passes(run, act)

        @block.vector
        def _(v):
            v.memset(zero16, 0.0).then_inc(s_consts, 1)
            v.memset(onesD[:, :], 1.0 / D).then_inc(s_consts, 1)
            v.memset(onesI[:, :], 1.0 / DI).then_inc(s_consts, 1)
            v.memset(eps[:, :], EPS).then_inc(s_consts, 1)
            v.memset(one[:, :], 1.0).then_inc(s_consts, 1)
            for e in range(NE):
                ins = v.memset(iota8[:, e:e + 1], float(e))
            ins.then_inc(s_consts, 1)
            v.memset(vpad[:, :, :], 0.0).then_inc(s_consts, 1)
            v.memset(c96[:, :, :, :], 0.0).then_inc(s_consts, 1)
            v.memset(xpad[:, :, 0:3], 0.0).then_inc(s_consts, 1)
            v.wait_ge(s_wload, 16 * N_WLOAD)
            src = rawqkv.rearrange("p (s c k r m e) -> p s r e k m c", s=3, c=NC, k=2, r=2, m=HD // 2)
            dst = wqk[:, :, :].rearrange("p u (r k m e c) -> p u r e k m c", r=2, k=2, m=HD // 2, e=2)
            bsrc = brow[:, :].rearrange("p (s c k r m e) -> p s r e k m c", s=3, c=NC, k=2, r=2, m=HD // 2)
            bdst = bperm[:, :, :].rearrange("p u (r k m e c) -> p u r e k m c", r=2, k=2, m=HD // 2, e=2)
            for u in range(4):
                for r in range(2):
                    for e in range(2):
                        f = e if u % 2 == 0 else 1 - e
                        v.tensor_copy(bdst[:, u, r, e], bsrc[:, u // 2, r, f])
                        ins = v.tensor_copy(dst[:, u, r, e], src[:, u // 2, r, f])
            v.tensor_copy(wv[:, :], rawqkv[:, 2 * D:3 * D])
            v.wait_ge(s_acol, 1)
            v.tensor_scalar(Acol[:, :], Acol[:, :], -1.0, None, ALU.mult).then_inc(s_acol, 1)
            v.wait_ge(s_setup_turned, 1)
            v.tensor_copy(WinT[:, :, :], ps[0][:, :].rearrange("p (e m) -> p e m", e=4))
            v.tensor_copy(WdtT[:, :, :], ps[1][:, :].rearrange("p (c o) -> p c o", c=2))
            v.tensor_copy(WoT[:, :, :], ps[2][:, 0:DI].rearrange("p (c d) -> p c d", c=2))
            for r in range(PARTS):
                v.tensor_copy(wxT[:, :, r * 2 * NS:(r + 1) * 2 * NS], ps[3][:, 0:4 * NS].rearrange("p (c s) -> p c s", c=2))
            v.tensor_copy(gateT[:, :], ps[4][:, 0:NE])
            v.tensor_copy(cols[:, :], ps[5][:, 0:NROW])
            v.tensor_copy(bqk[:, :], ps[6][:, 0:4]).then_inc(s_setup, 1)

            def pre(b, name, n):
                if name == "mean":
                    v.wait_ge(s_A_mean, floor(b + 1))
                    v.wait_ge(s_A_v, floor(b))
                    v.wait_ge(s_xA_done, floor(b + 1))
                    v.tensor_tensor(xnA[:, :], xA[:, :], ps[3][:, :], ALU.subtract).then_inc(s_A_xc, 1)
                elif name == "var":
                    v.wait_ge(s_A_rs, floor(2 * b + 2))
                    v.wait_ge(s_A_sq, floor(b + 1))
                    v.tensor_tensor(xnA[:, :], xnA[:, :], rsA, ALU.mult).then_inc(s_A_xn, 1)
                elif name == "til":
                    v.wait_ge(s_A_relu, floor(4 * b + n + 1))
                    v.wait_ge(s_A_exp, floor(4 * b + n + 1))
                    v.scalar_tensor_tensor(til[:, n, :], eA[:, n % 2, :], 1.0, til[:, n, :], ALU.min, ALU.add).then_inc(s_A_til, 1)
                elif name == "v":
                    v.wait_ge(s_A_v, floor(b + 1))
                    v.wait_ge(s_av, floor(STEPS * b))
                    v.tensor_tensor(vpad[:, :, :].rearrange("p g (k w) -> p g k w", w=40)[:, :, :, 0:HD],
                                    ps[3][:, :].rearrange("p (g k d) -> p g k d", g=JB * NC, k=NK),
                                    bvrow[:, :, :].rearrange("p j (c k d) -> p (j c) k d", c=NC, k=NK), ALU.add).then_inc(s_A_vp, 1)

            def att(b, name, s):
                if name == "unit":
                    step, c = divmod(s, NC)
                    if c == 0:
                        v.wait_ge(s_ex, floor(STEPS * b + step + 1))
                    v.wait_ge(s_num, floor(UNITS * b + s + 1))
                    v.tensor_tensor(rP[:, step % 2, c, :], ps[2][:, :], rP[:, step % 2, c, :], ALU.mult).then_inc(s_mul, 1)

            def att_close(b, f_before):
                v.wait_ge(s_oproj, floor(b + 1))
                v.wait_ge(s_yv, floor(f_before))
                v.scalar_tensor_tensor(xFin[:, :], ps[2][:, :], boc, xA[:, :], ALU.add, ALU.add).then_inc(s_x1_done, 1)

            def split_rows(src, pk, rest, base, chain):
                v.tensor_copy(pk[:, :], src).then_inc(chain, 1)
                v.wait_ge(chain, floor(base + 1))
                v.tensor_tensor(rest, src, pk[:, :], ALU.subtract).then_inc(chain, 1)
                v.wait_ge(chain, floor(base + 2))
                v.tensor_copy(mid[64:96, :], rest[64:96]).then_inc(chain, 1)
                v.tensor_copy(pk[32:64, :], rest[32:64]).then_inc(chain, 1)
                v.wait_ge(chain, floor(base + 4))
                v.tensor_tensor(pk[64:96, :], rest[64:96], mid[64:96, :], ALU.subtract).then_inc(chain, 1)

            def halves(high, low, src, chain, base):
                v.tensor_copy(high, src).then_inc(chain, 1)
                v.wait_ge(chain, floor(base + 1))
                v.tensor_tensor(low, src, high.bitcast(F32), ALU.subtract).then_inc(chain, 1)

            def ffn(f, beside_scan, acc_free, name, q):
                if name == "mean":
                    v.wait_ge(s_F_mean, floor(f + 1))
                    v.wait_ge(s_up, floor(NCH * f))
                    v.tensor_tensor(xnF[:, :], xFin[:, :], ps[7][:, :], ALU.subtract).then_inc(s_F_xc, 1)
                elif name == "var":
                    v.wait_ge(s_F_rs, floor(2 * f + 2))
                    v.tensor_tensor(xnF[:, :], xnF[:, :], rsF, ALU.mult).then_inc(s_F_xn, 1)
                    v.wait_ge(s_F_xn, floor(f + 1))
                    halves(xnH[:, :], xnL[:, :], xnF[:, :], s_F_low, 2 * f)
                elif name == "router":
                    base = N_ROUTE * f
                    count = [0]

                    def step(ins, wait=True):
                        ins.then_inc(s_F_route, 1)
                        count[0] += 1
                        if wait:
                            v.wait_ge(s_F_route, floor(base + count[0]))

                    v.wait_ge(s_F_log, floor(f + 1))
                    step(v.tensor_copy(lg[:, :, :], ps[7][:, 0:JB * NE].rearrange("p (j e) -> p j e", j=JB)))
                    settled(v)
                    for j in range(JB):
                        step(v.max(mx8[:, j, :], lg[:, j, :]), j == JB - 1)
                    settled(v)
                    for j in range(JB):
                        step(v.max_index(ix8[:, j, :], mx8[:, j, :], lg[:, j, :]), False)
                    step(v.tensor_tensor(gp[:, 0, :], mx8[:, :, 1], mx8[:, :, 0], ALU.subtract), False)
                    assert count[0] == 10
                    v.wait_ge(s_F_route, floor(base + 9))
                    step(v.tensor_copy(ixf[:, :, :], ix8[:, :, 0:2]), False)
                    v.wait_ge(s_F_ed, floor(f + 1))
                    step(v.tensor_scalar(gp[:, 2, :], gp[:, 1, :], 1.0, None, ALU.add))
                    step(v.reciprocal(gp[:, 2, :], gp[:, 2, :]))
                    step(v.tensor_tensor(gp[:, 3, :], gp[:, 1, :], gp[:, 2, :], ALU.mult))
                    wide = [P, JB, NE]
                    for t in range(2):
                        step(v.tensor_tensor(oh[:, t, :, :], iota8[:, :].unsqueeze(1).broadcast_to(wide),
                                             ixf[:, :, t:t + 1].broadcast_to(wide), ALU.is_equal), t == 1)
                    for t in range(2):
                        step(v.tensor_tensor(oh[:, t, :, :], oh[:, t, :, :],
                                             gp[:, 2 + t, :].unsqueeze(2).broadcast_to(wide), ALU.mult), t == 1)
                    v.wait_ge(s_F_turn, floor(f))
                    for r in range(PARTS):
                        step(v.tensor_tensor(c96[:, :, r, 0:NE], oh[:, 0, :, :], oh[:, 1, :, :], ALU.add), False)
                    assert count[0] == N_ROUTE
                elif name == "turn":
                    v.wait_ge(s_F_turn, floor(f + 1))
                    v.wait_ge(s_cb, floor(NE * f))
                    v.wait_ge(s_F_var, floor(f + 1))
                    split_rows(ps[7][0:96, :], cpk, rsF[0:96], 5 * f, s_F_cpk)
                elif name == "spread" and not beside_scan:
                    v.wait_ge(s_cb, floor(NE * f + q))
                    v.tensor_copy(cBs[:, :], ps[7][:, :]).then_inc(s_cbs, 1)
                elif name == "down" and q % FC == FC - 1:
                    q //= FC
                    v.wait_ge(s_dn, floor(NCH * f + FC * (q + 1)))
                    if q == 0:
                        v.wait_ge(s_fadd, floor(NE * f))
                        v.wait_ge(s_out_t, floor(acc_free))
                        v.scalar_tensor_tensor(acc[:, :], ps[7][:, :], b2c[:, NE:NE + 1], xFin[:, :], ALU.add, ALU.add).then_inc(s_yv, 1)
                    else:
                        v.wait_ge(s_cbs, floor(NE * f + q))
                        v.wait_ge(s_fadd, floor(NE * f + q - 2))
                        v.scalar_tensor_tensor(tmp[:, q % 2, :], ps[7][:, :], b2c[:, q - 1:q], cBs[:, :], ALU.add, ALU.mult).then_inc(s_yv, 1)

            def scan(m, name, s):
                if name == "mean":
                    v.wait_ge(s_M_mean, floor(m + 1))
                    v.wait_ge(s_M_ip, floor(4 * m))
                    v.tensor_tensor(xnM[:, :], xM[:, :], ps[0][:, :], ALU.subtract).then_inc(s_M_xc, 1)
                elif name == "var":
                    v.wait_ge(s_M_rs, floor(2 * m + 2))
                    v.tensor_tensor(xnM[:, :], xnM[:, :], rsM[:, :], ALU.mult).then_inc(s_M_xn, 1)
                elif name == "conv":
                    v.wait_ge(s_M_xp, floor(2 * m + 2))
                    for k in range(NCONV):
                        for h in range(2):
                            src = xpad[:, h, k:k + 512]
                            if k == 0:
                                v.tensor_scalar(xcs[:, h, :], src, convw[:, h, 0:1], cbc[:, h:h + 1], ALU.mult, ALU.add).then_inc(s_M_cv, 1)
                            else:
                                v.wait_ge(s_M_cv, floor(8 * m + 2 * (k - 1) + h + 1))
                                v.scalar_tensor_tensor(xcs[:, h, :], src, convw[:, h, k:k + 1], xcs[:, h, :], ALU.mult, ALU.add).then_inc(s_M_cv, 1)
                elif name == "dt":
                    v.wait_ge(s_M_sp, floor(4 * m + 4))
                    v.wait_ge(s_M_dtr, floor(2 * m + 2))
                    v.tensor_tensor(dte[:, :, :], dte[:, :, :], ws[:, 0, :, :], ALU.add).then_inc(s_M_dtx, 1)
                    v.wait_ge(s_M_dtx, floor(3 * m + 1))
                    v.tensor_tensor(dtx[:, :, :], dte[:, :, :], xcs[:, :, :], ALU.mult).then_inc(s_M_dtx, 1)
                    v.wait_ge(s_M_dtx, floor(3 * m + 2))
                    v.memset(dte[:, :, 0:1], RESET).then_inc(s_M_dtx, 1)
                elif name == "state":
                    v.wait_ge(s_M_ss, floor(m + 1))
                    v.wait_ge(s_Cm, floor(NS * m))
                    v.wait_ge(s_M_var, floor(m + 1))
                    split_rows(ps[0][0:96, :], spk, sqM[0:96], 5 * m, s_M_spk)
                elif name == "unit":
                    both = [P, 2, 512]
                    w = ws[:, s % 3, :, :]
                    if s == 0:
                        dbx(m, 0)
                    v.wait_ge(s_da, floor(NS * m + s + 1))
                    v.wait_ge(s_dbx, floor(NS * m + s + 1))
                    v.tensor_tensor_scan(w.rearrange("p h t -> p (h t)"), dAs[:, s % 2, :, :].rearrange("p h t -> p (h t)"),
                                         w.rearrange("p h t -> p (h t)"), 0.0, ALU.mult, ALU.add).then_inc(s_sc, 1)
                    if s + 1 < NS:
                        dbx(m, s + 1)
                    v.wait_ge(s_Cm, floor(NS * m + s + 1))
                    v.wait_ge(s_sc, floor(NS * m + s + 1))
                    dst = yM[:, :, :] if s == 0 else w
                    v.tensor_tensor(dst, ps[1][:, :].unsqueeze(1).broadcast_to(both), w, ALU.mult).then_inc(s_hc, 1)

            def scan_norm(m, f_before, name):
                if name == "norm_mean":
                    both = [P, 2, 512]
                    v.wait_ge(s_E_mean, floor(m + 1))
                    v.tensor_tensor(yM[:, :, :], yM[:, :, :], ps[3][:, :].unsqueeze(1).broadcast_to(both), ALU.subtract).then_inc(s_E_yc, 1)
                elif name == "norm_var":
                    both = [P, 2, 512]
                    v.wait_ge(s_E_rs, floor(2 * m + 2))
                    base = N_EOP * m
                    v.tensor_tensor(yM[:, :, :], yM[:, :, :], rsM[:, :].unsqueeze(1).broadcast_to(both), ALU.mult).then_inc(s_E_op, 1)
                    v.wait_ge(s_E_op, floor(base + 1))
                    for h in range(2):
                        v.tensor_scalar(yM[:, h, :], yM[:, h, :], lgc[:, h:h + 1], lbc[:, h:h + 1], ALU.mult, ALU.add).then_inc(s_E_op, 1)
                    for h in range(2):
                        v.wait_ge(s_E_op, floor(base + 2 + h))
                        v.scalar_tensor_tensor(yM[:, h, :], xcs[:, h, :], dpc[:, h:h + 1], yM[:, h, :], ALU.mult, ALU.add).then_inc(s_E_op, 1)
                    v.wait_ge(s_E_op, floor(base + 5))
                    v.tensor_tensor(yM[:, :, :], yM[:, :, :], zs[:, :, :], ALU.mult).then_inc(s_E_op, 1)
                elif name == "gate":
                    v.wait_ge(s_E_proj, floor(m + 1))
                    v.wait_ge(s_yv, floor(f_before))
                    v.tensor_tensor(xFin[:, :], ps[3][:, :], xM[:, :], ALU.add).then_inc(s_x3_done, 1)

            def dbx(m, s):
                v.wait_ge(s_Bm, floor(NS * m + s + 1))
                if s >= 3:
                    v.wait_ge(s_ya, floor((NS - 1) * m + s - 3))
                v.tensor_tensor(ws[:, s % 3, :, :], ps[0][:, :].unsqueeze(1).broadcast_to([P, 2, 512]), dtx[:, :, :], ALU.mult).then_inc(s_dbx, 1)

            def run(order, i, has_a, has_m, has_2, has_p):
                for kind, name, n in order:
                    if kind == "A" and has_a:
                        if name == "close":
                            att_close(i, (NE + 1) * f2(i) + 1 if has_2 else 0)
                        else:
                            att(i, name, n)
                    if kind == "E" and has_2:
                        scan_norm(i - 2, (NE + 1) * f1(i - 1) + 1 if has_m else 0, name)
                    if kind == "G" and has_2 and name != "close":
                        ffn(f2(i), False, outs_done(i - 1), name, n)
                    if kind == "F" and has_a:
                        ffn(f1(i), True, outs_done(i), name, n)
                    if kind == "M" and has_m:
                        scan(i - 1, name, n)
                    if kind == "P" and has_p:
                        pre(i + 1, name, n)

            for name, n in HEAD_ORDER:
                pre(0, name, n)
            v.wait_ge(s_wbig, 16 * N_WBIG)
            halves(W1H[:, :, :], W1L[:, :, :], rawW1, s_W1_low, 0)
            passes(run, v)

        @block.gpsimd
        def _(pool):
            g = nc.gpsimd
            g.memset(ident[:, :], 0.0).then_inc(s_pconst, 1)
            g.memset(pick[:, :], 0.0).then_inc(s_pconst, 1)
            pool.wait_ge(s_pconst, 2)
            g.affine_select(out=ident[:, :], in_=ident[:, :], compare_op=ALU.not_equal, fill=1.0, base=0,
                            pattern=[[-1, P]], channel_multiplier=1).then_inc(s_pconst, 1)
            for r in range(PARTS):
                pool.wait_ge(s_pconst, floor(3 + r))
                g.affine_select(out=pick[:, :], in_=pick[:, :], compare_op=ALU.not_equal, fill=1.0, base=-32 * r,
                                pattern=[[-1, 32]], channel_multiplier=1).then_inc(s_pconst, 1)

            def pre(b, name, n):
                if name == "rope":
                    pool.wait_ge(s_A_til, floor(4 * b + 2 * n + 2))
                    g.tensor_tensor(rot, til[:, 2 * n, :], ropeC[:, :], ALU.mult).then_inc(s_A_rope, 1)
                    g.tensor_tensor(til[:, 2 * n + 1, :], til[:, 2 * n + 1, :], ropeS[:, :], ALU.mult).then_inc(s_A_rope, 1)
                    pool.wait_ge(s_A_rope, floor(6 * b + 3 * n + 2))
                    g.tensor_tensor(til[:, 2 * n + 1, :], rot, til[:, 2 * n + 1, :], ALU.add).then_inc(s_A_rope, 1)
                elif name == "rest":
                    t, part = divmod(n, 2)
                    pool.wait_ge(s_A_split, floor(16 * b + 2 * n + 1))
                    left = til[:, t, :] if part == 0 else parts[:, t % 2, 2, :]
                    g.tensor_tensor(left, til[:, t, :], parts[:, t % 2, part, :], ALU.subtract).then_inc(s_A_split, 1)

            def ffn(f, dst, name, q):
                if name == "down":
                    e, c = divmod(q, FC)
                    q = e if c == FC - 1 else 0
                if (name == "down" and 1 <= q < NE) or name == "close":
                    pool.wait_ge(s_yv, floor((NE + 1) * f + q + 1))
                    pool.wait_ge(s_fadd, floor(NE * f + q - 1))
                    g.tensor_tensor(dst, acc[:, :], tmp[:, q % 2, :], ALU.add).then_inc(s_fadd, 1)

            def run(order, i, has_a, has_m, has_2, has_p):
                for kind, name, n in order:
                    if kind == "G" and has_2:
                        ffn(f2(i), acc[:, :], name, NE if name == "close" else n)
                    if kind == "F" and has_a:
                        ffn(f1(i), acc[:, :], name, n)
                    if kind == "M" and has_m and name == "take":
                        pool.wait_ge(s_x3_done, floor(i - 1))
                        ffn(f1(i - 1), xM[:, :], "close", NE)
                    if kind == "M" and has_m and name == "unit" and n >= 1:
                        m = i - 1
                        pool.wait_ge(s_hc, floor(NS * m + n + 1))
                        pool.wait_ge(s_ya, floor((NS - 1) * m + n - 1))
                        g.tensor_tensor(yM[:, :, :], yM[:, :, :], ws[:, n % 3, :, :], ALU.add).then_inc(s_ya, 1)
                    if kind == "P" and has_p:
                        pre(i + 1, name, n)

            for name, n in HEAD_ORDER:
                pre(0, name, n)
            passes(run, pool)


_INS = ['L0_attn_a_x', 'L0_attn_a_w_qkv', 'L0_attn_a_b_qkv', 'L0_attn_a_w_out', 'L0_attn_a_b_out',
        'L0_attn_b_W_in', 'L0_attn_b_conv_w', 'L0_attn_b_conv_b', 'L0_attn_b_W_x', 'L0_attn_b_W_dt', 'L0_attn_b_b_dt',
        'L0_attn_b_A_log', 'L0_attn_b_D_param', 'L0_attn_b_W_out', 'L0_attn_b_ln_g', 'L0_attn_b_ln_b',
        'L0_ffn_gate_w', 'L0_ffn_W1', 'L0_ffn_b1', 'L0_ffn_W2', 'L0_ffn_b2',
        'L0_ffn_sW1', 'L0_ffn_sb1', 'L0_ffn_sW2', 'L0_ffn_sb2']


def rope_tables(n_tokens):
    half = HD // 2
    theta = (1.0 / np.float32(1250) ** (np.arange(half, dtype=np.float32) / np.float32(half))).astype(np.float32)
    angles = np.arange(n_tokens, dtype=np.float32)[:, None] * theta[None, :]
    dim = (np.arange(P) // NC) % HD
    sign = np.where(dim % 2 == 0, np.float32(-1), np.float32(1))
    cos = np.cos(angles).astype(np.float32).T[dim // 2]
    sin = sign[:, None] * np.sin(angles).astype(np.float32).T[dim // 2]
    return np.ascontiguousarray(cos), np.ascontiguousarray(sin.astype(np.float32))


def kernel(**inputs):
    import concourse.bacc as _bacc
    from concourse.bass_utils import run_bass_kernel_spmd as _run

    nc = _bacc.Bacc("TRN2", target_bir_lowering=False, num_devices=1)
    arrays, args = {}, []
    cos, sin = rope_tables(inputs[_INS[0]].shape[1])
    for name, a in [(n, inputs[n]) for n in _INS] + [("rope_cos", cos), ("rope_sin", sin)]:
        a = np.ascontiguousarray(a)
        arrays[f"in_{name}"] = a
        args.append(nc.dram_tensor(f"in_{name}", a.shape, mybir.dt.from_np(a.dtype), kind="ExternalInput").ap())
    out = nc.dram_tensor("out_0", inputs[_INS[0]].shape, F32, kind="ExternalOutput").ap()
    hybrid_layer_kernel(nc, *args, out)
    r = _run(nc, [arrays], core_ids=[0])
    return r.results[0]["out_0"]
```
